# Optimizing a Trainium2 kernel written in Bass

```python
import numpy as np
import jax
import jax.numpy as jnp

def _softmax(x, axis=-1):
    return jax.nn.softmax(x, axis=axis)

def _gelu(x):
    return jax.nn.gelu(x, approximate=True)

def _silu(x):
    return jax.nn.silu(x)

def _sigmoid(x):
    return jax.nn.sigmoid(x)

def _layernorm(x, axis=-1, eps=1e-05):
    m = jnp.mean(x, axis=axis, keepdims=True)
    v = jnp.var(x, axis=axis, keepdims=True)
    return (x - m) / jnp.sqrt(v + eps)

def _scatter_add(tgt, idx, src, axis=0):
    return tgt.at[idx].add(src)

def _segment_sum(src, seg, n):
    return jax.ops.segment_sum(src, seg, n)
kernel_name = 'mk_seq_postln_d1_jaxref_r4_373e85'

def setup_inputs(seed: int=0):
    np.random.seed(seed)
    _w = jnp.asarray

    def _L0_attn_setup():
        import jax, jax.numpy as jnp
        import numpy as np
        EMBED_DIM = 256
        NUM_HEADS = 16
        HEAD_DIM = EMBED_DIM // NUM_HEADS
        B, N = (2, 512)
        BIAS_S = 32

        def _interp_matrix(n, s):
            pos = jnp.arange(n, dtype=jnp.float32) * ((s - 1) / (n - 1))
            i0 = jnp.floor(pos).astype(jnp.int32)
            i1 = jnp.minimum(i0 + 1, s - 1)
            frac = pos - i0.astype(jnp.float32)
            rows = jnp.arange(n)
            M = jnp.zeros((n, s), dtype=jnp.float32)
            M = M.at[rows, i0].add(1.0 - frac).at[rows, i1].add(frac)
            return M
        key = jax.random.key(seed)
        ks = jax.random.split(key, 12)
        std = 0.02
        d = {'x': jax.random.normal(ks[0], (B, N, EMBED_DIM), dtype=jnp.float32), 'Wq': jax.random.normal(ks[1], (EMBED_DIM, EMBED_DIM), dtype=jnp.float32) * std, 'bq': jnp.zeros((EMBED_DIM,), dtype=jnp.float32), 'Wk': jax.random.normal(ks[2], (EMBED_DIM, EMBED_DIM), dtype=jnp.float32) * std, 'bk': jnp.zeros((EMBED_DIM,), dtype=jnp.float32), 'Wv': jax.random.normal(ks[3], (EMBED_DIM, EMBED_DIM), dtype=jnp.float32) * std, 'bv': jnp.zeros((EMBED_DIM,), dtype=jnp.float32), 'Wo': jax.random.normal(ks[4], (EMBED_DIM, EMBED_DIM), dtype=jnp.float32) * std, 'bo': jnp.zeros((EMBED_DIM,), dtype=jnp.float32), 'gamma': jnp.ones((EMBED_DIM,), dtype=jnp.float32), 'beta': jnp.zeros((EMBED_DIM,), dtype=jnp.float32), 'rel_bias': jax.random.normal(ks[5], (NUM_HEADS, BIAS_S, BIAS_S), dtype=jnp.float32) * std}
        return d
    _L0_attn_in = _L0_attn_setup()

    def _L0_ffn_setup():
        import jax, jax.numpy as jnp
        import numpy as np
        B, S, D, E, K = (2, 512, 256, 8, 2)
        H = 4 * D
        key = jax.random.key(seed)
        ks = jax.random.split(key, 6)
        x = jax.random.normal(ks[0], (B, S, D), dtype=jnp.float32)
        lim_g = np.sqrt(6.0 / (D + E)).astype(np.float32)
        W_gate = jax.random.uniform(ks[1], (D, E), minval=-lim_g, maxval=lim_g, dtype=jnp.float32)
        lim1 = np.sqrt(1.0 / D).astype(np.float32)
        lim2 = np.sqrt(1.0 / H).astype(np.float32)
        W1 = jax.random.uniform(ks[2], (E, D, H), minval=-lim1, maxval=lim1, dtype=jnp.float32)
        b1 = jax.random.uniform(ks[3], (E, H), minval=-lim1, maxval=lim1, dtype=jnp.float32)
        W2 = jax.random.uniform(ks[4], (E, H, D), minval=-lim2, maxval=lim2, dtype=jnp.float32)
        b2 = jax.random.uniform(ks[5], (E, D), minval=-lim2, maxval=lim2, dtype=jnp.float32)
        return {'x': x, 'W_gate': W_gate, 'W1': W1, 'b1': b1, 'W2': W2, 'b2': b2}
    _L0_ffn_in = _L0_ffn_setup()
    _d = {'L0_attn_x': _L0_attn_in['x'], 'L0_attn_Wq': _L0_attn_in['Wq'], 'L0_attn_bq': _L0_attn_in['bq'], 'L0_attn_Wk': _L0_attn_in['Wk'], 'L0_attn_bk': _L0_attn_in['bk'], 'L0_attn_Wv': _L0_attn_in['Wv'], 'L0_attn_bv': _L0_attn_in['bv'], 'L0_attn_Wo': _L0_attn_in['Wo'], 'L0_attn_bo': _L0_attn_in['bo'], 'L0_attn_gamma': _L0_attn_in['gamma'], 'L0_attn_beta': _L0_attn_in['beta'], 'L0_attn_rel_bias': _L0_attn_in['rel_bias'], 'L0_ffn_W_gate': _L0_ffn_in['W_gate'], 'L0_ffn_W1': _L0_ffn_in['W1'], 'L0_ffn_b1': _L0_ffn_in['b1'], 'L0_ffn_W2': _L0_ffn_in['W2'], 'L0_ffn_b2': _L0_ffn_in['b2']}
    _x0 = _d['L0_attn_x']
    _d['L0_attn_x'] = jax.random.normal(jax.random.fold_in(jax.random.key(seed), 1), (8, 512, 256), dtype=_x0.dtype)
    del _x0
    return _d

def reference(L0_attn_x, L0_attn_Wq, L0_attn_bq, L0_attn_Wk, L0_attn_bk, L0_attn_Wv, L0_attn_bv, L0_attn_Wo, L0_attn_bo, L0_attn_gamma, L0_attn_beta, L0_attn_rel_bias, L0_ffn_W_gate, L0_ffn_W1, L0_ffn_b1, L0_ffn_W2, L0_ffn_b2):

    def _L0_attn_ref(x, Wq, bq, Wk, bk, Wv, bv, Wo, bo, gamma, beta, rel_bias):
        import jax, jax.numpy as jnp
        import numpy as np
        EMBED_DIM = 256
        NUM_HEADS = 16
        HEAD_DIM = EMBED_DIM // NUM_HEADS
        B, N = (2, 512)
        BIAS_S = 32

        def _interp_matrix(n, s):
            pos = jnp.arange(n, dtype=jnp.float32) * ((s - 1) / (n - 1))
            i0 = jnp.floor(pos).astype(jnp.int32)
            i1 = jnp.minimum(i0 + 1, s - 1)
            frac = pos - i0.astype(jnp.float32)
            rows = jnp.arange(n)
            M = jnp.zeros((n, s), dtype=jnp.float32)
            M = M.at[rows, i0].add(1.0 - frac).at[rows, i1].add(frac)
            return M
        Bx, Nx, C = x.shape
        H, D = (NUM_HEADS, HEAD_DIM)
        scale = 1.0 / jnp.sqrt(jnp.float32(D))
        mu = jnp.mean(x, axis=-1, keepdims=True)
        var = jnp.mean(jnp.square(x - mu), axis=-1, keepdims=True)
        xn = (x - mu) * jax.lax.rsqrt(var + 1e-05) * gamma + beta
        q = (xn @ Wq.T + bq).reshape(Bx, Nx, H, D).transpose(0, 2, 1, 3)
        k = (xn @ Wk.T + bk).reshape(Bx, Nx, H, D).transpose(0, 2, 1, 3)
        v = (xn @ Wv.T + bv).reshape(Bx, Nx, H, D).transpose(0, 2, 1, 3)
        attn = jnp.einsum('bhnd,bhmd->bhnm', q, k) * scale
        M = _interp_matrix(Nx, BIAS_S)
        rel = jnp.einsum('ni,hij,mj->hnm', M, rel_bias, M)
        rel = rel.at[:, -1, :].set(0.0).at[:, :, -1].set(0.0)
        attn = attn + rel[None]
        mask = jnp.triu(jnp.ones((Nx, Nx), dtype=bool), k=1)
        attn = jnp.where(mask, -jnp.inf, attn)
        attn = jax.nn.softmax(attn, axis=-1)
        out = jnp.einsum('bhnm,bhmd->bhnd', attn, v)
        out = out.transpose(0, 2, 1, 3).reshape(Bx, Nx, C)
        out = out @ Wo.T + bo
        return out

    def _L0_ffn_ref(x, W_gate, W1, b1, W2, b2):
        import jax, jax.numpy as jnp
        import numpy as np
        B, S, D, E, K = (2, 512, 256, 8, 2)
        H = 4 * D
        gate = jnp.einsum('bsd,de->bse', x, W_gate)
        kth = jax.lax.top_k(gate, K)[0][..., -1:]
        mask = jax.nn.softmax(jnp.where(gate >= kth, gate, -jnp.inf), axis=-1)
        h = jax.nn.relu(jnp.einsum('bsd,edh->bseh', x, W1) + b1)
        y = jnp.einsum('bseh,ehd->bsed', h, W2) + b2
        return (y * mask[..., None]).mean(axis=-2)
    x = L0_attn_x
    x = _layernorm(x + _L0_attn_ref(x, L0_attn_Wq, L0_attn_bq, L0_attn_Wk, L0_attn_bk, L0_attn_Wv, L0_attn_bv, L0_attn_Wo, L0_attn_bo, L0_attn_gamma, L0_attn_beta, L0_attn_rel_bias), axis=-1)
    x = _layernorm(x + _L0_ffn_ref(x, L0_ffn_W_gate, L0_ffn_W1, L0_ffn_b1, L0_ffn_W2, L0_ffn_b2), axis=-1)
    return x

_drawn_inputs = setup_inputs


def setup_inputs(seed=0):
    import zlib

    import numpy as np

    out = dict(_drawn_inputs(seed))
    spreads = {'L0_attn_bq': (0.0, 0.8),
     'L0_attn_bk': (0.0, 2.0),
     'L0_attn_bv': (0.0, 0.289),
     'L0_attn_bo': (0.0, 0.1),
     'L0_attn_gamma': (1.0, 0.6),
     'L0_attn_beta': (0.0, 0.8)}
    factors = {'L0_attn_Wq': 8.0,
     'L0_attn_Wk': 8.0,
     'L0_attn_Wv': 3.524,
     'L0_attn_rel_bias': 42.794,
     'L0_ffn_W_gate': 2.83,
     'L0_ffn_W1': 3.043,
     'L0_ffn_b1': 36.182,
     'L0_ffn_b2': 28.287}
    for name, (base, spread) in spreads.items():
        noise = np.random.default_rng([zlib.crc32(name.encode()), seed]).standard_normal(out[name].shape)
        drawn = base * np.exp(spread * noise) if base else spread * noise
        out[name] = jnp.asarray(drawn.astype(out[name].dtype))
    for name, factor in factors.items():
        out[name] = (out[name] * factor).astype(out[name].dtype)
    return out
```

```python
from contextlib import ExitStack

import concourse.bass as bass
from concourse import mybir
from concourse.alu_op_type import AluOpType as ALU

ACT = mybir.ActivationFunctionType
AX = mybir.AxisListType
F32 = mybir.dt.float32
F32R = mybir.dt.float32r
BF16 = mybir.dt.bfloat16
I32 = mybir.dt.int32

P = 128
B, N, D = 8, 512, 256
T = B * N
H, DH = 16, 16
S = 32
HH = H // 2
NT = N // P
DC = D // P
VW = 32
BANK = 512
PAIRS = HH // 2
JOBS = 5
UJOBS = PAIRS * JOBS
ST_BANKS, MX_BANKS = 4, 2
SCALE = DH ** -0.5
EPS = 1e-5
MASKED = -1e30
E, TOPK, FF = 8, 2, 4 * D
FC = FF // P
TT = T // P
MT = 256
MH = MT // P
ET = T // MT
SPARE = P
PROLOGUE_GEN = 9
STEP_GEN = (6, 4)
GEN = sum(STEP_GEN)


def score_jobs(first_wide):
    wide = (lambda t: N - t * P) if first_wide else (lambda t: (t + 1) * P)
    order = (0, 1, 3, 2) if first_wide else (3, 2, 0, 1)
    full, long, short, half = order
    jobs = []
    for a in range(2):
        jobs.append([(a, full, wide(full), 0)])
        jobs.append([(a, long, wide(long), 0), (a, short, wide(short), wide(long))])
    jobs.append([(0, half, wide(half), 0), (1, half, wide(half), wide(half))])
    return jobs


KEY_JOBS = score_jobs(True)
QUERY_JOBS = score_jobs(False)


NEWTON = 3
RSQRT_STEPS = 3 + 3 * NEWTON


def rsqrt(nc, dve, var, y, tmp, done, base):
    nc.vector.tensor_scalar(tmp[0], var, EPS, None, ALU.add).then_inc(done, 1)
    dve.wait_ge(done, base + 1)
    nc.vector.tensor_scalar(tmp[1].bitcast(I32), tmp[0].bitcast(I32), 1, None, ALU.arith_shift_right).then_inc(done, 1)
    dve.wait_ge(done, base + 2)
    nc.vector.tensor_scalar(y.bitcast(I32), tmp[1].bitcast(I32), -1.0, float(0x5F3759DF), ALU.mult, ALU.add
                            ).then_inc(done, 1)
    for k in range(NEWTON):
        dve.wait_ge(done, base + 3 + 3 * k)
        nc.vector.scalar_tensor_tensor(tmp[1], y, -0.5, y, ALU.mult, ALU.mult).then_inc(done, 1)
        dve.wait_ge(done, base + 4 + 3 * k)
        nc.vector.tensor_tensor(tmp[2], tmp[1], tmp[0], ALU.mult).then_inc(done, 1)
        dve.wait_ge(done, base + 5 + 3 * k)
        nc.vector.scalar_tensor_tensor(y, tmp[2], 1.5, y, ALU.add, ALU.mult).then_inc(done, 1)


def attention(nc, x, mt, w, rel, scratch_qk, scratch_o):
    ctx = ExitStack()
    with ctx:
        def sb(name, shape, dt=F32):
            return ctx.enter_context(nc.sbuf_tensor(name, shape, dt))

        def pb(name, shape, dt=F32):
            return ctx.enter_context(nc.psum_tensor(name, shape, dt))

        def sem(name):
            return ctx.enter_context(nc.semaphore(name))

        qs = sb("qs", [P, 2, HH, N], F32R)
        ks = sb("ks", [P, 2, HH, N], F32R)
        qs2 = sb("qs2", [P, 2, HH, N], F32R)
        ks2 = sb("ks2", [P, N], F32R)
        probs = sb("probs", [P, 2, 2 * JOBS, BANK])
        vaug = sb("vaug", [P, 2, NT, HH, VW])
        wq_s = sb("wq_s", [P, DC, D])
        wk_s = sb("wk_s", [P, DC, D])
        wv_s = sb("wv_s", [P, DC, D])
        bq_s = sb("bq_s", [P, 2])
        bq4 = sb("bq4", [P, 2])
        bk_s = sb("bk_s", [P, 2])
        bv_s = sb("bv_s", [P, D])
        gam = sb("gam", [P, DC])
        bet = sb("bet", [P, DC])
        xt = sb("xt", [P, NT, D])
        xh = sb("xh", [P, NT, D])
        xnt = sb("xnt", [P, DC, N])
        qf = sb("qf", [P, 2, N])
        qsp = sb("qsp", [P, 2, 2, N], F32R)
        mx = sb("mx", [P, HH, NT])
        negm = sb("negm", [HH * NT, P], F32R)
        ov = sb("ov", [P, 2, N])
        st6 = sb("st6", [P, NT, 6])
        mv = sb("mv", [P, NT, 2])
        rs = sb("rs", [P, NT])
        rt = sb("rt", [P, 3, NT])
        idf = sb("idf", [P, P])
        idb = sb("idb", [P, P], BF16)
        mask_q = sb("mask_q", [P, P], BF16)
        mask_k = sb("mask_k", [P, P], BF16)
        mtf = xt[:, 0:2, :].rearrange("p a n -> p (a n)")
        relr = probs[0:S, 0, 0:4, :].rearrange("p a n -> p (a n)")[:, 0:H * 2 * S].rearrange(
            "p (h a j) -> p h a j", h=H, a=2)
        rhi = qsp[:, 0, 0, :]

        st = [pb(f"st{i}", [P, BANK]) for i in range(ST_BANKS)]
        sm = [pb(f"sm{i}", [P, BANK]) for i in range(MX_BANKS)]
        po = pb("po", [P, BANK])
        pg = pb("pg", [P, BANK])

        w_in, x_in = sem("w_in"), sem("x_in")
        consts = sem("consts")
        r_ready, r_used = sem("r_ready"), sem("r_used")
        ks_const = sem("ks_const")
        ln_step, stats_seen, xh_ready = sem("ln_step"), sem("stats_seen"), sem("xh_ready")
        gen_ready, gen_free = sem("gen_ready"), sem("gen_free")
        split_step, split_ready = sem("split_step"), sem("split_ready")
        scr_out = [sem(f"scr_out{i}") for i in range(2)]
        rows_in = [sem(f"rows_in{i}") for i in range(2)]
        st_ready, st_free = sem("st_ready"), sem("st_free")
        sm_ready, sm_free = sem("sm_ready"), sem("sm_free")
        max_in = sem("max_in")
        pv_ready, pv_free = sem("pv_ready"), sem("pv_free")
        o_out = [sem(f"o_out{i}") for i in range(2)]
        block = ctx.enter_context(nc.Block())

        WEIGHTS = 14

        def xnt_at(c):
            return xnt[:, c, :]

        @block.sync
        def _(sp):
            sp.sem_inc(scr_out[1], 32)
            for dst, src in (
                (mtf[0:S, :], mt), (mtf[64:96, :], mt), (mtf[96:128, :], mt),
                (relr[:, :, 0, :], rel.rearrange("h i j -> i h j")),
                (relr[:, :, 1, :], rel.rearrange("h i j -> i h j")),
                (wq_s[:, :, :], w["wq"].rearrange("(k p) o -> p k o", p=P)),
                (wk_s[:, :, :], w["wk"].rearrange("(k p) o -> p k o", p=P)),
                (wv_s[:, :, :], w["wv"].rearrange("(k p) o -> p k o", p=P)),
                (bq_s[:, :], w["bq"]), (bk_s[:, :], w["bk"]),
                (bv_s[:, :], w["bv"].partition_broadcast(P)),
                (gam[:, :], w["gamma"]), (bet[:, :], w["beta"]),
                (xh[:, :, :], x[0].rearrange("(t p) d -> p t d", p=P)),
            ):
                sp.dma_start(dst, src).then_inc(w_in, 16)

            def load_x(b):
                sp.dma_start(xt[:, :, :], x[bass.ds(b, 1), :, :].rearrange("a (t p) d -> p (a t) d", p=P)
                             ).then_inc(x_in, 16)

            def store_split(b, half):
                un = 2 * b + half
                for a in range(2):
                    sp.wait_ge(split_ready, 2 * un + a + 1)
                    sp.dma_start(scratch_qk[half, a].rearrange("t p n -> p t n"), qsp[:, a, :, :].bitcast(F32)
                                 ).then_inc(scr_out[half], 16)

            def load_rows(b, half):
                sp.wait_ge(scr_out[half], 32 * (b + 1 + half))
                q_parts = scratch_qk[half, 0].rearrange("t (i h) n -> (t i) (h n)", h=HH)
                k_parts = scratch_qk[half, 1].rearrange("t (i h) n -> t i (h n)", h=HH)
                for r in range(2):
                    sp.dma_start(qs[2 * DH * r:2 * DH * (r + 1), half, :, :].bitcast(F32).rearrange(
                        "p h n -> p (h n)"), q_parts).then_inc(rows_in[half], 16)
                for r in range(4):
                    sp.dma_start(ks[DH * r:DH * (r + 1), half, :, :].bitcast(F32).rearrange(
                        "p h n -> p (h n)"), k_parts[r // 2]).then_inc(rows_in[half], 16)

            def load_max(g, half):
                sp.wait_ge(gen_free, g + 1)
                sp.dma_start(qs2[0:1, half, :, :].bitcast(F32).rearrange("p h (t n) -> p (h t) n", n=P),
                             negm[:, :].bitcast(F32)).then_inc(max_in, 16)

            def store_o(b, half, q):
                un = 2 * b + half
                sp.wait_ge(pv_free, 1 + 2 * un + q + 1)
                sp.dma_start(scratch_o[bass.ds(4 * b + 2 * half + q, 1), :, :].rearrange("a p n -> (a p) n"),
                             ov[:, q, :]).then_inc(o_out[q], 16)

            def step(b, half, more):
                un = 2 * b + half
                g = PROLOGUE_GEN + GEN * b + half * STEP_GEN[0]
                if more and half == 0:
                    sp.wait_ge(xh_ready, NT * (b + 1))
                    load_x(b + 1)
                if more:
                    store_split(b + 1, half)
                store_o(b, half, 0)
                if more:
                    sp.wait_ge(st_ready, UJOBS * (un + 1))
                    load_rows(b + 1, half)
                if more or half == 0:
                    load_max(g + (2 if half == 0 else 0) + 2 if more else g, 1 - half)
                store_o(b, half, 1)

            for half in range(2):
                store_split(0, half)
            for half in range(2):
                load_rows(0, half)
            load_max(PROLOGUE_GEN - 1, 0)
            with sp.Fori(0, B - 1) as b:
                for half in range(2):
                    step(b, half, True)
            for half in range(2):
                step(B - 1, half, False)
            for q in range(2):
                sp.wait_ge(o_out[q], 16 + 16 * 2 * B)

        @block.gpsimd
        def _(pool):
            nc.gpsimd.memset(idf[:, :], 0.0).then_inc(consts, 1)
            nc.gpsimd.memset(idb[:, :], 0.0).then_inc(consts, 1)
            nc.gpsimd.memset(mask_q[:, :], 0.0).then_inc(consts, 1)
            nc.gpsimd.memset(mask_k[:, :], 0.0).then_inc(consts, 1)
            nc.gpsimd.memset(vaug[:, :, :, :, :], 0.0).then_inc(consts, 1)
            pool.wait_ge(consts, 5)
            for t in (idf, idb):
                nc.gpsimd.affine_select(out=t[:, :], in_=t[:, :], compare_op=ALU.not_equal, fill=1.0, base=0,
                                        pattern=[[-1, P]], channel_multiplier=1).then_inc(consts, 1)
            nc.gpsimd.affine_select(out=mask_q[:, :], in_=mask_q[:, :], compare_op=ALU.is_ge, fill=MASKED, base=0,
                                    pattern=[[-1, P]], channel_multiplier=1).then_inc(consts, 1)
            nc.gpsimd.affine_select(out=mask_k[:, :], in_=mask_k[:, :], compare_op=ALU.is_ge, fill=MASKED, base=0,
                                    pattern=[[1, P]], channel_multiplier=-1).then_inc(consts, 1)
            nc.gpsimd.memset(vaug[:, :, :, :, DH:DH + 1], 1.0).then_inc(consts, 1)
            nc.gpsimd.memset(qs2[0:64, :, :, :].bitcast(F32), 0.0).then_inc(consts, 1)
            nc.gpsimd.memset(ks2[0:64, :].bitcast(F32), 0.0).then_inc(consts, 1)
            pool.wait_ge(consts, 12)
            nc.gpsimd.memset(ks2[0:1, :].bitcast(F32), 1.0).then_inc(consts, 1)

        CONSTS = 13

        @block.scalar
        def _(act):
            act.sem_inc(st_free, ST_BANKS)
            act.sem_inc(pv_free, 1)
            act.sem_inc(o_out[0], 16)
            act.sem_inc(o_out[1], 16)
            act.wait_ge(w_in, 16 * WEIGHTS)
            nc.scalar.mul(bq4[:, :], bq_s[:, :], SCALE).then_inc(r_used, 1)
            act.wait_ge(r_used, 1)

            def project_out(un, half, a, g):
                act.wait_ge(gen_ready, g + 1)
                if a == 0:
                    nc.scalar.activation(qf[:, 0, :], pg[:, :], ACT.Identity, bias=bq4[:, half:half + 1],
                                         scale=SCALE).then_inc(gen_free, 1)
                else:
                    nc.scalar.activation(qf[:, 1, :], pg[:, :], ACT.Identity, bias=bk_s[:, half:half + 1],
                                         scale=1.0).then_inc(gen_free, 1)

            def exps(un, half, pair):
                q = pair // 2
                if pair % 2 == 0:
                    act.wait_ge(pv_ready, 2 * un + q + 1)
                for j in range(JOBS):
                    job = UJOBS * un + JOBS * pair + j
                    act.wait_ge(st_ready, job + 1)
                    nc.scalar.activation(probs[:, q, JOBS * (pair % 2) + j, :], st[(JOBS * pair + j) % ST_BANKS][:, :],
                                         ACT.Exp).then_inc(st_free, 1)

            def o_from_psum(un, q):
                act.wait_ge(pv_ready, 2 + 2 * un + q + 1)
                act.wait_ge(o_out[q], 16 * (un + 1))
                nc.scalar.copy(ov[:, q, :], po[:, :]).then_inc(pv_free, 1)

            act.sem_inc(pv_ready, 2)
            for half in range(2):
                for a in range(2):
                    if half:
                        act.wait_ge(split_ready, 2 * (half - 1) + a + 1)
                    project_out(half, half, a, 2 + 3 * half + a)

            def step(b, half, more):
                un = 2 * b + half
                g = PROLOGUE_GEN + GEN * b + half * STEP_GEN[0]
                for pair in range(3):
                    exps(un, half, pair)
                o_from_psum(un, 0)
                if more:
                    for a in range(2):
                        act.wait_ge(split_ready, 2 * (un + 1) + a + 1)
                        project_out(un + 2, half, a, g + (2 if half == 0 else 0) + a)
                exps(un, half, 3)
                o_from_psum(un, 1)

            with act.Fori(0, B - 1) as b:
                for half in range(2):
                    step(b, half, True)
            for half in range(2):
                step(B - 1, half, False)

        @block.vector
        def _(dve):
            dve.sem_inc(sm_free, MX_BANKS)
            dve.wait_ge(w_in, 16 * WEIGHTS)

            nc.vector.tensor_copy(ks[64:128, 0, 0, :], mtf[64:128, :]).then_inc(ks_const, 1)
            dve.wait_ge(ks_const, 1)
            nc.vector.tensor_tensor(ks2[64:128, :], mtf[64:128, :], ks[64:128, 0, 0, :].bitcast(F32), ALU.subtract
                                    ).then_inc(ks_const, 1)
            for half in range(2):
                for h in range(HH):
                    if half + h:
                        nc.vector.tensor_copy(ks[64:128, half, h, :], mtf[64:128, :]).then_inc(ks_const, 1)
            for h in range(H):
                dve.wait_ge(r_ready, h + 1)
                if h:
                    dve.wait_ge(ks_const, 1 + H + 3 * h)
                nc.vector.tensor_copy(rhi[64:128, :], st[h % 2][64:128, :]).then_inc(ks_const, 1)
                dve.wait_ge(ks_const, 1 + H + 3 * h + 1)
                nc.vector.tensor_copy(qs[64:96, h // HH, h % HH, :], rhi[64:96, :].bitcast(F32)).then_inc(ks_const, 1)
                nc.vector.tensor_tensor(qs[96:128, h // HH, h % HH, :], st[h % 2][96:128, :],
                                        rhi[96:128, :].bitcast(F32), ALU.subtract).then_inc(ks_const, 1)
            dve.wait_ge(ks_const, 1 + H + 3 * H)
            nc.vector.tensor_copy(qs2[64:128, :, :, :], qs[64:128, :, :, :].bitcast(F32)).then_inc(ks_const, 1)

            def layernorm(src, n):
                base = (2 * NT + RSQRT_STEPS) * n
                for t in range(NT):
                    nc.vector.bn_stats(st6[:, t, :], src[:, t, :]).then_inc(ln_step, 1)
                dve.wait_ge(ln_step, base + NT).then_inc(stats_seen, 1)
                for t in range(NT):
                    nc.vector.bn_aggr(mv[:, t, :], st6[:, t, :]).then_inc(ln_step, 1)
                dve.wait_ge(ln_step, base + 2 * NT)
                rsqrt(nc, dve, mv[:, :, 1], rs[:, :], [rt[:, k, :] for k in range(3)], ln_step, base + 2 * NT)
                dve.wait_ge(ln_step, base + 2 * NT + RSQRT_STEPS)
                for t in range(NT):
                    nc.vector.tensor_scalar(xh[:, t, :], src[:, t, :], mv[:, t, 0:1], rs[:, t:t + 1],
                                            ALU.subtract, ALU.mult).then_inc(xh_ready, 1)

            def xnt_out(g):
                for c in range(DC):
                    dve.wait_ge(gen_ready, g + c + 1)
                    nc.vector.tensor_scalar(xnt[:, c, :], pg[:, :], gam[:, c:c + 1], bet[:, c:c + 1],
                                            ALU.mult, ALU.add).then_inc(gen_free, 1)

            def split(b, half, a, g):
                un = 2 * b + half
                dve.wait_ge(gen_free, g + 1)
                if half:
                    dve.wait_ge(scr_out[0], 32 * (b + 1))
                else:
                    dve.wait_ge(scr_out[1], 32 * (b + 1))
                nc.vector.tensor_copy(qsp[:, a, 0, :], qf[:, a, :]).then_inc(split_step, 1)
                dve.wait_ge(split_step, 2 * un + a + 1)
                nc.vector.tensor_tensor(qsp[:, a, 1, :], qf[:, a, :], qsp[:, a, 0, :].bitcast(F32), ALU.subtract
                                        ).then_inc(split_ready, 1)

            def v_out(half, g):
                dve.wait_ge(gen_ready, g + 1)
                nc.vector.tensor_tensor(
                    vaug[:, half, :, :, 0:DH], pg[:, :].rearrange("p (t h d) -> p t h d", t=NT, h=HH),
                    bv_s[:, half * P:(half + 1) * P].rearrange("p (a h d) -> p a h d", a=1, h=HH).to_broadcast(
                        [P, NT, HH, DH]), ALU.add).then_inc(gen_free, 1)

            def maxima(un, pair):
                for j, job in enumerate(QUERY_JOBS):
                    dve.wait_ge(sm_ready, UJOBS * un + JOBS * pair + j + 1)
                    bank = sm[(JOBS * pair + j) % MX_BANKS]
                    if job[0][2] == job[-1][2] and len(job) == 2:
                        t = job[0][1]
                        ins = nc.vector.tensor_reduce(
                            mx[:, 2 * pair:2 * pair + 2, t], bank[:, :].rearrange("p (a m) -> p a m", a=2), AX.X, ALU.max)
                    else:
                        for a, t, cols, at in job:
                            ins = nc.vector.tensor_reduce(mx[:, 2 * pair + a, t:t + 1], bank[:, at:at + cols],
                                                          AX.X, ALU.max)
                    ins.then_inc(sm_free, 1)

            def neg_out(un, g):
                dve.wait_ge(gen_ready, g + 1)
                if not isinstance(un, int) or un:
                    dve.wait_ge(max_in, 16 * un)
                nc.vector.tensor_scalar(negm[:, :], pg[0:HH * NT, 0:P], -1.0, None, ALU.mult).then_inc(gen_free, 1)

            layernorm(xh, 0)
            xnt_out(0)
            for half in range(2):
                for a in range(2):
                    split(0, half, a, 2 + 3 * half + a)
                v_out(half, 4 + 3 * half)
            for pair in range(PAIRS):
                maxima(0, pair)
            neg_out(0, PROLOGUE_GEN - 1)

            def step(b, half, more):
                un = 2 * b + half
                g = PROLOGUE_GEN + GEN * b + half * STEP_GEN[0]
                if more and half == 0:
                    dve.wait_ge(x_in, 16 * (b + 1))
                    layernorm(xt, b + 1)
                    xnt_out(g)
                if more or half == 0:
                    qk = g + (2 if half == 0 else 0)
                    neg = qk + 2 if more else g
                    for pair in range(PAIRS):
                        if more and pair in (1, 2):
                            split(b + 1, half, pair - 1, qk + pair - 1)
                        maxima(un + 1, pair)
                    neg_out(un + 1, neg)
                    if more:
                        v_out(half, neg + 1)

            with dve.Fori(0, B - 1) as b:
                for half in range(2):
                    step(b, half, True)
            for half in range(2):
                step(B - 1, half, False)

        @block.tensor
        def _(pe):
            pe.wait_ge(w_in, 16 * WEIGHTS)
            for h in range(H):
                if h >= 2:
                    pe.wait_ge(ks_const, 1 + H + 3 * (h - 1))
                nc.tensor.matmul(st[h % 2][64:128, :], relr[:, h, :, :].rearrange("p a j -> p (a j)"), mtf[0:S, :],
                                 start=True, stop=True).then_inc(r_ready, 1)
            pe.wait_ge(consts, CONSTS)
            pe.wait_ge(ks_const, 2 + H + 3 * H)

            def free_gen(g):
                if not isinstance(g, int) or g:
                    pe.wait_ge(gen_free, g)

            def transpose_x(b, g):
                for c in range(DC):
                    free_gen(g + c)
                    if c == 0:
                        pe.wait_ge(xh_ready, NT * (b + 1))
                    for t in range(NT):
                        ins = nc.tensor.transpose(pg[:, t * P:(t + 1) * P], xh[:, t, c * P:(c + 1) * P], idf[:, :])
                    ins.then_inc(gen_ready, 1)

            def project(half, wts, g):
                free_gen(g)
                for c in range(DC):
                    ins = nc.tensor.matmul(pg[:, :], wts[:, c, half * P:(half + 1) * P], xnt_at(c),
                                           start=(c == 0), stop=(c == DC - 1))
                ins.then_inc(gen_ready, 1)

            def project_v(half, g):
                free_gen(g)
                for t in range(NT):
                    for c in range(DC):
                        ins = nc.tensor.matmul(pg[:, t * P:(t + 1) * P], xnt[:, c, t * P:(t + 1) * P],
                                               wv_s[:, c, half * P:(half + 1) * P],
                                               start=(t == 0 and c == 0), stop=(c == DC - 1), skip_group_check=True)
                ins.then_inc(gen_ready, 1)

            def query_scores(un, half, pair):
                for j, job in enumerate(QUERY_JOBS):
                    pe.wait_ge(sm_free, UJOBS * un + JOBS * pair + j + 1)
                    bank = sm[(JOBS * pair + j) % MX_BANKS]
                    for n, (a, t, cols, at) in enumerate(job):
                        h = 2 * pair + a
                        nc.tensor.matmul(bank[:, at:at + cols], qs[:, half, h, t * P:(t + 1) * P],
                                         ks[:, half, h, 0:cols], start=(n == 0), stop=False, skip_group_check=True)
                        ins = nc.tensor.matmul(bank[:, at + cols - P:at + cols], idb[:, :], mask_q[:, :],
                                               start=False, stop=True, skip_group_check=True)
                    ins.then_inc(sm_ready, 1)

            def key_scores(un, half, pair):
                for j, job in enumerate(KEY_JOBS):
                    pe.wait_ge(st_free, UJOBS * un + JOBS * pair + j + 1)
                    bank = st[(JOBS * pair + j) % ST_BANKS]
                    for n, (a, t, cols, at) in enumerate(job):
                        h = 2 * pair + a
                        out = bank[:, at:at + cols]
                        nc.tensor.matmul(out, ks[:, half, h, t * P:(t + 1) * P], qs[:, half, h, t * P:N],
                                         start=(n == 0), stop=False, skip_group_check=True)
                        nc.tensor.matmul(out, ks2[:, t * P:(t + 1) * P], qs2[:, half, h, t * P:N],
                                         start=False, stop=False, skip_group_check=True)
                        ins = nc.tensor.matmul(bank[:, at:at + P], idb[:, :], mask_k[:, :],
                                               start=False, stop=True, skip_group_check=True)
                    ins.then_inc(st_ready, 1)

            def transpose_max(un, g):
                pe.wait_ge(sm_free, MX_BANKS + UJOBS * (un + 1))
                free_gen(g)
                nc.tensor.transpose(pg[0:HH * NT, 0:P], mx[:, :, :].rearrange("p h t -> p (h t)"), idf[:, :]
                                    ).then_inc(gen_ready, 1)

            def values(un, half, q):
                pe.wait_ge(st_free, ST_BANKS + UJOBS * un + 2 * JOBS * (q + 1))
                pe.wait_ge(pv_free, 2 * un + q + 1)
                for t in range(NT):
                    for r in range(4):
                        pr, a = divmod(r, 2)
                        j, at = [(j, c[3]) for j, job in enumerate(KEY_JOBS) for c in job if c[:2] == (a, t)][0]
                        ins = nc.tensor.matmul(po[VW * r:VW * (r + 1), t * P:N], vaug[:, half, t, 4 * q + r, :],
                                               probs[:, q, JOBS * pr + j, at:at + N - t * P],
                                               start=(t == 0), stop=(t == NT - 1), skip_group_check=True,
                                               tile_position=(0, VW * r))
                ins.then_inc(pv_ready, 1)

            transpose_x(0, 0)
            for half in range(2):
                project(half, wq_s, 2 + 3 * half)
                project(half, wk_s, 3 + 3 * half)
                project_v(half, 4 + 3 * half)
            pe.wait_ge(rows_in[0], 96)
            for pair in range(PAIRS):
                query_scores(0, 0, pair)
            transpose_max(0, PROLOGUE_GEN - 1)

            def step(b, half, more):
                un = 2 * b + half
                g = PROLOGUE_GEN + GEN * b + half * STEP_GEN[0]
                ahead = more or half == 0
                qk = g + (2 if half == 0 else 0)
                neg = qk + 2 if more else g
                pe.wait_ge(max_in, 16 * (un + 1))
                key_scores(un, half, 0)
                key_scores(un, half, 1)
                if more and half == 0:
                    transpose_x(b + 1, g)
                if ahead:
                    pe.wait_ge(rows_in[1 - half], 96 * (b + 1 + half))
                    query_scores(un + 1, 1 - half, 0)
                key_scores(un, half, 2)
                values(un, half, 0)
                if more:
                    project(half, wq_s, qk)
                if ahead:
                    query_scores(un + 1, 1 - half, 1)
                if more:
                    project(half, wk_s, qk + 1)
                if ahead:
                    query_scores(un + 1, 1 - half, 2)
                key_scores(un, half, 3)
                if ahead:
                    query_scores(un + 1, 1 - half, 3)
                    transpose_max(un + 1, neg)
                values(un, half, 1)
                if more:
                    project_v(half, neg + 1)

            with pe.Fori(0, B - 1) as b:
                for half in range(2):
                    step(b, half, True)
            for half in range(2):
                step(B - 1, half, False)


BIG = float(1 << 20)
RANKS = E


def after_attention(nc, w, scratch_o, rows, acc, slots, table):
    ctx = ExitStack()
    with ctx:
        def sb(name, shape, dt=F32):
            return ctx.enter_context(nc.sbuf_tensor(name, shape, dt))

        def pb(name, shape, dt=F32):
            return ctx.enter_context(nc.psum_tensor(name, shape, dt))

        def sem(name):
            return ctx.enter_context(nc.semaphore(name))

        wo_s = sb("wo_s", [P, DC, D])
        bo_s = sb("bo_s", [P, D])
        wg_s = sb("wg_s", [P, DC, E])
        idf = sb("idf2", [P, P])
        below = sb("below", [P, P], BF16)
        ones = sb("ones", [P, P], BF16)
        zero = sb("zero", [P, D])
        empty = sb("empty", [P, 2, P, 2], I32)
        ov = sb("ov2", [P, 4, N])
        xt = sb("xt2", [P, NT, D])
        xb = sb("xb2", [P, NT, D])
        rec = sb("rec", [P, NT, H])
        oh = sb("oh", [P, NT, D])
        oT = sb("oT", [P, NT, DC * P])
        res = sb("res", [P, NT, D])
        st6 = sb("st62", [P, NT, 6])
        mv = sb("mv2", [P, NT, 2])
        rs = sb("rs2", [P, NT])
        rt = sb("rt2", [P, 3, NT])
        x1 = sb("x1", [P, NT, D])
        x1T = sb("x1T", [P, NT, DC * P])
        gate = sb("gate", [P, NT, E])
        top = sb("top", [P, NT, E])
        picked = sb("picked", [P, NT, E])
        picked_b = sb("picked_b", [P, NT, E], BF16)
        before = sb("before", [P, NT + 1, E], BF16)
        expo = sb("expo", [P, NT, E])
        expm = sb("expm", [P, NT, E])
        tot = sb("tot", [P, NT])
        rtot = sb("rtot", [P, NT])
        wt = sb("wt", [P, NT, E])
        cums = [sb(f"cum{i}", [P, NT, 2 * E]) for i in range(4)]
        ebase = sb("ebase", [P, NT, E])
        slot = sb("slot", [P, NT, E])
        rank = sb("rank", [P, RANKS, E])
        pick = sb("pick", [P, NT, RANKS, E])
        pickm = sb("pickm", [P, NT, RANKS, E])
        tmp1 = sb("tmp1", [P, NT, RANKS, E])
        tmp2 = sb("tmp2", [P, NT, RANKS, E])
        idxf = sb("idxf", [P, NT, RANKS])
        idx = sb("idx", [P, NT, RANKS], I32)
        pay = sb("pay", [P, NT, RANKS, 2], I32)
        tied = sb("tied", [1, 4])
        tied_i = sb("tied_i", [1, 2], I32)
        cnt = sb("cnt", [1, E])
        over = sb("over", [1, 2, E, ET // 2])
        lim = sb("lim", [1, 2, E, ET // 2])
        tiles = sb("tiles", [1, 2, E])
        tcum = [sb(f"tcum{i}", [1, 2, 2 * E]) for i in range(4)]
        tokf = sb("tokf", [P, NT, RANKS])

        pa = pb("pa", [P, NT, BANK])
        pt = pb("pt", [P, 2, BANK])
        pc = pb("pc", [P, 2, BANK])

        w_in, o_in, x_in = sem("w_in2"), sem("o_in"), sem("x_in2")
        c_done = sem("c_done")
        spare_out, empty_out = sem("spare_out"), sem("empty_out")
        xb_ready = sem("xb_ready")
        a_ready, oh_ready, b_ready, oT_ready = sem("a_ready"), sem("oh_ready"), sem("b_ready"), sem("oT_ready")
        c_ready, d = sem("c_ready"), sem("dve_step")
        x1_ready, d_ready, x1T_ready, g_ready = sem("x1_ready"), sem("d_ready"), sem("x1T_ready"), sem("g_ready")
        diff_ready, expo_ready, picked_ready = sem("diff_ready"), sem("expo_ready"), sem("picked_ready")
        pos_ready, idx_ready, x1_out = sem("pos_ready"), sem("idx_ready"), sem("x1_out")
        scat, scat_ties, own = sem("scat"), sem("scat_ties"), sem("own")
        table_ready, lists_out = sem("table_ready"), sem("lists_out")
        block = ctx.enter_context(nc.Block())

        CONSTS = 20

        @block.sync
        def _(sp):
            sp.sem_inc(x1_out, 32)
            for dst, src in ((wo_s[:, :, :], w["wo"].rearrange("(k p) o -> p k o", p=P)),
                             (bo_s[:, :], w["bo"].partition_broadcast(P)),
                             (wg_s[:, :, :], w["wg"].rearrange("(k p) e -> p k e", p=P))):
                sp.dma_start(dst, src).then_inc(w_in, 16)
            sp.wait_ge(c_done, CONSTS)
            sp.dma_start(rows[T:T + SPARE, :], zero[:, :]).then_inc(spare_out, 16)
            sp.dma_start(acc[T:T + SPARE, :], zero[:, :]).then_inc(spare_out, 16)
            sp.dma_start(slots.rearrange("(p s) c -> p (s c)", p=P), empty[:, :, :, :].rearrange("p a s c -> p (a s c)")
                         ).then_inc(empty_out, 16)
            with sp.Fori(0, B) as b:
                sp.wait_ge(a_ready, b + 1)
                sp.dma_start(ov[:, :, :], scratch_o[bass.ds(4 * b, 4), :, :].rearrange("q p n -> p q n")
                             ).then_inc(o_in, 16)
                sp.wait_ge(xb_ready, b + 1)
                sp.dma_start(xt[:, :, :], w["x"][bass.ds(b, 1), :, :].rearrange("a (t p) d -> p (a t) d", p=P)
                             ).then_inc(x_in, 16)
                sp.wait_ge(x1_ready, b + 1)
                for dst in (rows, acc):
                    sp.dma_start(dst[bass.ds(N * b, N), :].rearrange("(t p) d -> p t d", p=P), x1[:, :, :]
                                 ).then_inc(x1_out, 16)
            sp.wait_ge(x1_out, 32 + 32 * B)
            sp.wait_ge(spare_out, 32)

        @block.gpsimd
        def _(pool):
            pool.sem_inc(xb_ready, 1)
            pool.sem_inc(lists_out, 1)
            nc.gpsimd.memset(idf[:, :], 0.0).then_inc(c_done, 1)
            nc.gpsimd.memset(below[:, :], 0.0).then_inc(c_done, 1)
            nc.gpsimd.memset(ones[:, :], 1.0).then_inc(c_done, 1)
            nc.gpsimd.memset(zero[:, :], 0.0).then_inc(c_done, 1)
            nc.gpsimd.memset(empty[:, :, :, :], 0).then_inc(c_done, 1)
            nc.gpsimd.memset(before[:, 0, :], 0.0).then_inc(c_done, 1)
            for c in cums[:3] + tcum[:3]:
                nc.gpsimd.memset(c[:, :, 0:E], 0.0).then_inc(c_done, 1)
            nc.gpsimd.memset(tied[:, :], 0.0).then_inc(c_done, 1)
            nc.gpsimd.iota(tokf[:, :, :], pattern=[[P, NT], [0, RANKS]], base=0, channel_multiplier=1,
                           allow_small_or_imprecise_dtypes=True).then_inc(c_done, 1)
            pool.wait_ge(c_done, 14)
            nc.gpsimd.affine_select(out=idf[:, :], in_=idf[:, :], compare_op=ALU.not_equal, fill=1.0, base=0,
                                    pattern=[[-1, P]], channel_multiplier=1).then_inc(c_done, 1)
            nc.gpsimd.affine_select(out=below[:, :], in_=below[:, :], compare_op=ALU.is_ge, fill=1.0, base=0,
                                    pattern=[[-1, P]], channel_multiplier=1).then_inc(c_done, 1)
            nc.gpsimd.iota(empty[:, :, :, 0], pattern=[[0, 2], [1, P]], base=T, channel_multiplier=0
                           ).then_inc(c_done, 1)
            nc.gpsimd.iota(ebase[:, :, :], pattern=[[0, NT], [T, E]], base=-int(BIG), channel_multiplier=0,
                           allow_small_or_imprecise_dtypes=True).then_inc(c_done, 1)
            nc.gpsimd.iota(rank[:, :, :], pattern=[[1, RANKS], [0, E]], base=1, channel_multiplier=0,
                           allow_small_or_imprecise_dtypes=True).then_inc(c_done, 1)
            nc.gpsimd.iota(lim[:, :, :, :], pattern=[[MT, 2], [0, E], [2 * MT, ET // 2]], base=0, channel_multiplier=0,
                           allow_small_or_imprecise_dtypes=True).then_inc(c_done, 1)
            pool.wait_ge(w_in, 48)
            pool.wait_ge(empty_out, 16)

            def scatter(t, r, done):
                nc.gpsimd.indirect_dma_start(out=slots, out_offset=bass.IndirectOffsetOnAxis(idx[:, t, r:r + 1], 0),
                                             in_=pay[:, t, r, :], in_offset=None, bounds_check=E * T - 1,
                                             oob_is_err=False).then_inc(done, 16)

            with pool.Fori(0, B) as b:
                pool.wait_ge(x_in, 16 * (b + 1)).then_inc(own, 1)
                for t in range(NT):
                    ins = nc.gpsimd.tensor_tensor(xb[:, t, :], xt[:, t, :], bo_s[:, :], ALU.add)
                ins.then_inc(xb_ready, 1)
                pool.wait_ge(idx_ready, b + 1).then_inc(own, 1)
                for t in range(NT):
                    for r in range(TOPK):
                        scatter(t, r, scat)
                some = pool.value_load(tied_i[0:1, 0:1], min_val=0, max_val=1)
                earlier = pool.value_load(tied_i[0:1, 1:2], min_val=0, max_val=B)
                with pool.If(some > 0):
                    for t in range(NT):
                        for r in range(TOPK, RANKS):
                            scatter(t, r, scat_ties)
                    pool.wait_ge(scat_ties, (earlier + 1) * (16 * NT * (RANKS - TOPK))).then_inc(own, 1)
                pool.wait_ge(scat, (b + 1) * (16 * NT * TOPK)).then_inc(own, 1)
                pool.sem_inc(lists_out, 1)

        @block.scalar
        def _(act):
            with act.Fori(0, B) as b:
                for k in range(2):
                    act.wait_ge(b_ready, 2 * b + k + 1)
                    nc.scalar.copy(oT[:, 2 * k:2 * k + 2, :].rearrange("p t n -> p (t n)"), pt[:, k, :]
                                   ).then_inc(oT_ready, 1)
                for k in range(2):
                    act.wait_ge(d_ready, 2 * b + k + 1)
                    nc.scalar.copy(x1T[:, 2 * k:2 * k + 2, :].rearrange("p t n -> p (t n)"), pt[:, k, :]
                                   ).then_inc(x1T_ready, 1)
                act.wait_ge(diff_ready, b + 1)
                nc.scalar.activation(expo[:, :, :], expo[:, :, :], ACT.Exp).then_inc(expo_ready, 1)

        @block.tensor
        def _(pe):
            pe.sem_inc(a_ready, 1)
            pe.wait_ge(c_done, CONSTS)
            pe.wait_ge(w_in, 48)
            with pe.Fori(0, B) as b:
                pe.wait_ge(o_in, 16 * (b + 1))
                for t in range(NT):
                    for q in range(4):
                        ins = nc.tensor.transpose(pa[:, t, q * P:(q + 1) * P], ov[:, q, t * P:(t + 1) * P], idf[:, :])
                ins.then_inc(a_ready, 1)
                pe.wait_ge(oh_ready, b + 1)
                for t in range(NT):
                    for c in range(DC):
                        ins = nc.tensor.transpose(pt[:, t // 2, (t % 2 * DC + c) * P:(t % 2 * DC + c + 1) * P],
                                                  oh[:, t, c * P:(c + 1) * P], idf[:, :])
                    if t % 2:
                        ins.then_inc(b_ready, 1)
                for t in range(NT):
                    if t % 2 == 0:
                        pe.wait_ge(oT_ready, 2 * b + t // 2 + 1)
                    for c in range(DC):
                        ins = nc.tensor.matmul(pc[:, t // 2, t % 2 * D:(t % 2 + 1) * D], oT[:, t, c * P:(c + 1) * P],
                                               wo_s[:, c, :], start=(t % 2 == 0 and c == 0), stop=(c == DC - 1),
                                               skip_group_check=True)
                    if t % 2:
                        ins.then_inc(c_ready, 1)
                pe.wait_ge(x1_ready, b + 1)
                for t in range(NT):
                    for c in range(DC):
                        ins = nc.tensor.transpose(pt[:, t // 2, (t % 2 * DC + c) * P:(t % 2 * DC + c + 1) * P],
                                                  x1[:, t, c * P:(c + 1) * P], idf[:, :])
                    if t % 2:
                        ins.then_inc(d_ready, 1)
                for t in range(NT):
                    if t % 2 == 0:
                        pe.wait_ge(x1T_ready, 2 * b + t // 2 + 1)
                    for c in range(DC):
                        ins = nc.tensor.matmul(pc[:, 0, t * E:(t + 1) * E], x1T[:, t, c * P:(c + 1) * P],
                                               wg_s[:, c, :], start=(t == 0 and c == 0), stop=(c == DC - 1),
                                               skip_group_check=True)
                ins.then_inc(g_ready, 1)
                pe.wait_ge(picked_ready, b + 1)
                nc.tensor.matmul(pc[:, 1, 0:NT * E], below[:, :], picked_b[:, :, :].rearrange("p t e -> p (t e)"),
                                 start=True, stop=False, skip_group_check=True)
                nc.tensor.matmul(pc[:, 1, 0:NT * E], ones[:, :], before[:, 0:NT, :].rearrange("p t e -> p (t e)"),
                                 start=False, stop=True, skip_group_check=True)
                nc.tensor.matmul(pc[:, 1, NT * E:2 * NT * E], ones[:, :],
                                 picked_b[:, :, :].rearrange("p t e -> p (t e)"),
                                 start=False, stop=True, skip_group_check=True).then_inc(pos_ready, 1)
            pe.wait_ge(idx_ready, B)
            nc.tensor.matmul(pc[:, 0, 0:E], ones[:, :], before[:, 0, :], start=True, stop=True).then_inc(pos_ready, 1)

        @block.vector
        def _(dve):
            dve.wait_ge(c_done, CONSTS)
            at = [0]

            def wide(ap, shape):
                return ap.to_broadcast(shape)

            STEPS = 58

            with dve.Fori(0, B) as b:
                at[0] = 0

                def link(ins):
                    ins.then_inc(d, 1)
                    at[0] += 1
                    dve.wait_ge(d, b * STEPS + at[0])

                dve.wait_ge(a_ready, b + 2)
                heads = pa[:, :, :].rearrange("p t (h e) -> p t h e", h=H)
                link(nc.vector.reciprocal(rec[:, :, :], heads[:, :, :, DH]))
                nc.vector.tensor_tensor(oh[:, :, :].rearrange("p t (h e) -> p t h e", h=H), heads[:, :, :, 0:DH],
                                        wide(rec[:, :, :].rearrange("p t (h a) -> p t h a", a=1), [P, NT, H, DH]),
                                        ALU.mult).then_inc(oh_ready, 1)
                dve.wait_ge(xb_ready, b + 2)
                dve.wait_ge(x1_out, 32 * (b + 1))
                for k in range(2):
                    dve.wait_ge(c_ready, 2 * b + k + 1)
                    link(nc.vector.tensor_tensor(res[:, 2 * k:2 * k + 2, :].rearrange("p t n -> p (t n)"), pc[:, k, :],
                                                 xb[:, 2 * k:2 * k + 2, :].rearrange("p t n -> p (t n)"), ALU.add))
                for t in range(NT):
                    ins = nc.vector.bn_stats(st6[:, t, :], res[:, t, :])
                    if t < NT - 1:
                        ins.then_inc(d, 1)
                        at[0] += 1
                ins.then_inc(d, 1)
                at[0] += 1
                dve.wait_ge(d, b * STEPS + at[0]).then_inc(own, 1)
                for t in range(NT):
                    ins = nc.vector.bn_aggr(mv[:, t, :], st6[:, t, :])
                    if t < NT - 1:
                        ins.then_inc(d, 1)
                        at[0] += 1
                link(ins)
                rsqrt(nc, dve, mv[:, :, 1], rs[:, :], [rt[:, k, :] for k in range(3)], d, b * STEPS + at[0])
                at[0] += RSQRT_STEPS
                dve.wait_ge(d, b * STEPS + at[0])
                for t in range(NT):
                    ins = nc.vector.tensor_scalar(x1[:, t, :], res[:, t, :], mv[:, t, 0:1], rs[:, t:t + 1],
                                                  ALU.subtract, ALU.mult)
                    if t < NT - 1:
                        ins.then_inc(d, 1)
                        at[0] += 1
                ins.then_inc(x1_ready, 1)
                dve.wait_ge(g_ready, b + 1)
                nc.vector.tensor_copy(gate[:, :, :], pc[:, 0, 0:NT * E].rearrange("p (t e) -> p t e", e=E)).then_inc(d, 1)
                at[0] += 1
                dve.wait_ge(d, b * STEPS + at[0]).then_inc(own, 1)
                for t in range(NT):
                    ins = nc.vector.max(top[:, t, :], gate[:, t, :])
                    if t < NT - 1:
                        ins.then_inc(d, 1)
                        at[0] += 1
                link(ins)
                full = [P, NT, E]
                nc.vector.tensor_tensor(expo[:, :, :], gate[:, :, :], wide(top[:, :, 0:1], full), ALU.subtract
                                        ).then_inc(diff_ready, 1)
                link(nc.vector.tensor_tensor(picked[:, :, :], gate[:, :, :], wide(top[:, :, TOPK - 1:TOPK], full),
                                             ALU.is_ge))
                link(nc.vector.tensor_copy(cums[0][:, :, E:2 * E], picked[:, :, :]))
                link(nc.vector.tensor_copy(picked_b[:, :, :], picked[:, :, :]))
                for t in range(NT):
                    ins = nc.vector.tensor_tensor(before[:, t + 1, :], before[:, t, :], picked_b[:, t, :], ALU.add)
                    if t < NT - 1:
                        link(ins)
                ins.then_inc(picked_ready, 1)
                for k in range(3):
                    s = 1 << k
                    link(nc.vector.tensor_tensor(cums[k + 1][:, :, E:2 * E], cums[k][:, :, E:2 * E],
                                                 cums[k][:, :, E - s:2 * E - s], ALU.add))
                dve.wait_ge(expo_ready, b + 1)
                link(nc.vector.tensor_tensor(expm[:, :, :], expo[:, :, :], picked[:, :, :], ALU.mult))
                link(nc.vector.tensor_reduce(tot[:, :], expm[:, :, :], AX.X, ALU.add))
                link(nc.vector.reciprocal(rtot[:, :], tot[:, :]))
                link(nc.vector.scalar_tensor_tensor(wt[:, :, :], expm[:, :, :], 1.0 / E,
                                                    wide(rtot[:, :].rearrange("p (t a) -> p t a", a=1), full),
                                                    ALU.mult, ALU.mult))
                four = [P, NT, RANKS, E]

                def over_ranks(ap):
                    return wide(ap.rearrange("p t (a e) -> p t a e", a=1), four)

                link(nc.vector.tensor_tensor(pick[:, :, :, :], over_ranks(cums[3][:, :, E:2 * E]),
                                             wide(rank[:, :, :].rearrange("p (a r) e -> p a r e", a=1), four),
                                             ALU.is_equal))
                link(nc.vector.tensor_tensor(pickm[:, :, :, :], pick[:, :, :, :], over_ranks(picked[:, :, :]), ALU.mult))
                link(nc.vector.tensor_tensor(tmp2[:, :, :, :], pickm[:, :, :, :], over_ranks(wt[:, :, :]), ALU.mult))
                dve.wait_ge(lists_out, b + 1)
                link(nc.vector.tensor_reduce(pay[:, :, :, 1].bitcast(F32), tmp2[:, :, :, :], AX.X, ALU.add))
                dve.wait_ge(pos_ready, b + 1)
                link(nc.vector.tensor_tensor(slot[:, :, :], pc[:, 1, 0:NT * E].rearrange("p (t e) -> p t e", e=E),
                                             ebase[:, :, :], ALU.add))
                link(nc.vector.tensor_copy(before[:, 0, :], before[:, NT, :]))
                link(nc.vector.tensor_tensor(tmp1[:, :, :, :], pickm[:, :, :, :], over_ranks(slot[:, :, :]), ALU.mult))
                link(nc.vector.tensor_reduce(idxf[:, :, :], tmp1[:, :, :, :], AX.X, ALU.add))
                link(nc.vector.tensor_scalar(idx[:, :, :], idxf[:, :, :], BIG, None, ALU.add))
                link(nc.vector.tensor_copy(pay[:, :, :, 0], tokf[:, :, :]))
                link(nc.vector.tensor_scalar(tokf[:, :, :], tokf[:, :, :], float(N), None, ALU.add))
                link(nc.vector.tensor_reduce(tied[0:1, 0:1], pc[0:1, 1, NT * E:2 * NT * E], AX.X, ALU.add))
                link(nc.vector.tensor_tensor(tied[0:1, 2:3], tied[0:1, 2:3], tied[0:1, 1:2], ALU.add))
                link(nc.vector.tensor_scalar(tied[0:1, 1:2], tied[0:1, 0:1], float(TOPK * N), None, ALU.is_gt))
                nc.vector.tensor_copy(tied_i[0:1, :], tied[0:1, 1:3]).then_inc(idx_ready, 1)
                assert at[0] == STEPS, at[0]

            at[0] = B * STEPS

            def then(ins):
                ins.then_inc(d, 1)
                at[0] += 1
                dve.wait_ge(d, at[0])

            dve.wait_ge(pos_ready, B + 1)
            then(nc.vector.tensor_copy(cnt[:, :], pc[0:1, 0, 0:E]))
            then(nc.vector.tensor_tensor(over[:, :, :, :], wide(cnt[:, :].rearrange("p (a e c) -> p a e c", a=1, c=1),
                                                                [1, 2, E, ET // 2]), lim[:, :, :, :], ALU.is_gt))
            then(nc.vector.tensor_reduce(tiles[:, :, :], over[:, :, :, :], AX.X, ALU.add))
            then(nc.vector.tensor_copy(tcum[0][:, :, E:2 * E], tiles[:, :, :]))
            for k in range(3):
                s = 1 << k
                then(nc.vector.tensor_tensor(tcum[k + 1][:, :, E:2 * E], tcum[k][:, :, E:2 * E],
                                             tcum[k][:, :, E - s:2 * E - s], ALU.add))
            then(nc.vector.tensor_copy(table[:, 0, :, :], tiles[:, :, :]))
            nc.vector.tensor_tensor(table[:, 1, :, :], tcum[3][:, :, E:2 * E], tiles[:, :, :], ALU.subtract
                                    ).then_inc(table_ready, 1)


def experts(nc, w, rows, acc, slots, table):
    ctx = ExitStack()
    with ctx:
        def sb(name, shape, dt=F32):
            return ctx.enter_context(nc.sbuf_tensor(name, shape, dt))

        def pb(name, shape, dt=F32):
            return ctx.enter_context(nc.psum_tensor(name, shape, dt))

        def sem(name):
            return ctx.enter_context(nc.semaphore(name))

        def two(name):
            return [sem(f"{name}{i}") for i in range(2)]

        w1_s = [sb(f"w1_s{i}", [P, DC, FF]) for i in range(2)]
        w2_s = [sb(f"w2_s{i}", [P, FC, D]) for i in range(2)]
        b1_s = [sb(f"b1_s{i}", [P, FC]) for i in range(2)]
        b2_s = [sb(f"b2_s{i}", [P, D]) for i in range(2)]
        lst = sb("lst", [P, 2, P, 2], I32)
        ids = sb("ids", [P, 2, P])
        tok_s = sb("tok_s", [P, 2 * P], I32)
        wts_s = sb("wts_s", [P, 2 * P])
        idf = sb("idf3", [P, P])
        idx = [sb(f"idx3{i}", [P, MH], I32) for i in range(2)]
        wt = [sb(f"wt3{i}", [P, MH]) for i in range(2)]
        xg = [sb(f"xg{i}", [P, MH, D]) for i in range(2)]
        xT = [sb(f"xT{i}", [P, DC, MT]) for i in range(2)]
        hT = sb("hT", [P, FC, MT])
        yb = sb("yb", [P, MH, D])
        ys = [sb(f"ys{i}", [P, MH, D]) for i in range(2)]

        px = [pb(f"px{i}", [P, DC, MT]) for i in range(2)]
        ph = [pb(f"ph{i}", [P, BANK]) for i in range(4)]
        py = [pb(f"py{i}", [P, BANK]) for i in range(2)]

        w_in = two("w_in3")
        lst_in, ids_f, lists_t, lists_ready, c_done = (sem("lst_in"), sem("ids_f"), sem("lists_t"),
                                                       sem("lists_ready"), sem("c_done3"))
        pe_done, act_done, dve_done = sem("pe_done"), sem("act_done"), sem("dve_done")
        idx_ready, xg_in, own = two("idx_ready3"), two("xg_in"), sem("own3")
        px_ready, xT_ready = two("px_ready"), two("xT_ready")
        h_ready, h_act, h_dve = sem("h_ready"), sem("h_act"), sem("h_dve")
        y_ready, y_free, yb_ready, ys_ready = sem("y_ready"), sem("y_free"), sem("yb_ready"), two("ys_ready")
        ys_free, added = two("ys_free"), two("added")
        block = ctx.enter_context(nc.Block())

        class Expert:

            def __init__(self, eng, e):
                self.tiles = [eng.value_load(table[0:1, 0, p, bass.ds(e, 1)], min_val=0, max_val=ET // 2)
                              for p in range(2)]
                self.before = [eng.value_load(table[0:1, 1, p, bass.ds(e, 1)], min_val=0, max_val=T)
                               for p in range(2)]

        def walk(eng, body, start=None, end=None):
            with eng.Fori(0, E // 2) as pair:
                for q in range(2):
                    e = 2 * pair + q
                    x = Expert(eng, e)
                    if start:
                        start(pair, e, q)
                    with eng.Fori(0, ET // 2) as j:
                        for p in range(2):
                            with eng.If(j < x.tiles[p]):
                                body(e, q, x, j, p)
                    if end:
                        end(pair, e, q, x)

        @block.sync
        def _(sp):
            sp.dma_start(lst[:, :, :, :].rearrange("p a s c -> p a (s c)"),
                         slots.rearrange("(a p s) c -> p a (s c)", a=2, p=P)).then_inc(lst_in, 16)
            with sp.Fori(0, E // 2) as pair:
                for q in range(2):
                    e = 2 * pair + q
                    sp.wait_ge(pe_done, e + 1)
                    sp.wait_ge(act_done, e + 1)
                    sp.wait_ge(dve_done, e + 1)
                    sp.dma_start(w1_s[q][:, :, :], w["w1"][bass.ds(e, 1), :, :].rearrange("a (k p) f -> p (a k) f", p=P)
                                 ).then_inc(w_in[q], 16)
                    sp.dma_start(b1_s[q][:, :], w["b1"][bass.ds(e, 1), :, :].rearrange("a p c -> (a p) c")
                                 ).then_inc(w_in[q], 16)
                    sp.dma_start(w2_s[q][:, :, :], w["w2"][bass.ds(e, 1), :, :].rearrange("a (k p) d -> p (a k) d", p=P)
                                 ).then_inc(w_in[q], 16)
                    sp.dma_start(b2_s[q][:, :], w["b2"][bass.ds(e, 1), :].to_broadcast([P, D])
                                 ).then_inc(w_in[q], 16)

        @block.gpsimd
        def _(pool):
            nc.gpsimd.memset(idf[:, :], 0.0).then_inc(c_done, 1)
            pool.wait_ge(c_done, 1)
            nc.gpsimd.affine_select(out=idf[:, :], in_=idf[:, :], compare_op=ALU.not_equal, fill=1.0, base=0,
                                    pattern=[[-1, P]], channel_multiplier=1).then_inc(c_done, 1)
            for p in range(2):
                pool.sem_inc(px_ready[p], 1)
                pool.sem_inc(ys_free[p], 1)
            pool.wait_ge(lists_ready, 4)

            def gather(e, q, x, j, p):
                pool.wait_ge(px_ready[p], x.before[p] + j + 1).then_inc(own, 1)
                col = e * (MH * ET) + (2 * j + p) * MH
                nc.gpsimd.tensor_copy(idx[p][:, :], tok_s[:, bass.ds(col, MH)]).then_inc(idx_ready[p], 1)
                nc.gpsimd.tensor_copy(wt[p][:, :], wts_s[:, bass.ds(col, MH)]).then_inc(idx_ready[p], 1)
                pool.wait_ge(idx_ready[p], 2 * (x.before[p] + j + 1)).then_inc(own, 1)
                for k in range(MH):
                    nc.gpsimd.indirect_dma_start(out=xg[p][:, k, :], out_offset=None, in_=rows,
                                                 in_offset=bass.IndirectOffsetOnAxis(idx[p][:, k:k + 1], 0),
                                                 bounds_check=T + SPARE - 1, oob_is_err=True).then_inc(xg_in[p], 16)

            def add(x, j, p):
                pool.wait_ge(ys_ready[p], x.before[p] + j + 1).then_inc(own, 1)
                for k in range(MH):
                    nc.gpsimd.indirect_dma_start(out=acc, out_offset=bass.IndirectOffsetOnAxis(idx[p][:, k:k + 1], 0),
                                                 in_=ys[p][:, k, :], in_offset=None, bounds_check=T + SPARE - 1,
                                                 oob_is_err=True, compute_op=ALU.add).then_inc(added[p], 16)
                    pool.wait_ge(added[p], (x.before[p] + j) * (16 * MH) + 16 * (k + 1)).then_inc(own, 1)
                pool.sem_inc(ys_free[p], 1)

            with pool.Fori(0, E // 2) as pair:
                for q in range(2):
                    e = 2 * pair + q
                    x = Expert(pool, e)
                    with pool.Fori(0, ET // 2) as j:
                        with pool.If(j < x.tiles[0]):
                            gather(e, q, x, j, 0)
                        with pool.If(j < x.tiles[1]):
                            gather(e, q, x, j, 1)
                        with pool.If(j < x.tiles[0]):
                            add(x, j, 0)
                        with pool.If(j < x.tiles[1]):
                            add(x, j, 1)

        @block.tensor
        def _(pe):
            pe.sem_inc(pe_done, 2)
            pe.wait_ge(c_done, 2)
            for c in range(2):
                pe.wait_ge(ids_f, c + 1)
                nc.tensor.transpose(ph[c][:, 0:P], ids[:, c, :], idf[:, :]).then_inc(lists_t, 1)
            for c in range(2):
                pe.wait_ge(ids_f, 3)
                nc.tensor.transpose(ph[2 + c][:, 0:P], lst[:, c, :, 1].bitcast(F32), idf[:, :]).then_inc(lists_t, 1)
            pe.wait_ge(lists_ready, 4)

            def start(pair, e, q):
                pe.wait_ge(w_in[q], 64 * (pair + 1)).then_inc(own, 1)

            def body(e, q, x, j, p):
                kp = x.before[p] + j
                k = x.before[0] + x.before[1] + 2 * j + p
                pe.wait_ge(xg_in[p], (kp + 1) * (16 * MH))
                for t in range(MH):
                    for c in range(DC):
                        ins = nc.tensor.transpose(px[p][:, c, t * P:(t + 1) * P], xg[p][:, t, c * P:(c + 1) * P],
                                                  idf[:, :])
                ins.then_inc(px_ready[p], 1)
                pe.wait_ge(xT_ready[p], kp + 1)
                for f in range(FC):
                    pe.wait_ge(h_dve if f % 2 else h_act, FC // 2 * k + f // 2 + 1)
                    for c in range(DC):
                        ins = nc.tensor.matmul(ph[f % 4][:, 0:MT], w1_s[q][:, c, f * P:(f + 1) * P], xT[p][:, c, :],
                                               start=(c == 0), stop=(c == DC - 1))
                    ins.then_inc(h_ready, 1)
                pe.wait_ge(y_free, k + 1)
                for f in range(FC):
                    pe.wait_ge(h_dve if f % 2 else h_act, 2 + FC // 2 * k + f // 2 + 1)
                    for t in range(MH):
                        ins = nc.tensor.matmul(py[t][:, 0:D], hT[:, f, t * P:(t + 1) * P], w2_s[q][:, f, :],
                                               start=(f == 0), stop=(f == FC - 1))
                        if f == FC - 1:
                            ins.then_inc(y_ready, 1)

            def end(pair, e, q, x):
                pe.drain().then_inc(pe_done, 1)

            walk(pe, body, start, end)

        @block.scalar
        def _(act):
            act.sem_inc(act_done, 2)
            act.sem_inc(h_act, 2)
            act.wait_ge(lists_ready, 4)

            def start(pair, e, q):
                act.wait_ge(w_in[q], 64 * (pair + 1)).then_inc(own, 1)

            def body(e, q, x, j, p):
                k = x.before[0] + x.before[1] + 2 * j + p
                act.wait_ge(px_ready[p], x.before[p] + j + 2)
                nc.scalar.copy(xT[p][:, :, :], px[p][:, :, :]).then_inc(xT_ready[p], 1)
                for f in range(0, FC, 2):
                    act.wait_ge(h_ready, FC * k + f + 1)
                    nc.scalar.activation(hT[:, f, :], ph[f % 4][:, 0:MT], ACT.Relu, bias=b1_s[q][:, f:f + 1],
                                         scale=1.0).then_inc(h_act, 1)

            def end(pair, e, q, x):
                act.drain().then_inc(act_done, 1)

            walk(act, body, start, end)

        @block.vector
        def _(dve):
            dve.sem_inc(dve_done, 2)
            dve.sem_inc(h_dve, 2)
            dve.sem_inc(y_free, 1)
            dve.wait_ge(lst_in, 16)
            for c in range(2):
                nc.vector.tensor_copy(ids[:, c, :], lst[:, c, :, 0]).then_inc(ids_f, 1)
            nc.vector.memset(yb[:, :, :], 0.0).then_inc(ids_f, 1)
            dve.wait_ge(lists_t, 4)
            for c in range(2):
                nc.vector.tensor_copy(tok_s[:, c * P:(c + 1) * P], ph[c][:, 0:P]).then_inc(lists_ready, 1)
                nc.vector.tensor_copy(wts_s[:, c * P:(c + 1) * P], ph[2 + c][:, 0:P]).then_inc(lists_ready, 1)
            dve.wait_ge(lists_ready, 4)

            def start(pair, e, q):
                dve.wait_ge(w_in[q], 64 * (pair + 1)).then_inc(own, 1)

            def body(e, q, x, j, p):
                kp = x.before[p] + j
                k = x.before[0] + x.before[1] + 2 * j + p
                for f in range(1, FC, 2):
                    dve.wait_ge(h_ready, FC * k + f + 1)
                    nc.vector.tensor_scalar(hT[:, f, :], ph[f % 4][:, 0:MT], b1_s[q][:, f:f + 1], 0.0,
                                            ALU.add, ALU.max).then_inc(h_dve, 1)
                for t in range(MH):
                    dve.wait_ge(y_ready, MH * k + t + 1)
                    nc.vector.tensor_tensor(yb[:, t, :], py[t][:, 0:D], b2_s[q][:, :], ALU.add
                                            ).then_inc(y_free if t == MH - 1 else yb_ready, 1)
                dve.wait_ge(y_free, k + 2)
                dve.wait_ge(ys_free[p], kp + 1)
                for t in range(MH):
                    ins = nc.vector.tensor_scalar(ys[p][:, t, :], yb[:, t, :], wt[p][:, t:t + 1], None, ALU.mult)
                ins.then_inc(ys_ready[p], 1)

            def end(pair, e, q, x):
                dve.drain().then_inc(dve_done, 1)

            walk(dve, body, start, end)


def last_layernorm(nc, acc, out):
    ctx = ExitStack()
    with ctx:
        def sb(name, shape, dt=F32):
            return ctx.enter_context(nc.sbuf_tensor(name, shape, dt))

        def sem(name):
            return ctx.enter_context(nc.semaphore(name))

        a = [sb(f"a4{i}", [P, NT, D]) for i in range(2)]
        y = [sb(f"y4{i}", [P, NT, D]) for i in range(2)]
        st6 = sb("st64", [P, NT, 6])
        mv = sb("mv4", [P, NT, 2])
        rs = sb("rs4", [P, NT])
        rt = sb("rt4", [P, 3, NT])
        a_in = [sem(f"a_in{i}") for i in range(2)]
        y_out = [sem(f"y_out{i}") for i in range(2)]
        y_ready, d, own = sem("y_ready4"), sem("dve_step4"), sem("own4")
        block = ctx.enter_context(nc.Block())

        @block.sync
        def _(sp):
            sp.sem_inc(y_ready, 2)
            with sp.Fori(0, B // 2) as pair:
                for q in range(2):
                    sp.wait_ge(y_ready, 2 * pair + q + 1)
                    sp.dma_start(a[q][:, :, :], acc[bass.ds(N * (2 * pair + q), N), :].rearrange(
                        "(t p) d -> p t d", p=P)).then_inc(a_in[q], 16)

        @block.scalar
        def _(act):
            for q in range(2):
                act.sem_inc(y_out[q], 16)
            with act.Fori(0, B // 2) as pair:
                for q in range(2):
                    act.wait_ge(y_ready, 2 * pair + q + 3)
                    act.dma_start(out[bass.ds(2 * pair + q, 1), :, :].rearrange("a (t p) d -> p (a t) d", p=P),
                                  y[q][:, :, :]).then_inc(y_out[q], 16)
            for q in range(2):
                act.wait_ge(y_out[q], 16 + 16 * B // 2)

        @block.vector
        def _(dve):
            STEPS = 2 * NT + RSQRT_STEPS + NT - 1
            with dve.Fori(0, B // 2) as pair:
                for q in range(2):
                    base = (2 * pair + q) * STEPS
                    dve.wait_ge(a_in[q], 16 * (pair + 1))
                    for t in range(NT):
                        nc.vector.bn_stats(st6[:, t, :], a[q][:, t, :]).then_inc(d, 1)
                    dve.wait_ge(d, base + NT).then_inc(own, 1)
                    for t in range(NT):
                        nc.vector.bn_aggr(mv[:, t, :], st6[:, t, :]).then_inc(d, 1)
                    dve.wait_ge(d, base + 2 * NT)
                    rsqrt(nc, dve, mv[:, :, 1], rs[:, :], [rt[:, k, :] for k in range(3)], d, base + 2 * NT)
                    dve.wait_ge(d, base + 2 * NT + RSQRT_STEPS)
                    dve.wait_ge(y_out[q], 16 * (pair + 1))
                    for t in range(NT):
                        nc.vector.tensor_scalar(y[q][:, t, :], a[q][:, t, :], mv[:, t, 0:1], rs[:, t:t + 1],
                                                ALU.subtract, ALU.mult).then_inc(y_ready if t == NT - 1 else d, 1)


def build(nc, w, out):
    scratch_qk = nc.dram_tensor("scratch_qk", (2, 2, 2, P, N), F32).ap()
    scratch_o = nc.dram_tensor("scratch_o", (4 * B, P, N), F32).ap()
    rows = nc.dram_tensor("rows", (T + SPARE, D), F32).ap()
    acc = nc.dram_tensor("acc", (T + SPARE, D), F32).ap()
    slots = nc.dram_tensor("slots", (E * T, 2), I32).ap()
    attention(nc, w["x"], w["mt"], w, w["rel"], scratch_qk, scratch_o)
    with nc.sbuf_tensor("table", [1, 2, 2, E], I32) as table:
        after_attention(nc, w, scratch_o, rows, acc, slots, table)
        experts(nc, w, rows, acc, slots, table)
        last_layernorm(nc, acc, out)


def interpolation():
    import numpy as np
    pos = np.arange(N, dtype=np.float32) * np.float32((S - 1) / (N - 1))
    low = np.floor(pos).astype(np.int32)
    frac = pos - low.astype(np.float32)
    m = np.zeros((N, S), np.float32)
    np.add.at(m, (np.arange(N), low), np.float32(1) - frac)
    np.add.at(m, (np.arange(N), np.minimum(low + 1, S - 1)), frac)
    m[-1] = 0
    return np.ascontiguousarray(m.T)


def kernel(**inputs):
    import numpy as np
    import concourse.bacc as bacc
    from concourse.bass_utils import run_bass_kernel_spmd

    a = {k: np.asarray(v) for k, v in inputs.items()}

    def by_lane(wt):
        return wt.reshape(2, HH, DH, D).transpose(3, 0, 2, 1).reshape(D, D)

    arrays = {
        "x": a["L0_attn_x"], "mt": interpolation(), "rel": a["L0_attn_rel_bias"],
        "wq": by_lane(a["L0_attn_Wq"]), "wk": by_lane(a["L0_attn_Wk"]),
        "wv": a["L0_attn_Wv"].T, "wo": a["L0_attn_Wo"].T,
        "bq": a["L0_attn_bq"].reshape(2, HH, DH).transpose(2, 1, 0).reshape(P, 2),
        "bk": a["L0_attn_bk"].reshape(2, HH, DH).transpose(2, 1, 0).reshape(P, 2),
        "bv": a["L0_attn_bv"], "bo": a["L0_attn_bo"],
        "gamma": a["L0_attn_gamma"].reshape(DC, P).T, "beta": a["L0_attn_beta"].reshape(DC, P).T,
        "wg": a["L0_ffn_W_gate"], "w1": a["L0_ffn_W1"],
        "b1": a["L0_ffn_b1"].reshape(E, FC, P).transpose(0, 2, 1),
        "w2": a["L0_ffn_W2"], "b2": a["L0_ffn_b2"],
    }
    arrays = {k: np.ascontiguousarray(v) for k, v in arrays.items()}
    nc = bacc.Bacc("TRN2", target_bir_lowering=False, num_devices=1)
    w = {k: nc.dram_tensor("in_" + k, v.shape, mybir.dt.from_np(v.dtype), kind="ExternalInput").ap()
         for k, v in arrays.items()}
    out = nc.dram_tensor("out", (B, N, D), F32, kind="ExternalOutput").ap()
    build(nc, w, out)
    r = run_bass_kernel_spmd(nc, [{"in_" + k: v for k, v in arrays.items()}], core_ids=[0])
    return r.results[0]["out"]
```

```python
from contextlib import ExitStack

import concourse.bass as bass
from concourse import mybir
from concourse.alu_op_type import AluOpType as ALU

ACT = mybir.ActivationFunctionType
AX = mybir.AxisListType
F32 = mybir.dt.float32
F32R = mybir.dt.float32r
BF16 = mybir.dt.bfloat16
I32 = mybir.dt.int32

P = 128
B, N, D = 8, 512, 256
T = B * N
H, DH = 16, 16
S = 32
HH = H // 2
NT = N // P
DC = D // P
VW = 32
BANK = 512
PAIRS = HH // 2
JOBS = 5
UJOBS = PAIRS * JOBS
ST_BANKS, MX_BANKS = 4, 2
SCALE = DH ** -0.5
EPS = 1e-5
MASKED = -1e30
E, TOPK, FF = 8, 2, 4 * D
FC = FF // P
TT = T // P
MT = 256
MH = MT // P
ET = T // MT
SPARE = P
PROLOGUE_GEN = 9
STEP_GEN = (6, 4)
GEN = sum(STEP_GEN)


def score_jobs(first_wide):
    wide = (lambda t: N - t * P) if first_wide else (lambda t: (t + 1) * P)
    order = (0, 1, 3, 2) if first_wide else (3, 2, 0, 1)
    full, long, short, half = order
    jobs = []
    for a in range(2):
        jobs.append([(a, full, wide(full), 0)])
        jobs.append([(a, long, wide(long), 0), (a, short, wide(short), wide(long))])
    jobs.append([(0, half, wide(half), 0), (1, half, wide(half), wide(half))])
    return jobs


KEY_JOBS = score_jobs(True)
QUERY_JOBS = score_jobs(False)


NEWTON = 3
RSQRT_STEPS = 3 + 3 * NEWTON


def rsqrt(nc, dve, var, y, tmp, done, base):
    nc.vector.tensor_scalar(tmp[0], var, EPS, None, ALU.add).then_inc(done, 1)
    dve.wait_ge(done, base + 1)
    nc.vector.tensor_scalar(tmp[1].bitcast(I32), tmp[0].bitcast(I32), 1, None, ALU.arith_shift_right).then_inc(done, 1)
    dve.wait_ge(done, base + 2)
    nc.vector.tensor_scalar(y.bitcast(I32), tmp[1].bitcast(I32), -1.0, float(0x5F3759DF), ALU.mult, ALU.add
                            ).then_inc(done, 1)
    for k in range(NEWTON):
        dve.wait_ge(done, base + 3 + 3 * k)
        nc.vector.scalar_tensor_tensor(tmp[1], y, -0.5, y, ALU.mult, ALU.mult).then_inc(done, 1)
        dve.wait_ge(done, base + 4 + 3 * k)
        nc.vector.tensor_tensor(tmp[2], tmp[1], tmp[0], ALU.mult).then_inc(done, 1)
        dve.wait_ge(done, base + 5 + 3 * k)
        nc.vector.scalar_tensor_tensor(y, tmp[2], 1.5, y, ALU.add, ALU.mult).then_inc(done, 1)


def attention(nc, x, mt, w, rel, scratch_qk, scratch_o):
    ctx = ExitStack()
    with ctx:
        def sb(name, shape, dt=F32):
            return ctx.enter_context(nc.sbuf_tensor(name, shape, dt))

        def pb(name, shape, dt=F32):
            return ctx.enter_context(nc.psum_tensor(name, shape, dt))

        def sem(name):
            return ctx.enter_context(nc.semaphore(name))

        qs = sb("qs", [P, 2, HH, N], F32R)
        ks = sb("ks", [P, 2, HH, N], F32R)
        qs2 = sb("qs2", [P, 2, HH, N], F32R)
        ks2 = sb("ks2", [P, N], F32R)
        probs = sb("probs", [P, 2, 2 * JOBS, BANK])
        vaug = sb("vaug", [P, 2, NT, HH, VW])
        wq_s = sb("wq_s", [P, DC, D])
        wk_s = sb("wk_s", [P, DC, D])
        wv_s = sb("wv_s", [P, DC, D])
        bq_s = sb("bq_s", [P, 2])
        bq4 = sb("bq4", [P, 2])
        bk_s = sb("bk_s", [P, 2])
        bv_s = sb("bv_s", [P, D])
        gam = sb("gam", [P, DC])
        bet = sb("bet", [P, DC])
        xt = sb("xt", [P, NT, D])
        xh = sb("xh", [P, NT, D])
        xnt = sb("xnt", [P, DC, N])
        qf = sb("qf", [P, 2, N])
        qsp = sb("qsp", [P, 2, 2, N], F32R)
        mx = sb("mx", [P, HH, NT])
        negm = sb("negm", [HH * NT, P], F32R)
        ov = sb("ov", [P, 2, N])
        st6 = sb("st6", [P, NT, 6])
        mv = sb("mv", [P, NT, 2])
        rs = sb("rs", [P, NT])
        rt = sb("rt", [P, 3, NT])
        idf = sb("idf", [P, P])
        idb = sb("idb", [P, P], BF16)
        mask_q = sb("mask_q", [P, P], BF16)
        mask_k = sb("mask_k", [P, P], BF16)
        mtf = xt[:, 0:2, :].rearrange("p a n -> p (a n)")
        relr = probs[0:S, 0, 0:4, :].rearrange("p a n -> p (a n)")[:, 0:H * 2 * S].rearrange(
            "p (h a j) -> p h a j", h=H, a=2)
        rhi = qsp[:, 0, 0, :]

        st = [pb(f"st{i}", [P, BANK]) for i in range(ST_BANKS)]
        sm = [pb(f"sm{i}", [P, BANK]) for i in range(MX_BANKS)]
        po = pb("po", [P, BANK])
        pg = pb("pg", [P, BANK])

        w_in, x_in = sem("w_in"), sem("x_in")
        consts = sem("consts")
        r_ready, r_used = sem("r_ready"), sem("r_used")
        ks_const = sem("ks_const")
        ln_step, stats_seen, xh_ready = sem("ln_step"), sem("stats_seen"), sem("xh_ready")
        gen_ready, gen_free = sem("gen_ready"), sem("gen_free")
        split_step, split_ready = sem("split_step"), sem("split_ready")
        scr_out = [sem(f"scr_out{i}") for i in range(2)]
        rows_in = [sem(f"rows_in{i}") for i in range(2)]
        st_ready, st_free = sem("st_ready"), sem("st_free")
        sm_ready, sm_free = sem("sm_ready"), sem("sm_free")
        max_in = sem("max_in")
        pv_ready, pv_free = sem("pv_ready"), sem("pv_free")
        o_out = [sem(f"o_out{i}") for i in range(2)]
        block = ctx.enter_context(nc.Block())

        WEIGHTS = 14

        def xnt_at(c):
            return xnt[:, c, :]

        @block.sync
        def _(sp):
            sp.sem_inc(scr_out[1], 32)
            for dst, src in (
                (mtf[0:S, :], mt), (mtf[64:96, :], mt), (mtf[96:128, :], mt),
                (relr[:, :, 0, :], rel.rearrange("h i j -> i h j")),
                (relr[:, :, 1, :], rel.rearrange("h i j -> i h j")),
                (wq_s[:, :, :], w["wq"].rearrange("(k p) o -> p k o", p=P)),
                (wk_s[:, :, :], w["wk"].rearrange("(k p) o -> p k o", p=P)),
                (wv_s[:, :, :], w["wv"].rearrange("(k p) o -> p k o", p=P)),
                (bq_s[:, :], w["bq"]), (bk_s[:, :], w["bk"]),
                (bv_s[:, :], w["bv"].partition_broadcast(P)),
                (gam[:, :], w["gamma"]), (bet[:, :], w["beta"]),
                (xh[:, :, :], x[0].rearrange("(t p) d -> p t d", p=P)),
            ):
                sp.dma_start(dst, src).then_inc(w_in, 16)

            def load_x(b):
                sp.dma_start(xt[:, :, :], x[bass.ds(b, 1), :, :].rearrange("a (t p) d -> p (a t) d", p=P)
                             ).then_inc(x_in, 16)

            def store_split(b, half):
                un = 2 * b + half
                for a in range(2):
                    sp.wait_ge(split_ready, 2 * un + a + 1)
                    sp.dma_start(scratch_qk[half, a].rearrange("t p n -> p t n"), qsp[:, a, :, :].bitcast(F32)
                                 ).then_inc(scr_out[half], 16)

            def load_rows(b, half):
                sp.wait_ge(scr_out[half], 32 * (b + 1 + half))
                q_parts = scratch_qk[half, 0].rearrange("t (i h) n -> (t i) (h n)", h=HH)
                k_parts = scratch_qk[half, 1].rearrange("t (i h) n -> t i (h n)", h=HH)
                for r in range(2):
                    sp.dma_start(qs[2 * DH * r:2 * DH * (r + 1), half, :, :].bitcast(F32).rearrange(
                        "p h n -> p (h n)"), q_parts).then_inc(rows_in[half], 16)
                for r in range(4):
                    sp.dma_start(ks[DH * r:DH * (r + 1), half, :, :].bitcast(F32).rearrange(
                        "p h n -> p (h n)"), k_parts[r // 2]).then_inc(rows_in[half], 16)

            def load_max(g, half):
                sp.wait_ge(gen_free, g + 1)
                sp.dma_start(qs2[0:1, half, :, :].bitcast(F32).rearrange("p h (t n) -> p (h t) n", n=P),
                             negm[:, :].bitcast(F32)).then_inc(max_in, 16)

            def store_o(b, half, q):
                un = 2 * b + half
                sp.wait_ge(pv_free, 1 + 2 * un + q + 1)
                sp.dma_start(scratch_o[bass.ds(4 * b + 2 * half + q, 1), :, :].rearrange("a p n -> (a p) n"),
                             ov[:, q, :]).then_inc(o_out[q], 16)

            def step(b, half, more):
                un = 2 * b + half
                g = PROLOGUE_GEN + GEN * b + half * STEP_GEN[0]
                if more and half == 0:
                    sp.wait_ge(xh_ready, NT * (b + 1))
                    load_x(b + 1)
                if more:
                    store_split(b + 1, half)
                store_o(b, half, 0)
                if more:
                    sp.wait_ge(st_ready, UJOBS * (un + 1))
                    load_rows(b + 1, half)
                if more or half == 0:
                    load_max(g + (2 if half == 0 else 0) + 2 if more else g, 1 - half)
                store_o(b, half, 1)

            for half in range(2):
                store_split(0, half)
            for half in range(2):
                load_rows(0, half)
            load_max(PROLOGUE_GEN - 1, 0)
            with sp.Fori(0, B - 1) as b:
                for half in range(2):
                    step(b, half, True)
            for half in range(2):
                step(B - 1, half, False)
            for q in range(2):
                sp.wait_ge(o_out[q], 16 + 16 * 2 * B)

        @block.gpsimd
        def _(pool):
            nc.gpsimd.memset(idf[:, :], 0.0).then_inc(consts, 1)
            nc.gpsimd.memset(idb[:, :], 0.0).then_inc(consts, 1)
            nc.gpsimd.memset(mask_q[:, :], 0.0).then_inc(consts, 1)
            nc.gpsimd.memset(mask_k[:, :], 0.0).then_inc(consts, 1)
            nc.gpsimd.memset(vaug[:, :, :, :, :], 0.0).then_inc(consts, 1)
            pool.wait_ge(consts, 5)
            for t in (idf, idb):
                nc.gpsimd.affine_select(out=t[:, :], in_=t[:, :], compare_op=ALU.not_equal, fill=1.0, base=0,
                                        pattern=[[-1, P]], channel_multiplier=1).then_inc(consts, 1)
            nc.gpsimd.affine_select(out=mask_q[:, :], in_=mask_q[:, :], compare_op=ALU.is_ge, fill=MASKED, base=0,
                                    pattern=[[-1, P]], channel_multiplier=1).then_inc(consts, 1)
            nc.gpsimd.affine_select(out=mask_k[:, :], in_=mask_k[:, :], compare_op=ALU.is_ge, fill=MASKED, base=0,
                                    pattern=[[1, P]], channel_multiplier=-1).then_inc(consts, 1)
            nc.gpsimd.memset(vaug[:, :, :, :, DH:DH + 1], 1.0).then_inc(consts, 1)
            nc.gpsimd.memset(qs2[0:64, :, :, :].bitcast(F32), 0.0).then_inc(consts, 1)
            nc.gpsimd.memset(ks2[0:64, :].bitcast(F32), 0.0).then_inc(consts, 1)
            pool.wait_ge(consts, 12)
            nc.gpsimd.memset(ks2[0:1, :].bitcast(F32), 1.0).then_inc(consts, 1)

        CONSTS = 13

        @block.scalar
        def _(act):
            act.sem_inc(st_free, ST_BANKS)
            act.sem_inc(pv_free, 1)
            act.sem_inc(o_out[0], 16)
            act.sem_inc(o_out[1], 16)
            act.wait_ge(w_in, 16 * WEIGHTS)
            nc.scalar.mul(bq4[:, :], bq_s[:, :], SCALE).then_inc(r_used, 1)
            act.wait_ge(r_used, 1)

            def project_out(un, half, a, g):
                act.wait_ge(gen_ready, g + 1)
                if a == 0:
                    nc.scalar.activation(qf[:, 0, :], pg[:, :], ACT.Identity, bias=bq4[:, half:half + 1],
                                         scale=SCALE).then_inc(gen_free, 1)
                else:
                    nc.scalar.activation(qf[:, 1, :], pg[:, :], ACT.Identity, bias=bk_s[:, half:half + 1],
                                         scale=1.0).then_inc(gen_free, 1)

            def exps(un, half, pair):
                q = pair // 2
                if pair % 2 == 0:
                    act.wait_ge(pv_ready, 2 * un + q + 1)
                for j in range(JOBS):
                    job = UJOBS * un + JOBS * pair + j
                    act.wait_ge(st_ready, job + 1)
                    nc.scalar.activation(probs[:, q, JOBS * (pair % 2) + j, :], st[(JOBS * pair + j) % ST_BANKS][:, :],
                                         ACT.Exp).then_inc(st_free, 1)

            def o_from_psum(un, q):
                act.wait_ge(pv_ready, 2 + 2 * un + q + 1)
                act.wait_ge(o_out[q], 16 * (un + 1))
                nc.scalar.copy(ov[:, q, :], po[:, :]).then_inc(pv_free, 1)

            act.sem_inc(pv_ready, 2)
            for half in range(2):
                for a in range(2):
                    if half:
                        act.wait_ge(split_ready, 2 * (half - 1) + a + 1)
                    project_out(half, half, a, 2 + 3 * half + a)

            def step(b, half, more):
                un = 2 * b + half
                g = PROLOGUE_GEN + GEN * b + half * STEP_GEN[0]
                for pair in range(3):
                    exps(un, half, pair)
                o_from_psum(un, 0)
                if more:
                    for a in range(2):
                        act.wait_ge(split_ready, 2 * (un + 1) + a + 1)
                        project_out(un + 2, half, a, g + (2 if half == 0 else 0) + a)
                exps(un, half, 3)
                o_from_psum(un, 1)

            with act.Fori(0, B - 1) as b:
                for half in range(2):
                    step(b, half, True)
            for half in range(2):
                step(B - 1, half, False)

        @block.vector
        def _(dve):
            dve.sem_inc(sm_free, MX_BANKS)
            dve.wait_ge(w_in, 16 * WEIGHTS)

            nc.vector.tensor_copy(ks[64:128, 0, 0, :], mtf[64:128, :]).then_inc(ks_const, 1)
            dve.wait_ge(ks_const, 1)
            nc.vector.tensor_tensor(ks2[64:128, :], mtf[64:128, :], ks[64:128, 0, 0, :].bitcast(F32), ALU.subtract
                                    ).then_inc(ks_const, 1)
            for half in range(2):
                for h in range(HH):
                    if half + h:
                        nc.vector.tensor_copy(ks[64:128, half, h, :], mtf[64:128, :]).then_inc(ks_const, 1)
            for h in range(H):
                dve.wait_ge(r_ready, h + 1)
                if h:
                    dve.wait_ge(ks_const, 1 + H + 3 * h)
                nc.vector.tensor_copy(rhi[64:128, :], st[h % 2][64:128, :]).then_inc(ks_const, 1)
                dve.wait_ge(ks_const, 1 + H + 3 * h + 1)
                nc.vector.tensor_copy(qs[64:96, h // HH, h % HH, :], rhi[64:96, :].bitcast(F32)).then_inc(ks_const, 1)
                nc.vector.tensor_tensor(qs[96:128, h // HH, h % HH, :], st[h % 2][96:128, :],
                                        rhi[96:128, :].bitcast(F32), ALU.subtract).then_inc(ks_const, 1)
            dve.wait_ge(ks_const, 1 + H + 3 * H)
            nc.vector.tensor_copy(qs2[64:128, :, :, :], qs[64:128, :, :, :].bitcast(F32)).then_inc(ks_const, 1)

            def layernorm(src, n):
                base = (2 * NT + RSQRT_STEPS) * n
                for t in range(NT):
                    nc.vector.bn_stats(st6[:, t, :], src[:, t, :]).then_inc(ln_step, 1)
                dve.wait_ge(ln_step, base + NT).then_inc(stats_seen, 1)
                for t in range(NT):
                    nc.vector.bn_aggr(mv[:, t, :], st6[:, t, :]).then_inc(ln_step, 1)
                dve.wait_ge(ln_step, base + 2 * NT)
                rsqrt(nc, dve, mv[:, :, 1], rs[:, :], [rt[:, k, :] for k in range(3)], ln_step, base + 2 * NT)
                dve.wait_ge(ln_step, base + 2 * NT + RSQRT_STEPS)
                for t in range(NT):
                    nc.vector.tensor_scalar(xh[:, t, :], src[:, t, :], mv[:, t, 0:1], rs[:, t:t + 1],
                                            ALU.subtract, ALU.mult).then_inc(xh_ready, 1)

            def xnt_out(g):
                for c in range(DC):
                    dve.wait_ge(gen_ready, g + c + 1)
                    nc.vector.tensor_scalar(xnt[:, c, :], pg[:, :], gam[:, c:c + 1], bet[:, c:c + 1],
                                            ALU.mult, ALU.add).then_inc(gen_free, 1)

            def split(b, half, a, g):
                un = 2 * b + half
                dve.wait_ge(gen_free, g + 1)
                if half:
                    dve.wait_ge(scr_out[0], 32 * (b + 1))
                else:
                    dve.wait_ge(scr_out[1], 32 * (b + 1))
                nc.vector.tensor_copy(qsp[:, a, 0, :], qf[:, a, :]).then_inc(split_step, 1)
                dve.wait_ge(split_step, 2 * un + a + 1)
                nc.vector.tensor_tensor(qsp[:, a, 1, :], qf[:, a, :], qsp[:, a, 0, :].bitcast(F32), ALU.subtract
                                        ).then_inc(split_ready, 1)

            def v_out(half, g):
                dve.wait_ge(gen_ready, g + 1)
                nc.vector.tensor_tensor(
                    vaug[:, half, :, :, 0:DH], pg[:, :].rearrange("p (t h d) -> p t h d", t=NT, h=HH),
                    bv_s[:, half * P:(half + 1) * P].rearrange("p (a h d) -> p a h d", a=1, h=HH).to_broadcast(
                        [P, NT, HH, DH]), ALU.add).then_inc(gen_free, 1)

            def maxima(un, pair):
                for j, job in enumerate(QUERY_JOBS):
                    dve.wait_ge(sm_ready, UJOBS * un + JOBS * pair + j + 1)
                    bank = sm[(JOBS * pair + j) % MX_BANKS]
                    if job[0][2] == job[-1][2] and len(job) == 2:
                        t = job[0][1]
                        ins = nc.vector.tensor_reduce(
                            mx[:, 2 * pair:2 * pair + 2, t], bank[:, :].rearrange("p (a m) -> p a m", a=2), AX.X, ALU.max)
                    else:
                        for a, t, cols, at in job:
                            ins = nc.vector.tensor_reduce(mx[:, 2 * pair + a, t:t + 1], bank[:, at:at + cols],
                                                          AX.X, ALU.max)
                    ins.then_inc(sm_free, 1)

            def neg_out(un, g):
                dve.wait_ge(gen_ready, g + 1)
                if not isinstance(un, int) or un:
                    dve.wait_ge(max_in, 16 * un)
                nc.vector.tensor_scalar(negm[:, :], pg[0:HH * NT, 0:P], -1.0, None, ALU.mult).then_inc(gen_free, 1)

            layernorm(xh, 0)
            xnt_out(0)
            for half in range(2):
                for a in range(2):
                    split(0, half, a, 2 + 3 * half + a)
                v_out(half, 4 + 3 * half)
            for pair in range(PAIRS):
                maxima(0, pair)
            neg_out(0, PROLOGUE_GEN - 1)

            def step(b, half, more):
                un = 2 * b + half
                g = PROLOGUE_GEN + GEN * b + half * STEP_GEN[0]
                if more and half == 0:
                    dve.wait_ge(x_in, 16 * (b + 1))
                    layernorm(xt, b + 1)
                    xnt_out(g)
                if more or half == 0:
                    qk = g + (2 if half == 0 else 0)
                    neg = qk + 2 if more else g
                    for pair in range(PAIRS):
                        if more and pair in (1, 2):
                            split(b + 1, half, pair - 1, qk + pair - 1)
                        maxima(un + 1, pair)
                    neg_out(un + 1, neg)
                    if more:
                        v_out(half, neg + 1)

            with dve.Fori(0, B - 1) as b:
                for half in range(2):
                    step(b, half, True)
            for half in range(2):
                step(B - 1, half, False)

        @block.tensor
        def _(pe):
            pe.wait_ge(w_in, 16 * WEIGHTS)
            for h in range(H):
                if h >= 2:
                    pe.wait_ge(ks_const, 1 + H + 3 * (h - 1))
                nc.tensor.matmul(st[h % 2][64:128, :], relr[:, h, :, :].rearrange("p a j -> p (a j)"), mtf[0:S, :],
                                 start=True, stop=True).then_inc(r_ready, 1)
            pe.wait_ge(consts, CONSTS)
            pe.wait_ge(ks_const, 2 + H + 3 * H)

            def free_gen(g):
                if not isinstance(g, int) or g:
                    pe.wait_ge(gen_free, g)

            def transpose_x(b, g):
                for c in range(DC):
                    free_gen(g + c)
                    if c == 0:
                        pe.wait_ge(xh_ready, NT * (b + 1))
                    for t in range(NT):
                        ins = nc.tensor.transpose(pg[:, t * P:(t + 1) * P], xh[:, t, c * P:(c + 1) * P], idf[:, :])
                    ins.then_inc(gen_ready, 1)

            def project(half, wts, g):
                free_gen(g)
                for c in range(DC):
                    ins = nc.tensor.matmul(pg[:, :], wts[:, c, half * P:(half + 1) * P], xnt_at(c),
                                           start=(c == 0), stop=(c == DC - 1))
                ins.then_inc(gen_ready, 1)

            def project_v(half, g):
                free_gen(g)
                for t in range(NT):
                    for c in range(DC):
                        ins = nc.tensor.matmul(pg[:, t * P:(t + 1) * P], xnt[:, c, t * P:(t + 1) * P],
                                               wv_s[:, c, half * P:(half + 1) * P],
                                               start=(t == 0 and c == 0), stop=(c == DC - 1), skip_group_check=True)
                ins.then_inc(gen_ready, 1)

            def query_scores(un, half, pair):
                for j, job in enumerate(QUERY_JOBS):
                    pe.wait_ge(sm_free, UJOBS * un + JOBS * pair + j + 1)
                    bank = sm[(JOBS * pair + j) % MX_BANKS]
                    for n, (a, t, cols, at) in enumerate(job):
                        h = 2 * pair + a
                        nc.tensor.matmul(bank[:, at:at + cols], qs[:, half, h, t * P:(t + 1) * P],
                                         ks[:, half, h, 0:cols], start=(n == 0), stop=False, skip_group_check=True)
                        ins = nc.tensor.matmul(bank[:, at + cols - P:at + cols], idb[:, :], mask_q[:, :],
                                               start=False, stop=True, skip_group_check=True)
                    ins.then_inc(sm_ready, 1)

            def key_scores(un, half, pair):
                for j, job in enumerate(KEY_JOBS):
                    pe.wait_ge(st_free, UJOBS * un + JOBS * pair + j + 1)
                    bank = st[(JOBS * pair + j) % ST_BANKS]
                    for n, (a, t, cols, at) in enumerate(job):
                        h = 2 * pair + a
                        out = bank[:, at:at + cols]
                        nc.tensor.matmul(out, ks[:, half, h, t * P:(t + 1) * P], qs[:, half, h, t * P:N],
                                         start=(n == 0), stop=False, skip_group_check=True)
                        nc.tensor.matmul(out, ks2[:, t * P:(t + 1) * P], qs2[:, half, h, t * P:N],
                                         start=False, stop=False, skip_group_check=True)
                        ins = nc.tensor.matmul(bank[:, at:at + P], idb[:, :], mask_k[:, :],
                                               start=False, stop=True, skip_group_check=True)
                    ins.then_inc(st_ready, 1)

            def transpose_max(un, g):
                pe.wait_ge(sm_free, MX_BANKS + UJOBS * (un + 1))
                free_gen(g)
                nc.tensor.transpose(pg[0:HH * NT, 0:P], mx[:, :, :].rearrange("p h t -> p (h t)"), idf[:, :]
                                    ).then_inc(gen_ready, 1)

            def values(un, half, q):
                pe.wait_ge(st_free, ST_BANKS + UJOBS * un + 2 * JOBS * (q + 1))
                pe.wait_ge(pv_free, 2 * un + q + 1)
                for t in range(NT):
                    for r in range(4):
                        pr, a = divmod(r, 2)
                        j, at = [(j, c[3]) for j, job in enumerate(KEY_JOBS) for c in job if c[:2] == (a, t)][0]
                        ins = nc.tensor.matmul(po[VW * r:VW * (r + 1), t * P:N], vaug[:, half, t, 4 * q + r, :],
                                               probs[:, q, JOBS * pr + j, at:at + N - t * P],
                                               start=(t == 0), stop=(t == NT - 1), skip_group_check=True,
                                               tile_position=(0, VW * r))
                ins.then_inc(pv_ready, 1)

            transpose_x(0, 0)
            for half in range(2):
                project(half, wq_s, 2 + 3 * half)
                project(half, wk_s, 3 + 3 * half)
                project_v(half, 4 + 3 * half)
            pe.wait_ge(rows_in[0], 96)
            for pair in range(PAIRS):
                query_scores(0, 0, pair)
            transpose_max(0, PROLOGUE_GEN - 1)

            def step(b, half, more):
                un = 2 * b + half
                g = PROLOGUE_GEN + GEN * b + half * STEP_GEN[0]
                ahead = more or half == 0
                qk = g + (2 if half == 0 else 0)
                neg = qk + 2 if more else g
                pe.wait_ge(max_in, 16 * (un + 1))
                key_scores(un, half, 0)
                key_scores(un, half, 1)
                if more and half == 0:
                    transpose_x(b + 1, g)
                if ahead:
                    pe.wait_ge(rows_in[1 - half], 96 * (b + 1 + half))
                    query_scores(un + 1, 1 - half, 0)
                key_scores(un, half, 2)
                values(un, half, 0)
                if more:
                    project(half, wq_s, qk)
                if ahead:
                    query_scores(un + 1, 1 - half, 1)
                if more:
                    project(half, wk_s, qk + 1)
                if ahead:
                    query_scores(un + 1, 1 - half, 2)
                key_scores(un, half, 3)
                if ahead:
                    query_scores(un + 1, 1 - half, 3)
                    transpose_max(un + 1, neg)
                values(un, half, 1)
                if more:
                    project_v(half, neg + 1)

            with pe.Fori(0, B - 1) as b:
                for half in range(2):
                    step(b, half, True)
            for half in range(2):
                step(B - 1, half, False)


BIG = float(1 << 20)
RANKS = E


def after_attention(nc, w, scratch_o, rows, acc, slots, table):
    ctx = ExitStack()
    with ctx:
        def sb(name, shape, dt=F32):
            return ctx.enter_context(nc.sbuf_tensor(name, shape, dt))

        def pb(name, shape, dt=F32):
            return ctx.enter_context(nc.psum_tensor(name, shape, dt))

        def sem(name):
            return ctx.enter_context(nc.semaphore(name))

        wo_s = sb("wo_s", [P, DC, D])
        bo_s = sb("bo_s", [P, D])
        wg_s = sb("wg_s", [P, DC, E])
        idf = sb("idf2", [P, P])
        below = sb("below", [P, P], BF16)
        ones = sb("ones", [P, P], BF16)
        zero = sb("zero", [P, D])
        empty = sb("empty", [P, 2, P, 2], I32)
        ov = sb("ov2", [P, 4, N])
        xt = sb("xt2", [P, NT, D])
        xb = sb("xb2", [P, NT, D])
        rec = sb("rec", [P, NT, H])
        oh = sb("oh", [P, NT, D])
        oT = sb("oT", [P, NT, DC * P])
        res = sb("res", [P, NT, D])
        st6 = sb("st62", [P, NT, 6])
        mv = sb("mv2", [P, NT, 2])
        rs = sb("rs2", [P, NT])
        rt = sb("rt2", [P, 3, NT])
        x1 = sb("x1", [P, NT, D])
        x1T = sb("x1T", [P, NT, DC * P])
        gate = sb("gate", [P, NT, E])
        top = sb("top", [P, NT, E])
        picked = sb("picked", [P, NT, E])
        picked_b = sb("picked_b", [P, NT, E], BF16)
        before = sb("before", [P, NT + 1, E], BF16)
        expo = sb("expo", [P, NT, E])
        expm = sb("expm", [P, NT, E])
        tot = sb("tot", [P, NT])
        rtot = sb("rtot", [P, NT])
        wt = sb("wt", [P, NT, E])
        cums = [sb(f"cum{i}", [P, NT, 2 * E]) for i in range(4)]
        ebase = sb("ebase", [P, NT, E])
        slot = sb("slot", [P, NT, E])
        rank = sb("rank", [P, RANKS, E])
        pick = sb("pick", [P, NT, RANKS, E])
        pickm = sb("pickm", [P, NT, RANKS, E])
        tmp1 = sb("tmp1", [P, NT, RANKS, E])
        tmp2 = sb("tmp2", [P, NT, RANKS, E])
        idxf = sb("idxf", [P, NT, RANKS])
        idx = sb("idx", [P, NT, RANKS], I32)
        pay = sb("pay", [P, NT, RANKS, 2], I32)
        tied = sb("tied", [1, 4])
        tied_i = sb("tied_i", [1, 2], I32)
        cnt = sb("cnt", [1, E])
        over = sb("over", [1, E, ET])
        lim = sb("lim", [1, E, ET])
        tiles = sb("tiles", [1, E])
        tcum = [sb(f"tcum{i}", [1, 1, 2 * E]) for i in range(4)]
        tokf = sb("tokf", [P, NT, RANKS])

        pa = pb("pa", [P, NT, BANK])
        pt = pb("pt", [P, 2, BANK])
        pc = pb("pc", [P, 2, BANK])

        w_in, o_in, x_in = sem("w_in2"), sem("o_in"), sem("x_in2")
        c_done = sem("c_done")
        spare_out, empty_out = sem("spare_out"), sem("empty_out")
        xb_ready = sem("xb_ready")
        a_ready, oh_ready, b_ready, oT_ready = sem("a_ready"), sem("oh_ready"), sem("b_ready"), sem("oT_ready")
        c_ready, d = sem("c_ready"), sem("dve_step")
        x1_ready, d_ready, x1T_ready, g_ready = sem("x1_ready"), sem("d_ready"), sem("x1T_ready"), sem("g_ready")
        diff_ready, expo_ready, picked_ready = sem("diff_ready"), sem("expo_ready"), sem("picked_ready")
        pos_ready, idx_ready, x1_out = sem("pos_ready"), sem("idx_ready"), sem("x1_out")
        scat, scat_ties, own = sem("scat"), sem("scat_ties"), sem("own")
        table_ready, lists_out = sem("table_ready"), sem("lists_out")
        block = ctx.enter_context(nc.Block())

        CONSTS = 20

        @block.sync
        def _(sp):
            sp.sem_inc(x1_out, 32)
            for dst, src in ((wo_s[:, :, :], w["wo"].rearrange("(k p) o -> p k o", p=P)),
                             (bo_s[:, :], w["bo"].partition_broadcast(P)),
                             (wg_s[:, :, :], w["wg"].rearrange("(k p) e -> p k e", p=P))):
                sp.dma_start(dst, src).then_inc(w_in, 16)
            sp.wait_ge(c_done, CONSTS)
            sp.dma_start(rows[T:T + SPARE, :], zero[:, :]).then_inc(spare_out, 16)
            sp.dma_start(acc[T:T + SPARE, :], zero[:, :]).then_inc(spare_out, 16)
            sp.dma_start(slots.rearrange("(p s) c -> p (s c)", p=P), empty[:, :, :, :].rearrange("p a s c -> p (a s c)")
                         ).then_inc(empty_out, 16)
            with sp.Fori(0, B) as b:
                sp.wait_ge(a_ready, b + 1)
                sp.dma_start(ov[:, :, :], scratch_o[bass.ds(4 * b, 4), :, :].rearrange("q p n -> p q n")
                             ).then_inc(o_in, 16)
                sp.wait_ge(xb_ready, b + 1)
                sp.dma_start(xt[:, :, :], w["x"][bass.ds(b, 1), :, :].rearrange("a (t p) d -> p (a t) d", p=P)
                             ).then_inc(x_in, 16)
                sp.wait_ge(x1_ready, b + 1)
                for dst in (rows, acc):
                    sp.dma_start(dst[bass.ds(N * b, N), :].rearrange("(t p) d -> p t d", p=P), x1[:, :, :]
                                 ).then_inc(x1_out, 16)
            sp.wait_ge(x1_out, 32 + 32 * B)
            sp.wait_ge(spare_out, 32)

        @block.gpsimd
        def _(pool):
            pool.sem_inc(xb_ready, 1)
            pool.sem_inc(lists_out, 1)
            nc.gpsimd.memset(idf[:, :], 0.0).then_inc(c_done, 1)
            nc.gpsimd.memset(below[:, :], 0.0).then_inc(c_done, 1)
            nc.gpsimd.memset(ones[:, :], 1.0).then_inc(c_done, 1)
            nc.gpsimd.memset(zero[:, :], 0.0).then_inc(c_done, 1)
            nc.gpsimd.memset(empty[:, :, :, :], 0).then_inc(c_done, 1)
            nc.gpsimd.memset(before[:, 0, :], 0.0).then_inc(c_done, 1)
            for c in cums[:3] + tcum[:3]:
                nc.gpsimd.memset(c[:, :, 0:E], 0.0).then_inc(c_done, 1)
            nc.gpsimd.memset(tied[:, :], 0.0).then_inc(c_done, 1)
            nc.gpsimd.iota(tokf[:, :, :], pattern=[[P, NT], [0, RANKS]], base=0, channel_multiplier=1,
                           allow_small_or_imprecise_dtypes=True).then_inc(c_done, 1)
            pool.wait_ge(c_done, 14)
            nc.gpsimd.affine_select(out=idf[:, :], in_=idf[:, :], compare_op=ALU.not_equal, fill=1.0, base=0,
                                    pattern=[[-1, P]], channel_multiplier=1).then_inc(c_done, 1)
            nc.gpsimd.affine_select(out=below[:, :], in_=below[:, :], compare_op=ALU.is_ge, fill=1.0, base=0,
                                    pattern=[[-1, P]], channel_multiplier=1).then_inc(c_done, 1)
            nc.gpsimd.iota(empty[:, :, :, 0], pattern=[[0, 2], [1, P]], base=T, channel_multiplier=0
                           ).then_inc(c_done, 1)
            nc.gpsimd.iota(ebase[:, :, :], pattern=[[0, NT], [T, E]], base=-int(BIG), channel_multiplier=0,
                           allow_small_or_imprecise_dtypes=True).then_inc(c_done, 1)
            nc.gpsimd.iota(rank[:, :, :], pattern=[[1, RANKS], [0, E]], base=1, channel_multiplier=0,
                           allow_small_or_imprecise_dtypes=True).then_inc(c_done, 1)
            nc.gpsimd.iota(lim[:, :, :], pattern=[[0, E], [MT, ET]], base=0, channel_multiplier=0,
                           allow_small_or_imprecise_dtypes=True).then_inc(c_done, 1)
            pool.wait_ge(w_in, 48)
            pool.wait_ge(empty_out, 16)

            def scatter(t, r, done):
                nc.gpsimd.indirect_dma_start(out=slots, out_offset=bass.IndirectOffsetOnAxis(idx[:, t, r:r + 1], 0),
                                             in_=pay[:, t, r, :], in_offset=None, bounds_check=E * T - 1,
                                             oob_is_err=False).then_inc(done, 16)

            with pool.Fori(0, B) as b:
                pool.wait_ge(x_in, 16 * (b + 1)).then_inc(own, 1)
                for t in range(NT):
                    ins = nc.gpsimd.tensor_tensor(xb[:, t, :], xt[:, t, :], bo_s[:, :], ALU.add)
                ins.then_inc(xb_ready, 1)
                pool.wait_ge(idx_ready, b + 1).then_inc(own, 1)
                for t in range(NT):
                    for r in range(TOPK):
                        scatter(t, r, scat)
                some = pool.value_load(tied_i[0:1, 0:1], min_val=0, max_val=1)
                earlier = pool.value_load(tied_i[0:1, 1:2], min_val=0, max_val=B)
                with pool.If(some > 0):
                    for t in range(NT):
                        for r in range(TOPK, RANKS):
                            scatter(t, r, scat_ties)
                    pool.wait_ge(scat_ties, (earlier + 1) * (16 * NT * (RANKS - TOPK))).then_inc(own, 1)
                pool.wait_ge(scat, (b + 1) * (16 * NT * TOPK)).then_inc(own, 1)
                pool.sem_inc(lists_out, 1)

        @block.scalar
        def _(act):
            with act.Fori(0, B) as b:
                for k in range(2):
                    act.wait_ge(b_ready, 2 * b + k + 1)
                    nc.scalar.copy(oT[:, 2 * k:2 * k + 2, :].rearrange("p t n -> p (t n)"), pt[:, k, :]
                                   ).then_inc(oT_ready, 1)
                for k in range(2):
                    act.wait_ge(d_ready, 2 * b + k + 1)
                    nc.scalar.copy(x1T[:, 2 * k:2 * k + 2, :].rearrange("p t n -> p (t n)"), pt[:, k, :]
                                   ).then_inc(x1T_ready, 1)
                act.wait_ge(diff_ready, b + 1)
                nc.scalar.activation(expo[:, :, :], expo[:, :, :], ACT.Exp).then_inc(expo_ready, 1)

        @block.tensor
        def _(pe):
            pe.sem_inc(a_ready, 1)
            pe.wait_ge(c_done, CONSTS)
            pe.wait_ge(w_in, 48)
            with pe.Fori(0, B) as b:
                pe.wait_ge(o_in, 16 * (b + 1))
                for t in range(NT):
                    for q in range(4):
                        ins = nc.tensor.transpose(pa[:, t, q * P:(q + 1) * P], ov[:, q, t * P:(t + 1) * P], idf[:, :])
                ins.then_inc(a_ready, 1)
                pe.wait_ge(oh_ready, b + 1)
                for t in range(NT):
                    for c in range(DC):
                        ins = nc.tensor.transpose(pt[:, t // 2, (t % 2 * DC + c) * P:(t % 2 * DC + c + 1) * P],
                                                  oh[:, t, c * P:(c + 1) * P], idf[:, :])
                    if t % 2:
                        ins.then_inc(b_ready, 1)
                for t in range(NT):
                    if t % 2 == 0:
                        pe.wait_ge(oT_ready, 2 * b + t // 2 + 1)
                    for c in range(DC):
                        ins = nc.tensor.matmul(pc[:, t // 2, t % 2 * D:(t % 2 + 1) * D], oT[:, t, c * P:(c + 1) * P],
                                               wo_s[:, c, :], start=(t % 2 == 0 and c == 0), stop=(c == DC - 1),
                                               skip_group_check=True)
                    if t % 2:
                        ins.then_inc(c_ready, 1)
                pe.wait_ge(x1_ready, b + 1)
                for t in range(NT):
                    for c in range(DC):
                        ins = nc.tensor.transpose(pt[:, t // 2, (t % 2 * DC + c) * P:(t % 2 * DC + c + 1) * P],
                                                  x1[:, t, c * P:(c + 1) * P], idf[:, :])
                    if t % 2:
                        ins.then_inc(d_ready, 1)
                for t in range(NT):
                    if t % 2 == 0:
                        pe.wait_ge(x1T_ready, 2 * b + t // 2 + 1)
                    for c in range(DC):
                        ins = nc.tensor.matmul(pc[:, 0, t * E:(t + 1) * E], x1T[:, t, c * P:(c + 1) * P],
                                               wg_s[:, c, :], start=(t == 0 and c == 0), stop=(c == DC - 1),
                                               skip_group_check=True)
                ins.then_inc(g_ready, 1)
                pe.wait_ge(picked_ready, b + 1)
                nc.tensor.matmul(pc[:, 1, 0:NT * E], below[:, :], picked_b[:, :, :].rearrange("p t e -> p (t e)"),
                                 start=True, stop=False, skip_group_check=True)
                nc.tensor.matmul(pc[:, 1, 0:NT * E], ones[:, :], before[:, 0:NT, :].rearrange("p t e -> p (t e)"),
                                 start=False, stop=True, skip_group_check=True)
                nc.tensor.matmul(pc[:, 1, NT * E:2 * NT * E], ones[:, :],
                                 picked_b[:, :, :].rearrange("p t e -> p (t e)"),
                                 start=False, stop=True, skip_group_check=True).then_inc(pos_ready, 1)
            pe.wait_ge(idx_ready, B)
            nc.tensor.matmul(pc[:, 0, 0:E], ones[:, :], before[:, 0, :], start=True, stop=True).then_inc(pos_ready, 1)

        @block.vector
        def _(dve):
            dve.wait_ge(c_done, CONSTS)
            at = [0]

            def wide(ap, shape):
                return ap.to_broadcast(shape)

            STEPS = 58

            with dve.Fori(0, B) as b:
                at[0] = 0

                def link(ins):
                    ins.then_inc(d, 1)
                    at[0] += 1
                    dve.wait_ge(d, b * STEPS + at[0])

                dve.wait_ge(a_ready, b + 2)
                heads = pa[:, :, :].rearrange("p t (h e) -> p t h e", h=H)
                link(nc.vector.reciprocal(rec[:, :, :], heads[:, :, :, DH]))
                nc.vector.tensor_tensor(oh[:, :, :].rearrange("p t (h e) -> p t h e", h=H), heads[:, :, :, 0:DH],
                                        wide(rec[:, :, :].rearrange("p t (h a) -> p t h a", a=1), [P, NT, H, DH]),
                                        ALU.mult).then_inc(oh_ready, 1)
                dve.wait_ge(xb_ready, b + 2)
                dve.wait_ge(x1_out, 32 * (b + 1))
                for k in range(2):
                    dve.wait_ge(c_ready, 2 * b + k + 1)
                    link(nc.vector.tensor_tensor(res[:, 2 * k:2 * k + 2, :].rearrange("p t n -> p (t n)"), pc[:, k, :],
                                                 xb[:, 2 * k:2 * k + 2, :].rearrange("p t n -> p (t n)"), ALU.add))
                for t in range(NT):
                    ins = nc.vector.bn_stats(st6[:, t, :], res[:, t, :])
                    if t < NT - 1:
                        ins.then_inc(d, 1)
                        at[0] += 1
                ins.then_inc(d, 1)
                at[0] += 1
                dve.wait_ge(d, b * STEPS + at[0]).then_inc(own, 1)
                for t in range(NT):
                    ins = nc.vector.bn_aggr(mv[:, t, :], st6[:, t, :])
                    if t < NT - 1:
                        ins.then_inc(d, 1)
                        at[0] += 1
                link(ins)
                rsqrt(nc, dve, mv[:, :, 1], rs[:, :], [rt[:, k, :] for k in range(3)], d, b * STEPS + at[0])
                at[0] += RSQRT_STEPS
                dve.wait_ge(d, b * STEPS + at[0])
                for t in range(NT):
                    ins = nc.vector.tensor_scalar(x1[:, t, :], res[:, t, :], mv[:, t, 0:1], rs[:, t:t + 1],
                                                  ALU.subtract, ALU.mult)
                    if t < NT - 1:
                        ins.then_inc(d, 1)
                        at[0] += 1
                ins.then_inc(x1_ready, 1)
                dve.wait_ge(g_ready, b + 1)
                nc.vector.tensor_copy(gate[:, :, :], pc[:, 0, 0:NT * E].rearrange("p (t e) -> p t e", e=E)).then_inc(d, 1)
                at[0] += 1
                dve.wait_ge(d, b * STEPS + at[0]).then_inc(own, 1)
                for t in range(NT):
                    ins = nc.vector.max(top[:, t, :], gate[:, t, :])
                    if t < NT - 1:
                        ins.then_inc(d, 1)
                        at[0] += 1
                link(ins)
                full = [P, NT, E]
                nc.vector.tensor_tensor(expo[:, :, :], gate[:, :, :], wide(top[:, :, 0:1], full), ALU.subtract
                                        ).then_inc(diff_ready, 1)
                link(nc.vector.tensor_tensor(picked[:, :, :], gate[:, :, :], wide(top[:, :, TOPK - 1:TOPK], full),
                                             ALU.is_ge))
                link(nc.vector.tensor_copy(cums[0][:, :, E:2 * E], picked[:, :, :]))
                link(nc.vector.tensor_copy(picked_b[:, :, :], picked[:, :, :]))
                for t in range(NT):
                    ins = nc.vector.tensor_tensor(before[:, t + 1, :], before[:, t, :], picked_b[:, t, :], ALU.add)
                    if t < NT - 1:
                        link(ins)
                ins.then_inc(picked_ready, 1)
                for k in range(3):
                    s = 1 << k
                    link(nc.vector.tensor_tensor(cums[k + 1][:, :, E:2 * E], cums[k][:, :, E:2 * E],
                                                 cums[k][:, :, E - s:2 * E - s], ALU.add))
                dve.wait_ge(expo_ready, b + 1)
                link(nc.vector.tensor_tensor(expm[:, :, :], expo[:, :, :], picked[:, :, :], ALU.mult))
                link(nc.vector.tensor_reduce(tot[:, :], expm[:, :, :], AX.X, ALU.add))
                link(nc.vector.reciprocal(rtot[:, :], tot[:, :]))
                link(nc.vector.scalar_tensor_tensor(wt[:, :, :], expm[:, :, :], 1.0 / E,
                                                    wide(rtot[:, :].rearrange("p (t a) -> p t a", a=1), full),
                                                    ALU.mult, ALU.mult))
                four = [P, NT, RANKS, E]

                def over_ranks(ap):
                    return wide(ap.rearrange("p t (a e) -> p t a e", a=1), four)

                link(nc.vector.tensor_tensor(pick[:, :, :, :], over_ranks(cums[3][:, :, E:2 * E]),
                                             wide(rank[:, :, :].rearrange("p (a r) e -> p a r e", a=1), four),
                                             ALU.is_equal))
                link(nc.vector.tensor_tensor(pickm[:, :, :, :], pick[:, :, :, :], over_ranks(picked[:, :, :]), ALU.mult))
                link(nc.vector.tensor_tensor(tmp2[:, :, :, :], pickm[:, :, :, :], over_ranks(wt[:, :, :]), ALU.mult))
                dve.wait_ge(lists_out, b + 1)
                link(nc.vector.tensor_reduce(pay[:, :, :, 1].bitcast(F32), tmp2[:, :, :, :], AX.X, ALU.add))
                dve.wait_ge(pos_ready, b + 1)
                link(nc.vector.tensor_tensor(slot[:, :, :], pc[:, 1, 0:NT * E].rearrange("p (t e) -> p t e", e=E),
                                             ebase[:, :, :], ALU.add))
                link(nc.vector.tensor_copy(before[:, 0, :], before[:, NT, :]))
                link(nc.vector.tensor_tensor(tmp1[:, :, :, :], pickm[:, :, :, :], over_ranks(slot[:, :, :]), ALU.mult))
                link(nc.vector.tensor_reduce(idxf[:, :, :], tmp1[:, :, :, :], AX.X, ALU.add))
                link(nc.vector.tensor_scalar(idx[:, :, :], idxf[:, :, :], BIG, None, ALU.add))
                link(nc.vector.tensor_copy(pay[:, :, :, 0], tokf[:, :, :]))
                link(nc.vector.tensor_scalar(tokf[:, :, :], tokf[:, :, :], float(N), None, ALU.add))
                link(nc.vector.tensor_reduce(tied[0:1, 0:1], pc[0:1, 1, NT * E:2 * NT * E], AX.X, ALU.add))
                link(nc.vector.tensor_tensor(tied[0:1, 2:3], tied[0:1, 2:3], tied[0:1, 1:2], ALU.add))
                link(nc.vector.tensor_scalar(tied[0:1, 1:2], tied[0:1, 0:1], float(TOPK * N), None, ALU.is_gt))
                nc.vector.tensor_copy(tied_i[0:1, :], tied[0:1, 1:3]).then_inc(idx_ready, 1)
                assert at[0] == STEPS, at[0]

            at[0] = B * STEPS

            def then(ins):
                ins.then_inc(d, 1)
                at[0] += 1
                dve.wait_ge(d, at[0])

            dve.wait_ge(pos_ready, B + 1)
            then(nc.vector.tensor_copy(cnt[:, :], pc[0:1, 0, 0:E]))
            then(nc.vector.tensor_tensor(over[:, :, :], wide(cnt[:, :].rearrange("p (e c) -> p e c", c=1), [1, E, ET]),
                                         lim[:, :, :], ALU.is_gt))
            then(nc.vector.tensor_reduce(tiles[:, :], over[:, :, :], AX.X, ALU.add))
            then(nc.vector.tensor_copy(tcum[0][:, 0, E:2 * E], tiles[:, :]))
            for k in range(3):
                s = 1 << k
                then(nc.vector.tensor_tensor(tcum[k + 1][:, :, E:2 * E], tcum[k][:, :, E:2 * E],
                                             tcum[k][:, :, E - s:2 * E - s], ALU.add))
            then(nc.vector.tensor_copy(table[:, 0, :], tiles[:, :]))
            then(nc.vector.tensor_copy(table[:, 2, :], tcum[3][:, 0, E:2 * E]))
            nc.vector.tensor_tensor(table[:, 1, :], tcum[3][:, 0, E:2 * E], tiles[:, :], ALU.subtract
                                    ).then_inc(table_ready, 1)


def experts(nc, w, rows, acc, slots, table):
    ctx = ExitStack()
    with ctx:
        def sb(name, shape, dt=F32):
            return ctx.enter_context(nc.sbuf_tensor(name, shape, dt))

        def pb(name, shape, dt=F32):
            return ctx.enter_context(nc.psum_tensor(name, shape, dt))

        def sem(name):
            return ctx.enter_context(nc.semaphore(name))

        def two(name):
            return [sem(f"{name}{i}") for i in range(2)]

        w1_s = [sb(f"w1_s{i}", [P, DC, FF]) for i in range(2)]
        w2_s = [sb(f"w2_s{i}", [P, FC, D]) for i in range(2)]
        w1_hi = [sb(f"w1_hi{i}", [P, DC, FF], F32R) for i in range(2)]
        w1_lo = [sb(f"w1_lo{i}", [P, DC, FF], F32R) for i in range(2)]
        w2_hi = [sb(f"w2_hi{i}", [P, FC, D], F32R) for i in range(2)]
        w2_lo = [sb(f"w2_lo{i}", [P, FC, D], F32R) for i in range(2)]
        b1_s = [sb(f"b1_s{i}", [P, FC]) for i in range(2)]
        b2_s = [sb(f"b2_s{i}", [P, D]) for i in range(2)]
        lst = sb("lst", [P, 2, P, 2], I32)
        ids = sb("ids", [P, 2, P])
        tok_s = sb("tok_s", [P, 2 * P], I32)
        wts_s = sb("wts_s", [P, 2 * P])
        idf = sb("idf3", [P, P])
        spare = sb("spare", [P, MH], I32)
        idx = [sb(f"idx3{i}", [P, MH], I32) for i in range(3)]
        xg = sb("xg", [P, MH, D])
        xT_hi = sb("xT_hi", [P, DC, MT], F32R)
        xT_lo = sb("xT_lo", [P, DC, MT], F32R)
        hT = sb("hT", [P, FC, MT])
        hT_hi = sb("hT_hi", [P, FC, MT], F32R)
        hT_lo = sb("hT_lo", [P, FC, MT], F32R)
        yb = sb("yb", [P, MH, D])
        ys = sb("ys", [P, MH, D])

        px = pb("px", [P, DC, MT])
        ph = [pb(f"ph{i}", [P, 2, MT]) for i in range(FC // 2)]
        py = [pb(f"py{i}", [P, BANK]) for i in range(MH)]

        w_in, b_in = two("w_in3"), two("b_in")
        lst_in, ids_f, lists_t, lists_ready, c_done = (sem("lst_in"), sem("ids_f"), sem("lists_t"),
                                                       sem("lists_ready"), sem("c_done3"))
        pe_done, act_done, dve_done = sem("pe_done"), sem("act_done"), sem("dve_done")
        w_hi_ready, w1_ready, w2_ready = sem("w_hi_ready"), sem("w1_ready"), sem("w2_ready")
        idx_step, xg_in, own = sem("idx_step"), sem("xg_in"), sem("own3")
        px_ready, xT_hi_ready, xT_ready = sem("px_ready"), sem("xT_hi_ready"), sem("xT_ready")
        ph_ready, h_ready, h_hi_ready, h_lo_ready = sem("ph_ready"), sem("h_ready"), sem("h_hi_ready"), sem("h_lo_ready")
        y_ready, y_free, yb_ready, ys_ready = sem("y_ready"), sem("y_free"), sem("yb_ready"), sem("ys_ready")
        ys_free, added = sem("ys_free"), sem("added")
        block = ctx.enter_context(nc.Block())

        GROUP = 4

        def walk(eng, body, start=None, end=None):
            with eng.Fori(0, E // 2) as pair:
                for q in range(2):
                    e = 2 * pair + q
                    tiles = eng.value_load(table[0:1, 0, bass.ds(e, 1)], min_val=0, max_val=ET)
                    before = eng.value_load(table[0:1, 1, bass.ds(e, 1)], min_val=0, max_val=E * ET)
                    if start:
                        start(pair, e, q)
                    with eng.Fori(0, ET // GROUP) as group:
                        with eng.If(group * GROUP < tiles):
                            with eng.Fori(0, GROUP) as i:
                                with eng.If(group * GROUP + i < tiles):
                                    body(e, q, group * GROUP + i, before + group * GROUP + i)
                    if end:
                        end(pair, e, q)

        def ahead(eng, split, pair, e, q):
            eng.wait_ge(pe_done, e + 1).then_inc(own, 1)
            if q == 0:
                split(e + 1, 1, pair + 1)
            else:
                with eng.If(pair < E // 2 - 1):
                    split(e + 1, 0, pair + 2)

        @block.sync
        def _(sp):
            sp.dma_start(lst[:, :, :, :].rearrange("p a s c -> p a (s c)"),
                         slots.rearrange("(a p s) c -> p a (s c)", a=2, p=P)).then_inc(lst_in, 16)

            def load_weights(e, q):
                for dst, src in ((w1_s[q], w["w1"][bass.ds(e, 1), :, :].rearrange("a (k p) f -> p (a k) f", p=P)),
                                 (w2_s[q], w["w2"][bass.ds(e, 1), :, :].rearrange("a (k p) d -> p (a k) d", p=P))):
                    sp.dma_start(dst[:, :, :], src).then_inc(w_in[q], 16)

            def load_biases(e, q):
                for dst, src in ((b1_s[q], w["b1"][bass.ds(e, 1), :, :].rearrange("a p c -> (a p) c")),
                                 (b2_s[q], w["b2"][bass.ds(e, 1), :].to_broadcast([P, D]))):
                    sp.dma_start(dst[:, :], src).then_inc(b_in[q], 16)

            for e in range(2):
                load_weights(e, e)
                load_biases(e, e)
            with sp.Fori(0, E // 2 - 1) as pair:
                for q in range(2):
                    e = 2 * pair + q
                    sp.wait_ge(w2_ready, e + 1)
                    load_weights(e + 2, q)
                    sp.wait_ge(act_done, e + 1)
                    sp.wait_ge(dve_done, e + 1)
                    load_biases(e + 2, q)

        @block.gpsimd
        def _(pool):
            nc.gpsimd.memset(idf[:, :], 0.0).then_inc(c_done, 1)
            nc.gpsimd.iota(spare[:, :], pattern=[[0, MH]], base=T, channel_multiplier=1).then_inc(c_done, 1)
            pool.wait_ge(c_done, 2)
            nc.gpsimd.affine_select(out=idf[:, :], in_=idf[:, :], compare_op=ALU.not_equal, fill=1.0, base=0,
                                    pattern=[[-1, P]], channel_multiplier=1).then_inc(c_done, 1)
            for i in range(2):
                nc.gpsimd.tensor_copy(idx[i][:, :], spare[:, :]).then_inc(idx_step, 1)
            pool.sem_inc(px_ready, 1)
            pool.wait_ge(lists_ready, 4)

            def shift(k, source):
                pool.wait_ge(idx_step, 3 * k + 2).then_inc(own, 1)
                nc.gpsimd.tensor_copy(idx[2][:, :], idx[1][:, :]).then_inc(idx_step, 1)
                pool.wait_ge(idx_step, 3 * k + 3).then_inc(own, 1)
                nc.gpsimd.tensor_copy(idx[1][:, :], idx[0][:, :]).then_inc(idx_step, 1)
                pool.wait_ge(idx_step, 3 * k + 4).then_inc(own, 1)
                nc.gpsimd.tensor_copy(idx[0][:, :], source).then_inc(idx_step, 1)
                pool.wait_ge(idx_step, 3 * k + 5).then_inc(own, 1)

            def gather():
                for h in range(MH):
                    nc.gpsimd.indirect_dma_start(out=xg[:, h, :], out_offset=None, in_=rows,
                                                 in_offset=bass.IndirectOffsetOnAxis(idx[0][:, h:h + 1], 0),
                                                 bounds_check=T + SPARE - 1, oob_is_err=True).then_inc(xg_in, 16)

            def add(k):
                pool.wait_ge(ys_ready, k + 1).then_inc(own, 1)
                for h in range(MH):
                    nc.gpsimd.indirect_dma_start(out=acc, out_offset=bass.IndirectOffsetOnAxis(idx[2][:, h:h + 1], 0),
                                                 in_=ys[:, h, :], in_offset=None, bounds_check=T + SPARE - 1,
                                                 oob_is_err=True, compute_op=ALU.add).then_inc(added, 16)
                    pool.wait_ge(added, k * (16 * MH) + 16 * (h + 1)).then_inc(own, 1)
                pool.sem_inc(ys_free, 1)

            def body(e, q, t, k):
                pool.wait_ge(px_ready, k + 1).then_inc(own, 1)
                shift(k, tok_s[:, bass.ds(e * (MH * ET) + t * MH, MH)])
                gather()
                add(k)

            walk(pool, body)
            last = pool.value_load(table[0:1, 2, E - 1:E], min_val=0, max_val=E * ET)
            pool.wait_ge(px_ready, last + 1).then_inc(own, 1)
            shift(last, spare[:, :])
            gather()
            add(last)
            shift(last + 1, spare[:, :])
            add(last + 1)

        @block.tensor
        def _(pe):
            pe.sem_inc(pe_done, 1)
            pe.wait_ge(c_done, 3)
            for c in range(2):
                pe.wait_ge(ids_f, c + 1)
                nc.tensor.transpose(ph[c][:, 0, 0:P], ids[:, c, :], idf[:, :]).then_inc(lists_t, 1)
            for c in range(2):
                nc.tensor.transpose(ph[2 + c][:, 0, 0:P], lst[:, c, :, 1].bitcast(F32), idf[:, :]).then_inc(lists_t, 1)
            pe.wait_ge(lists_ready, 4)

            def transpose_rows(k):
                pe.wait_ge(xg_in, (k + 1) * (16 * MH))
                for h in range(MH):
                    for c in range(DC):
                        ins = nc.tensor.transpose(px[:, c, h * P:(h + 1) * P], xg[:, h, c * P:(c + 1) * P], idf[:, :])
                ins.then_inc(px_ready, 1)

            def start(pair, e, q):
                pe.wait_ge(w1_ready, e + 1).then_inc(own, 1)

            def body(e, q, t, k):
                pe.wait_ge(xT_ready, k + 1)
                for i in range(FC // 2):
                    for f in (2 * i, 2 * i + 1):
                        cols = slice(f * P, (f + 1) * P)
                        for c in range(DC):
                            for n, (lhs, rhs) in enumerate(((w1_hi, xT_hi), (w1_hi, xT_lo), (w1_lo, xT_hi))):
                                ins = nc.tensor.matmul(ph[i][:, f % 2, :], lhs[q][:, c, cols], rhs[:, c, :],
                                                       start=(f % 2 == 0 and c == 0 and n == 0),
                                                       stop=(c == DC - 1 and n == 2), skip_group_check=True)
                    ins.then_inc(ph_ready, 1)
                transpose_rows(k + 1)
                pe.wait_ge(w2_ready, e + 1)
                pe.wait_ge(y_free, k + 1)
                for i in range(FC // 2):
                    pe.wait_ge(h_lo_ready, FC // 2 * k + i + 1)
                    for f in (2 * i, 2 * i + 1):
                        for h in range(MH):
                            cols = slice(h * P, (h + 1) * P)
                            for n, (lhs, rhs) in enumerate(((hT_hi, w2_hi), (hT_hi, w2_lo), (hT_lo, w2_hi))):
                                ins = nc.tensor.matmul(py[h][:, 0:D], lhs[:, f, cols], rhs[q][:, f, :],
                                                       start=(f == 0 and n == 0), stop=(f == FC - 1 and n == 2))
                            if f == FC - 1:
                                ins.then_inc(y_ready, 1)

            def end(pair, e, q):
                pe.drain().then_inc(pe_done, 1)

            transpose_rows(0)
            walk(pe, body, start, end)

        @block.scalar
        def _(act):
            act.wait_ge(lists_ready, 4)

            def x_hi(k):
                act.wait_ge(px_ready, k + 2)
                nc.scalar.copy(xT_hi[:, :, :], px[:, :, :]).then_inc(xT_hi_ready, 1)

            def split_high(x, q, loads):
                act.wait_ge(w_in[q], 32 * loads).then_inc(own, 1)
                for c in range(DC):
                    nc.scalar.copy(w1_hi[q][:, c, :], w1_s[q][:, c, :]).then_inc(w_hi_ready, 1)
                for c in range(2):
                    half = slice(FC // 2 * c, FC // 2 * (c + 1))
                    nc.scalar.copy(w2_hi[q][:, half, :], w2_s[q][:, half, :]).then_inc(w_hi_ready, 1)

            def start(pair, e, q):
                act.wait_ge(b_in[q], 32 * (pair + 1)).then_inc(own, 1)
                ahead(act, split_high, pair, e, q)

            def body(e, q, t, k):
                def h_hi(i):
                    act.wait_ge(h_ready, FC * k + 2 * i + 2)
                    nc.scalar.copy(hT_hi[:, 2 * i:2 * i + 2, :], hT[:, 2 * i:2 * i + 2, :]).then_inc(h_hi_ready, 1)

                for i in range(FC // 2):
                    act.wait_ge(ph_ready, FC // 2 * k + i + 1)
                    for f in (2 * i, 2 * i + 1):
                        nc.scalar.activation(hT[:, f, :], ph[i][:, f % 2, :], ACT.Relu, bias=b1_s[q][:, f:f + 1],
                                             scale=1.0).then_inc(h_ready, 1)
                    if i:
                        h_hi(i - 1)
                h_hi(FC // 2 - 1)
                x_hi(k + 1)

            def end(pair, e, q):
                act.drain().then_inc(act_done, 1)

            x_hi(0)
            split_high(0, 0, 1)
            walk(act, body, start, end)

        @block.vector
        def _(dve):
            dve.sem_inc(y_free, 1)
            nc.vector.memset(ys[:, :, :], 0.0).then_inc(ys_ready, 2)
            dve.wait_ge(lst_in, 16)
            for c in range(2):
                nc.vector.tensor_copy(ids[:, c, :], lst[:, c, :, 0]).then_inc(ids_f, 1)
            dve.wait_ge(lists_t, 4)
            for c in range(2):
                nc.vector.tensor_copy(tok_s[:, c * P:(c + 1) * P], ph[c][:, 0, 0:P]).then_inc(lists_ready, 1)
                nc.vector.tensor_copy(wts_s[:, c * P:(c + 1) * P], ph[2 + c][:, 0, 0:P]).then_inc(lists_ready, 1)
            dve.wait_ge(lists_ready, 4)

            def x_lo(k):
                dve.wait_ge(xT_hi_ready, k + 1)
                nc.vector.tensor_tensor(xT_lo[:, :, :], px[:, :, :], xT_hi[:, :, :].bitcast(F32), ALU.subtract
                                        ).then_inc(xT_ready, 1)

            def split_low(x, q, loads):
                for c in range(DC):
                    dve.wait_ge(w_hi_ready, 4 * x + c + 1)
                    ins = nc.vector.tensor_tensor(w1_lo[q][:, c, :], w1_s[q][:, c, :],
                                                  w1_hi[q][:, c, :].bitcast(F32), ALU.subtract)
                ins.then_inc(w1_ready, 1)
                for c in range(2):
                    half = slice(FC // 2 * c, FC // 2 * (c + 1))
                    dve.wait_ge(w_hi_ready, 4 * x + c + 3)
                    ins = nc.vector.tensor_tensor(w2_lo[q][:, half, :], w2_s[q][:, half, :],
                                                  w2_hi[q][:, half, :].bitcast(F32), ALU.subtract)
                ins.then_inc(w2_ready, 1)

            def start(pair, e, q):
                dve.wait_ge(b_in[q], 32 * (pair + 1)).then_inc(own, 1)
                ahead(dve, split_low, pair, e, q)

            def body(e, q, t, k):
                for i in range(FC // 2):
                    dve.wait_ge(h_hi_ready, FC // 2 * k + i + 1)
                    pair_of = slice(2 * i, 2 * i + 2)
                    nc.vector.tensor_tensor(hT_lo[:, pair_of, :], hT[:, pair_of, :], hT_hi[:, pair_of, :].bitcast(F32),
                                            ALU.subtract).then_inc(h_lo_ready, 1)
                x_lo(k + 1)
                for h in range(MH):
                    dve.wait_ge(y_ready, MH * k + h + 1)
                    nc.vector.tensor_tensor(yb[:, h, :], py[h][:, 0:D], b2_s[q][:, :], ALU.add
                                            ).then_inc(y_free if h == MH - 1 else yb_ready, 1)
                dve.wait_ge(y_free, k + 2)
                dve.wait_ge(ys_free, k + 2)
                for h in range(MH):
                    ins = nc.vector.tensor_scalar(ys[:, h, :], yb[:, h, :],
                                                  wts_s[:, bass.ds(e * (MH * ET) + t * MH + h, 1)], None, ALU.mult)
                ins.then_inc(ys_ready, 1)

            def end(pair, e, q):
                dve.drain().then_inc(dve_done, 1)

            x_lo(0)
            split_low(0, 0, 1)
            walk(dve, body, start, end)


def last_layernorm(nc, acc, out):
    ctx = ExitStack()
    with ctx:
        def sb(name, shape, dt=F32):
            return ctx.enter_context(nc.sbuf_tensor(name, shape, dt))

        def sem(name):
            return ctx.enter_context(nc.semaphore(name))

        a = [sb(f"a4{i}", [P, NT, D]) for i in range(2)]
        y = [sb(f"y4{i}", [P, NT, D]) for i in range(2)]
        st6 = sb("st64", [P, NT, 6])
        mv = sb("mv4", [P, NT, 2])
        rs = sb("rs4", [P, NT])
        rt = sb("rt4", [P, 3, NT])
        a_in = [sem(f"a_in{i}") for i in range(2)]
        y_out = [sem(f"y_out{i}") for i in range(2)]
        y_ready, d, own = sem("y_ready4"), sem("dve_step4"), sem("own4")
        block = ctx.enter_context(nc.Block())

        @block.sync
        def _(sp):
            sp.sem_inc(y_ready, 2)
            with sp.Fori(0, B // 2) as pair:
                for q in range(2):
                    sp.wait_ge(y_ready, 2 * pair + q + 1)
                    sp.dma_start(a[q][:, :, :], acc[bass.ds(N * (2 * pair + q), N), :].rearrange(
                        "(t p) d -> p t d", p=P)).then_inc(a_in[q], 16)

        @block.scalar
        def _(act):
            for q in range(2):
                act.sem_inc(y_out[q], 16)
            with act.Fori(0, B // 2) as pair:
                for q in range(2):
                    act.wait_ge(y_ready, 2 * pair + q + 3)
                    act.dma_start(out[bass.ds(2 * pair + q, 1), :, :].rearrange("a (t p) d -> p (a t) d", p=P),
                                  y[q][:, :, :]).then_inc(y_out[q], 16)
            for q in range(2):
                act.wait_ge(y_out[q], 16 + 16 * B // 2)

        @block.vector
        def _(dve):
            STEPS = 2 * NT + RSQRT_STEPS + NT - 1
            with dve.Fori(0, B // 2) as pair:
                for q in range(2):
                    base = (2 * pair + q) * STEPS
                    dve.wait_ge(a_in[q], 16 * (pair + 1))
                    for t in range(NT):
                        nc.vector.bn_stats(st6[:, t, :], a[q][:, t, :]).then_inc(d, 1)
                    dve.wait_ge(d, base + NT).then_inc(own, 1)
                    for t in range(NT):
                        nc.vector.bn_aggr(mv[:, t, :], st6[:, t, :]).then_inc(d, 1)
                    dve.wait_ge(d, base + 2 * NT)
                    rsqrt(nc, dve, mv[:, :, 1], rs[:, :], [rt[:, k, :] for k in range(3)], d, base + 2 * NT)
                    dve.wait_ge(d, base + 2 * NT + RSQRT_STEPS)
                    dve.wait_ge(y_out[q], 16 * (pair + 1))
                    for t in range(NT):
                        nc.vector.tensor_scalar(y[q][:, t, :], a[q][:, t, :], mv[:, t, 0:1], rs[:, t:t + 1],
                                                ALU.subtract, ALU.mult).then_inc(y_ready if t == NT - 1 else d, 1)


def build(nc, w, out):
    scratch_qk = nc.dram_tensor("scratch_qk", (2, 2, 2, P, N), F32).ap()
    scratch_o = nc.dram_tensor("scratch_o", (4 * B, P, N), F32).ap()
    rows = nc.dram_tensor("rows", (T + SPARE, D), F32).ap()
    acc = nc.dram_tensor("acc", (T + SPARE, D), F32).ap()
    slots = nc.dram_tensor("slots", (E * T, 2), I32).ap()
    attention(nc, w["x"], w["mt"], w, w["rel"], scratch_qk, scratch_o)
    with nc.sbuf_tensor("table", [1, 3, E], I32) as table:
        after_attention(nc, w, scratch_o, rows, acc, slots, table)
        experts(nc, w, rows, acc, slots, table)
        last_layernorm(nc, acc, out)


def interpolation():
    import numpy as np
    pos = np.arange(N, dtype=np.float32) * np.float32((S - 1) / (N - 1))
    low = np.floor(pos).astype(np.int32)
    frac = pos - low.astype(np.float32)
    m = np.zeros((N, S), np.float32)
    np.add.at(m, (np.arange(N), low), np.float32(1) - frac)
    np.add.at(m, (np.arange(N), np.minimum(low + 1, S - 1)), frac)
    m[-1] = 0
    return np.ascontiguousarray(m.T)


def kernel(**inputs):
    import numpy as np
    import concourse.bacc as bacc
    from concourse.bass_utils import run_bass_kernel_spmd

    a = {k: np.asarray(v) for k, v in inputs.items()}

    def by_lane(wt):
        return wt.reshape(2, HH, DH, D).transpose(3, 0, 2, 1).reshape(D, D)

    arrays = {
        "x": a["L0_attn_x"], "mt": interpolation(), "rel": a["L0_attn_rel_bias"],
        "wq": by_lane(a["L0_attn_Wq"]), "wk": by_lane(a["L0_attn_Wk"]),
        "wv": a["L0_attn_Wv"].T, "wo": a["L0_attn_Wo"].T,
        "bq": a["L0_attn_bq"].reshape(2, HH, DH).transpose(2, 1, 0).reshape(P, 2),
        "bk": a["L0_attn_bk"].reshape(2, HH, DH).transpose(2, 1, 0).reshape(P, 2),
        "bv": a["L0_attn_bv"], "bo": a["L0_attn_bo"],
        "gamma": a["L0_attn_gamma"].reshape(DC, P).T, "beta": a["L0_attn_beta"].reshape(DC, P).T,
        "wg": a["L0_ffn_W_gate"], "w1": a["L0_ffn_W1"],
        "b1": a["L0_ffn_b1"].reshape(E, FC, P).transpose(0, 2, 1),
        "w2": a["L0_ffn_W2"], "b2": a["L0_ffn_b2"],
    }
    arrays = {k: np.ascontiguousarray(v) for k, v in arrays.items()}
    nc = bacc.Bacc("TRN2", target_bir_lowering=False, num_devices=1)
    w = {k: nc.dram_tensor("in_" + k, v.shape, mybir.dt.from_np(v.dtype), kind="ExternalInput").ap()
         for k, v in arrays.items()}
    out = nc.dram_tensor("out", (B, N, D), F32, kind="ExternalOutput").ap()
    build(nc, w, out)
    r = run_bass_kernel_spmd(nc, [{"in_" + k: v for k, v in arrays.items()}], core_ids=[0])
    return r.results[0]["out"]
```

```python
from contextlib import ExitStack

import concourse.bass as bass
from concourse import mybir
from concourse.alu_op_type import AluOpType as ALU

ACT = mybir.ActivationFunctionType
AX = mybir.AxisListType
F32 = mybir.dt.float32
F32R = mybir.dt.float32r
BF16 = mybir.dt.bfloat16
I32 = mybir.dt.int32

P = 128
B, N, D = 8, 512, 256
T = B * N
H, DH = 16, 16
S = 32
HH = H // 2
NT = N // P
DC = D // P
VW = 32
BANK = 512
PAIRS = HH // 2
JOBS = 5
UJOBS = PAIRS * JOBS
ST_BANKS, MX_BANKS = 4, 2
SCALE = DH ** -0.5
GRID_SCALE = (N - 1) ** -2
QK_AT_ROW = 2 * S
MAX_ROW = QK_AT_ROW + 3 * DH
EPS = 1e-5
MASKED = -1e30
E, TOPK, FF = 8, 2, 4 * D
FC = FF // P
MT = 256
MH = MT // P
ET = T // MT
SPARE = P
PROLOGUE_GEN = 9
STEP_GEN = (6, 4)
GEN = sum(STEP_GEN)
X_AT = (1, 2)
PARTS_AT = (2, 3)
QK_AT = (5, 8)
PV_AT = 13
STATS_AT = (4, 6, 9, 11)
DEVIATION_AT = 13


def score_jobs(first_wide):
    wide = (lambda t: N - t * P) if first_wide else (lambda t: (t + 1) * P)
    order = (0, 1, 3, 2) if first_wide else (3, 2, 0, 1)
    full, long, short, half = order
    jobs = []
    for a in range(2):
        jobs.append([(a, full, wide(full), 0)])
        jobs.append([(a, long, wide(long), 0), (a, short, wide(short), wide(long))])
    jobs.append([(0, half, wide(half), 0), (1, half, wide(half), wide(half))])
    return jobs


KEY_JOBS = score_jobs(True)
QUERY_JOBS = score_jobs(False)


NEWTON = 3
RSQRT_STEPS = 3 + 3 * NEWTON


def guess(nc, dve, var, y, tmp, done, base):
    nc.vector.tensor_scalar(tmp[0], var, EPS, None, ALU.add).then_inc(done, 1)
    dve.wait_ge(done, base + 1)
    nc.vector.tensor_scalar(tmp[1].bitcast(I32), tmp[0].bitcast(I32), 1, None, ALU.arith_shift_right).then_inc(done, 1)
    dve.wait_ge(done, base + 2)
    nc.vector.tensor_scalar(y.bitcast(I32), tmp[1].bitcast(I32), -1.0, float(0x5F3759DF), ALU.mult, ALU.add
                            ).then_inc(done, 1)


def rsqrt(nc, dve, var, y, tmp, done, base):
    guess(nc, dve, var, y, tmp, done, base)
    for k in range(NEWTON):
        dve.wait_ge(done, base + 3 + 3 * k)
        nc.vector.scalar_tensor_tensor(tmp[1], y, -0.5, y, ALU.mult, ALU.mult).then_inc(done, 1)
        dve.wait_ge(done, base + 4 + 3 * k)
        nc.vector.tensor_tensor(tmp[2], tmp[1], tmp[0], ALU.mult).then_inc(done, 1)
        dve.wait_ge(done, base + 5 + 3 * k)
        nc.vector.scalar_tensor_tensor(y, tmp[2], 1.5, y, ALU.add, ALU.mult).then_inc(done, 1)


def attention(nc, x, mt, w, rel, scratch_qk, scratch_o, sorting, rows, acc, slots):
    ctx = ExitStack()
    with ctx:
        def sb(name, shape, dt=F32):
            return ctx.enter_context(nc.sbuf_tensor(name, shape, dt))

        def pb(name, shape, dt=F32):
            return ctx.enter_context(nc.psum_tensor(name, shape, dt))

        def sem(name):
            return ctx.enter_context(nc.semaphore(name))

        qs = sb("qs", [P, 2, HH, N], F32R)
        ks = sb("ks", [P, 2, HH, N], F32R)
        mt_r = sb("mt_r", [2 * S, 1, N], F32R)
        probs = sb("probs", [P, 2, 2 * JOBS, BANK])
        vaug = sb("vaug", [P, 2, NT, HH, VW])
        wq_s = sb("wq_s", [P, DC, D])
        wk_s = sb("wk_s", [P, DC, D])
        wv_s = sb("wv_s", [P, DC, D])
        bq_s = sb("bq_s", [P, 2])
        bq4 = sb("bq4", [P, 2])
        bk_s = sb("bk_s", [P, 2])
        bv_s = sb("bv_s", [P, D])
        gam = sb("gam", [P, DC])
        bet = sb("bet", [P, DC])
        xt = sb("xt", [P, NT, D])
        xh = sb("xh", [P, NT, D])
        xnt = sb("xnt", [P, DC, N])
        xnt_hi = sb("xnt_hi", [P, DC, N], F32R)
        xnt_lo = sb("xnt_lo", [P, DC, N], F32R)
        wqk_hi = sb("wqk_hi", [P, 2, DC, D], F32R)
        wqk_lo = sb("wqk_lo", [P, 2, DC, D], F32R)
        qf = sb("qf", [P, 2, N])
        qsp = sb("qsp", [P, 2, 2, N], F32R)
        mx = sb("mx", [P, HH, NT])
        negm = sb("negm", [HH * NT, P], F32R)
        ov = sb("ov", [P, 2, N])
        st6 = sb("st6", [P, NT, 6])
        mv = sb("mv", [P, NT, 2])
        rs = sb("rs", [P, NT])
        rt = sb("rt", [P, 3, NT])
        idf = sb("idf", [P, P])
        idb = sb("idb", [P, P], BF16)
        mask_q = sb("mask_q", [P, P], BF16)
        mask_k = sb("mask_k", [P, P], BF16)
        mtf = sb("mtf", [2 * S, N])
        relr = probs[0:S, 0, 0:4, :].rearrange("p a n -> p (a n)")[:, 0:H * 2 * S].rearrange(
            "p (h a j) -> p h a j", h=H, a=2)

        st = [pb(f"st{i}", [P, BANK]) for i in range(ST_BANKS)]
        sm = [pb(f"sm{i}", [P, BANK]) for i in range(MX_BANKS)]
        po = pb("po", [P, BANK])
        pg = pb("pg", [P, BANK])

        mt_in, x0_in, w_in, x_in = sem("mt_in"), sem("x0_in"), sem("w_in"), sem("x_in")
        mt_ready, ks_rel = sem("mt_ready"), sem("ks_rel")
        consts = sem("consts")
        r_ready, r_high, r_low, bq_ready = sem("r_ready"), sem("r_high"), sem("r_low"), sem("bq_ready")
        ln_step, xh_ready = sem("ln_step"), sem("xh_ready")
        wait_apart, sp_wait_apart, dve_wait_apart = sem("wait_apart"), sem("sp_wait_apart"), sem("dve_wait_apart")
        xnt_high, xnt_low, w_high, w_low = sem("xnt_high"), sem("xnt_low"), sem("w_high"), sem("w_low")
        gen_ready, gen_free = sem("gen_ready"), sem("gen_free")
        split_step, split_ready = sem("split_step"), sem("split_ready")
        scr_out = [sem(f"scr_out{i}") for i in range(2)]
        rows_in = [[sem(f"rows_in{i}{j}") for j in range(2)] for i in range(2)]
        st_ready, st_free = sem("st_ready"), sem("st_free")
        sm_ready, sm_free = sem("sm_ready"), sem("sm_free")
        max_in = sem("max_in")
        pv_ready, pv_free = sem("pv_ready"), sem("pv_free")
        o_out = [sem(f"o_out{i}") for i in range(2)]
        block = ctx.enter_context(nc.Block())

        CONSTS = 11
        WEIGHTS = 9
        LN_STEPS = 2 * NT + RSQRT_STEPS

        @block.sync
        def _(sp):
            sp.sem_inc(scr_out[1], 32)
            for dst, src, done in (
                (xh[:, :, :], x[0].rearrange("(t p) d -> p t d", p=P), x0_in),
                (mtf[0:S, :], mt, mt_in), (mtf[S:2 * S, :], mt, mt_in),
                (relr[:, :, 0, :], rel.rearrange("h i j -> i h j"), mt_in),
                (relr[:, :, 1, :], rel.rearrange("h i j -> i h j"), mt_in),
                (wq_s[:, :, :], w["wq"].rearrange("(k p) o -> p k o", p=P), w_in),
                (gam[:, :], w["gamma"], w_in), (bet[:, :], w["beta"], w_in),
                (bq_s[:, :], w["bq"], w_in), (bk_s[:, :], w["bk"], w_in),
                (wk_s[:, :, :], w["wk"].rearrange("(k p) o -> p k o", p=P), w_in),
                (wv_s[:, :, :], w["wv"].rearrange("(k p) o -> p k o", p=P), w_in),
                (bv_s[:, :], w["bv"].partition_broadcast(P), w_in),
                (xt[:, :, :], x[1].rearrange("(t p) d -> p t d", p=P), w_in),
            ):
                sp.dma_start(dst, src).then_inc(done, 16)
            sp.wait_ge(mt_ready, 1)
            sp.dma_start(ks[0:2 * S, :, :, :].bitcast(F32).rearrange("p a h n -> p (a h) n"),
                         mt_r[:, :, :].bitcast(F32).to_broadcast([2 * S, H, N])).then_inc(ks_rel, 16)

            def load_x(b):
                sp.dma_start(xt[:, :, :], x[bass.ds(b, 1), :, :].rearrange("a (t p) d -> p (a t) d", p=P)
                             ).then_inc(x_in, 16)

            def store_split(b, half):
                un = 2 * b + half
                for a in range(2):
                    sp.wait_ge(split_ready, 2 * un + a + 1)
                    sp.dma_start(scratch_qk[half, a].rearrange("t p n -> p t n"), qsp[:, a, :, :].bitcast(F32)
                                 ).then_inc(scr_out[half], 16)

            def load_rows(b, half, part):
                heads = slice(HH // 2 * part, HH // 2 * (part + 1))
                q_parts = scratch_qk[half, 0].rearrange("t (i h) n -> (t i) h n", h=HH)
                k_parts = scratch_qk[half, 1].rearrange("t (i h) n -> (t i) h n", h=HH)
                at = QK_AT_ROW
                for dst, src in ((qs[at:at + 2 * DH], q_parts), (qs[at + 2 * DH:at + 3 * DH], q_parts[0:DH]),
                                 (ks[at:at + DH], k_parts[0:DH]), (ks[at + DH:at + 3 * DH], k_parts)):
                    sp.dma_start(dst[:, half, heads, :].bitcast(F32), src[:, heads, :]).then_inc(rows_in[half][part], 16)

            def load_max(g, half):
                sp.wait_ge(gen_free, g + 1)
                sp.dma_start(qs[MAX_ROW:MAX_ROW + 1, half, :, :].bitcast(F32).rearrange("p h (t n) -> p (h t) n", n=P),
                             negm[:, :].bitcast(F32)).then_inc(max_in, 16)

            def store_o(b, half, q):
                un = 2 * b + half
                sp.wait_ge(pv_free, 1 + 2 * un + q + 1)
                sp.dma_start(scratch_o[bass.ds(4 * b + 2 * half + q, 1), :, :].rearrange("a p n -> (a p) n"),
                             ov[:, q, :]).then_inc(o_out[q], 16)

            def step(b, half, more, more_x):
                un = 2 * b + half
                g = PROLOGUE_GEN + GEN * b + half * STEP_GEN[0]
                if more_x and half == 0:
                    sp.wait_ge(xh_ready, NT * (b + 2))
                    load_x(b + 2)
                if more:
                    store_split(b + 1, half)
                    sp.wait_ge(scr_out[half], 32 * (b + 2 + half)).then_inc(sp_wait_apart, 1)
                    sp.wait_ge(st_ready, UJOBS * un + UJOBS // 2)
                    load_rows(b + 1, half, 0)
                store_o(b, half, 0)
                if more or half == 0:
                    load_max(g + (2 if half == 0 else 0) + 2 if more else g, 1 - half)
                if more:
                    sp.wait_ge(st_ready, UJOBS * (un + 1))
                    load_rows(b + 1, half, 1)
                store_o(b, half, 1)

            for half in range(2):
                store_split(0, half)
                sp.wait_ge(scr_out[half], 32 * (1 + half))
                for part in range(2):
                    load_rows(0, half, part)
            load_max(PROLOGUE_GEN - 1, 0)
            sorting.load(sp, rows, acc, slots)
            with sp.Fori(0, B - 2) as b:
                for half in range(2):
                    step(b, half, True, True)
            for half in range(2):
                step(B - 2, half, True, False)
            for q in range(2):
                sp.wait_ge(o_out[q], 16 + 16 * 2)
            sorting.load_heads(sp, scratch_o, 0)
            sorting.load_rows(sp, 0)
            for half in range(2):
                step(B - 1, half, False, False)
            for q in range(2):
                sp.wait_ge(o_out[q], 16 + 16 * 2 * B)

        @block.gpsimd
        def _(pool):
            nc.gpsimd.memset(idf[:, :], 0.0).then_inc(consts, 1)
            nc.gpsimd.memset(idb[:, :], 0.0).then_inc(consts, 1)
            nc.gpsimd.memset(mask_q[:, :], 0.0).then_inc(consts, 1)
            nc.gpsimd.memset(mask_k[:, :], 0.0).then_inc(consts, 1)
            nc.gpsimd.memset(vaug[:, :, :, :, :], 0.0).then_inc(consts, 1)
            pool.wait_ge(consts, 5)
            for t in (idf, idb):
                nc.gpsimd.affine_select(out=t[:, :], in_=t[:, :], compare_op=ALU.not_equal, fill=1.0, base=0,
                                        pattern=[[-1, P]], channel_multiplier=1).then_inc(consts, 1)
            nc.gpsimd.affine_select(out=mask_q[:, :], in_=mask_q[:, :], compare_op=ALU.is_ge, fill=MASKED, base=0,
                                    pattern=[[-1, P]], channel_multiplier=1).then_inc(consts, 1)
            nc.gpsimd.affine_select(out=mask_k[:, :], in_=mask_k[:, :], compare_op=ALU.is_ge, fill=MASKED, base=0,
                                    pattern=[[1, P]], channel_multiplier=-1).then_inc(consts, 1)
            nc.gpsimd.memset(vaug[:, :, :, :, DH:DH + 1], 1.0).then_inc(consts, 1)
            pool.wait_ge(consts, CONSTS - 1)
            nc.gpsimd.memset(ks[3 * S:P, :, :, :].bitcast(F32), 1.0).then_inc(consts, 1)
            pool.wait_ge(consts, CONSTS)

            def split(b, half, a, g):
                un = 2 * b + half
                pool.wait_ge(gen_free, g + 1).then_inc(wait_apart, 1)
                if half:
                    pool.wait_ge(scr_out[0], 32 * (b + 1)).then_inc(wait_apart, 1)
                else:
                    pool.wait_ge(scr_out[1], 32 * (b + 1)).then_inc(wait_apart, 1)
                nc.gpsimd.tensor_copy(qsp[:, a, 0, :], qf[:, a, :]).then_inc(split_step, 1)
                pool.wait_ge(split_step, 2 * un + a + 1).then_inc(wait_apart, 1)
                nc.gpsimd.tensor_tensor(qsp[:, a, 1, :], qf[:, a, :], qsp[:, a, 0, :].bitcast(F32), ALU.subtract
                                        ).then_inc(split_ready, 1)

            def normalise(n, src):
                pool.wait_ge(ln_step, LN_STEPS * (n + 1)).then_inc(wait_apart, 1)
                for t in range(NT):
                    nc.gpsimd.tensor_scalar(xh[:, t, :], src[:, t, :], mv[:, t, 0:1], rs[:, t:t + 1],
                                            ALU.subtract, ALU.mult).then_inc(xh_ready, 1)

            normalise(0, xh)
            for half in range(2):
                for a in range(2):
                    split(0, half, a, 2 + 3 * half + a)
            pool.wait_ge(gen_ready, 2).then_inc(wait_apart, 1)
            normalise(1, xt)
            sorting.prepare(pool)

            def step(b, half, more, more_x):
                g = PROLOGUE_GEN + GEN * b + half * STEP_GEN[0]
                if more:
                    for a in range(2):
                        split(b + 1, half, a, g + (2 if half == 0 else 0) + a)
                if more_x and half:
                    normalise(b + 2, xt)

            with pool.Fori(0, B - 2) as b:
                for half in range(2):
                    step(b, half, True, True)
            for half in range(2):
                step(B - 2, half, True, False)

        @block.scalar
        def _(act):
            act.sem_inc(st_free, ST_BANKS)
            act.sem_inc(pv_free, 1)
            act.sem_inc(o_out[0], 16)
            act.sem_inc(o_out[1], 16)
            for h in range(H):
                act.wait_ge(r_ready, h + 1)
                nc.scalar.mul(qs[0:2 * S, h // HH, h % HH, :], st[h % ST_BANKS][0:2 * S, :], GRID_SCALE
                              ).then_inc(r_high, 1)
            act.wait_ge(w_in, 16 * WEIGHTS)
            nc.scalar.mul(bq4[:, :], bq_s[:, :], SCALE).then_inc(bq_ready, 1)
            act.wait_ge(bq_ready, 1)
            for a, wts in enumerate((wq_s, wk_s)):
                nc.scalar.copy(wqk_hi[:, a, :, :], wts[:, :, :]).then_inc(w_high, 1)

            def high_part(b, g, c):
                act.wait_ge(gen_free, g + c + 1)
                nc.scalar.copy(xnt_hi[:, c, :], xnt[:, c, :]).then_inc(xnt_high, 1)

            def project_out(un, half, a, g):
                act.wait_ge(gen_ready, g + 1)
                if a == 0:
                    nc.scalar.activation(qf[:, 0, :], pg[:, :], ACT.Identity, bias=bq4[:, half:half + 1],
                                         scale=SCALE).then_inc(gen_free, 1)
                else:
                    nc.scalar.activation(qf[:, 1, :], pg[:, :], ACT.Identity, bias=bk_s[:, half:half + 1],
                                         scale=1.0).then_inc(gen_free, 1)

            def exps(un, n):
                pair, j = divmod(n, JOBS)
                q = pair // 2
                if n % (UJOBS // 2) == 0:
                    act.wait_ge(pv_ready, 2 * un + q + 1)
                act.wait_ge(st_ready, UJOBS * un + n + 1)
                nc.scalar.activation(probs[:, q, JOBS * (pair % 2) + j, :], st[n % ST_BANKS][:, :],
                                     ACT.Exp).then_inc(st_free, 1)

            def o_from_psum(un, q):
                act.wait_ge(pv_ready, 2 + 2 * un + q + 1)
                act.wait_ge(o_out[q], 16 * (un + 1))
                nc.scalar.copy(ov[:, q, :], po[:, :]).then_inc(pv_free, 1)

            act.sem_inc(pv_ready, 2)
            for c in range(DC):
                high_part(0, 0, c)
            for half in range(2):
                for a in range(2):
                    if half:
                        act.wait_ge(split_ready, 2 * (half - 1) + a + 1)
                    project_out(half, half, a, 2 + 3 * half + a)

            def step(b, half, more):
                un = 2 * b + half
                g = PROLOGUE_GEN + GEN * b + half * STEP_GEN[0]
                for n in range(UJOBS):
                    if more and half == 0 and n in PARTS_AT:
                        high_part(b + 1, g, PARTS_AT.index(n))
                    if more and n in QK_AT:
                        a = QK_AT.index(n)
                        act.wait_ge(split_ready, 2 * (un + 1) + a + 1)
                        project_out(un + 2, half, a, g + (2 if half == 0 else 0) + a)
                    if n == PV_AT:
                        o_from_psum(un, 0)
                    exps(un, n)
                o_from_psum(un, 1)

            with act.Fori(0, B - 1) as b:
                for half in range(2):
                    step(b, half, True)
            for half in range(2):
                step(B - 1, half, False)

        @block.vector
        def _(dve):
            dve.sem_inc(sm_free, MX_BANKS)
            def statistics(t, src):
                nc.vector.bn_stats(st6[:, t, :], src[:, t, :]).then_inc(ln_step, 1)

            def deviations(n):
                base = LN_STEPS * n
                dve.wait_ge(ln_step, base + NT).then_inc(dve_wait_apart, 1)
                for t in range(NT):
                    nc.vector.bn_aggr(mv[:, t, :], st6[:, t, :]).then_inc(ln_step, 1)
                dve.wait_ge(ln_step, base + 2 * NT)
                rsqrt(nc, dve, mv[:, :, 1], rs[:, :], [rt[:, k, :] for k in range(3)], ln_step, base + 2 * NT)

            def xnt_out(g, c):
                dve.wait_ge(gen_ready, g + c + 1)
                nc.vector.tensor_scalar(xnt[:, c, :], pg[:, :], gam[:, c:c + 1], bet[:, c:c + 1],
                                        ALU.mult, ALU.add).then_inc(gen_free, 1)

            def low_part(b, c):
                dve.wait_ge(xnt_high, DC * b + c + 1)
                nc.vector.tensor_tensor(xnt_lo[:, c, :], xnt[:, c, :], xnt_hi[:, c, :].bitcast(F32), ALU.subtract
                                        ).then_inc(xnt_low, 1)

            def v_out(half, g):
                dve.wait_ge(gen_ready, g + 1)
                nc.vector.tensor_tensor(
                    vaug[:, half, :, :, 0:DH], pg[:, :].rearrange("p (t h d) -> p t h d", t=NT, h=HH),
                    bv_s[:, half * P:(half + 1) * P].rearrange("p (a h d) -> p a h d", a=1, h=HH).to_broadcast(
                        [P, NT, HH, DH]), ALU.add).then_inc(gen_free, 1)

            def maxima(un, n):
                pair, j = divmod(n, JOBS)
                job = QUERY_JOBS[j]
                dve.wait_ge(sm_ready, UJOBS * un + n + 1)
                bank = sm[n % MX_BANKS]
                if job[0][2] == job[-1][2] and len(job) == 2:
                    t = job[0][1]
                    ins = nc.vector.tensor_reduce(
                        mx[:, 2 * pair:2 * pair + 2, t], bank[:, :].rearrange("p (a m) -> p a m", a=2), AX.X, ALU.max)
                else:
                    for a, t, cols, at in job:
                        ins = nc.vector.tensor_reduce(mx[:, 2 * pair + a, t:t + 1], bank[:, at:at + cols],
                                                      AX.X, ALU.max)
                ins.then_inc(sm_free, 1)

            def neg_out(un, g):
                dve.wait_ge(gen_ready, g + 1)
                if not isinstance(un, int) or un:
                    dve.wait_ge(max_in, 16 * un)
                nc.vector.tensor_scalar(negm[:, :], pg[0:HH * NT, 0:P], -1.0, None, ALU.mult).then_inc(gen_free, 1)

            dve.wait_ge(mt_in, 64)
            nc.vector.tensor_copy(mt_r[:, 0, :], mtf[:, :]).then_inc(mt_ready, 1)
            dve.wait_ge(x0_in, 16)
            for t in range(NT):
                statistics(t, xh)
            deviations(0)
            for h in range(H):
                dve.wait_ge(r_high, h + 1)
                low = qs[S:2 * S, h // HH, h % HH, :]
                nc.vector.scalar_tensor_tensor(low, st[h % ST_BANKS][S:2 * S, :], GRID_SCALE, low.bitcast(F32),
                                               ALU.mult, ALU.subtract).then_inc(r_low, 1)
            dve.wait_ge(w_in, 16 * WEIGHTS)
            for a, wts in enumerate((wq_s, wk_s)):
                dve.wait_ge(w_high, a + 1)
                nc.vector.tensor_tensor(wqk_lo[:, a, :, :], wts[:, :, :], wqk_hi[:, a, :, :].bitcast(F32), ALU.subtract
                                        ).then_inc(w_low, 1)
            for c in range(DC):
                xnt_out(0, c)
            for c in range(DC):
                low_part(0, c)
            for t in range(NT):
                statistics(t, xt)
            dve.wait_ge(xh_ready, NT)
            deviations(1)
            for half in range(2):
                v_out(half, 4 + 3 * half)
            for n in range(UJOBS):
                maxima(0, n)
            neg_out(0, PROLOGUE_GEN - 1)

            def step(b, half, more, more_x):
                un = 2 * b + half
                g = PROLOGUE_GEN + GEN * b + half * STEP_GEN[0]
                if more or half == 0:
                    neg = g + (2 if half == 0 else 0) + 2 if more else g
                    for n in range(UJOBS):
                        if more and half == 0 and n in X_AT:
                            xnt_out(g, X_AT.index(n))
                        if more and half == 0 and n in PARTS_AT:
                            low_part(b + 1, PARTS_AT.index(n))
                        if more_x and half:
                            if n in STATS_AT:
                                if n == STATS_AT[0]:
                                    dve.wait_ge(x_in, 16 * (b + 1)).then_inc(dve_wait_apart, 1)
                                statistics(STATS_AT.index(n), xt)
                            if n == DEVIATION_AT:
                                deviations(b + 2)
                        maxima(un + 1, n)
                    neg_out(un + 1, neg)
                    if more:
                        v_out(half, neg + 1)

            with dve.Fori(0, B - 2) as b:
                for half in range(2):
                    step(b, half, True, True)
            for half in range(2):
                step(B - 2, half, True, False)
            for half in range(2):
                step(B - 1, half, False, False)

        @block.tensor
        def _(pe):
            pe.wait_ge(mt_in, 64)
            for h in range(H):
                if h >= ST_BANKS:
                    pe.wait_ge(r_low, h - ST_BANKS + 1)
                nc.tensor.matmul(st[h % ST_BANKS][0:2 * S, :], relr[:, h, :, :].rearrange("p a j -> p (a j)"),
                                 mtf[0:S, :], start=True, stop=True).then_inc(r_ready, 1)
            pe.wait_ge(consts, CONSTS)
            pe.wait_ge(w_in, 16 * WEIGHTS)
            pe.wait_ge(w_low, 2)

            def free_gen(g):
                if not isinstance(g, int) or g:
                    pe.wait_ge(gen_free, g)

            def transpose_x(b, g, c):
                free_gen(g + c)
                if c == 0:
                    pe.wait_ge(xh_ready, NT * (b + 1))
                for t in range(NT):
                    ins = nc.tensor.transpose(pg[:, t * P:(t + 1) * P], xh[:, t, c * P:(c + 1) * P], idf[:, :])
                ins.then_inc(gen_ready, 1)

            def project(b, half, a, g):
                free_gen(g)
                cols = slice(half * P, (half + 1) * P)
                for c in range(DC):
                    pe.wait_ge(xnt_low, DC * b + c + 1)
                    for n, (lhs, rhs) in enumerate(((wqk_hi, xnt_hi), (wqk_hi, xnt_lo), (wqk_lo, xnt_hi))):
                        ins = nc.tensor.matmul(pg[:, :], lhs[:, a, c, cols], rhs[:, c, :],
                                               start=(c == 0 and n == 0), stop=(c == DC - 1 and n == 2))
                ins.then_inc(gen_ready, 1)

            def project_v(half, g):
                free_gen(g)
                for t in range(NT):
                    for c in range(DC):
                        ins = nc.tensor.matmul(pg[:, t * P:(t + 1) * P], xnt[:, c, t * P:(t + 1) * P],
                                               wv_s[:, c, half * P:(half + 1) * P],
                                               start=(t == 0 and c == 0), stop=(c == DC - 1), skip_group_check=True)
                ins.then_inc(gen_ready, 1)

            def masks(bank, blocks, mask):
                step = blocks[-1] - blocks[0] or 1
                out = bank[:, :].rearrange("p (k n) -> p k n", n=P)[:, blocks[0]:blocks[-1] + 1:step, :]
                nc.tensor.matmul(out, idb[:, :], mask[:, :].rearrange("p (a n) -> p a n", a=1).to_broadcast(
                    [P, len(blocks), P]), start=True, stop=False, skip_group_check=True)

            def query_scores(un, half, n):
                pair, j = divmod(n, JOBS)
                pe.wait_ge(sm_free, UJOBS * un + n + 1)
                bank = sm[n % MX_BANKS]
                masks(bank, [(at + cols) // P - 1 for _, _, cols, at in QUERY_JOBS[j]], mask_q)
                for a, t, cols, at in QUERY_JOBS[j]:
                    h = 2 * pair + a
                    ins = nc.tensor.matmul(bank[:, at:at + cols], qs[0:MAX_ROW, half, h, t * P:(t + 1) * P],
                                           ks[0:MAX_ROW, half, h, 0:cols], start=False, stop=True,
                                           skip_group_check=True)
                ins.then_inc(sm_ready, 1)

            def key_scores(un, half, n):
                pair, j = divmod(n, JOBS)
                pe.wait_ge(st_free, UJOBS * un + n + 1)
                bank = st[n % ST_BANKS]
                masks(bank, [at // P for _, _, _, at in KEY_JOBS[j]], mask_k)
                for a, t, cols, at in KEY_JOBS[j]:
                    h = 2 * pair + a
                    ins = nc.tensor.matmul(bank[:, at:at + cols], ks[0:MAX_ROW + 1, half, h, t * P:(t + 1) * P],
                                           qs[0:MAX_ROW + 1, half, h, t * P:N], start=False, stop=True,
                                           skip_group_check=True)
                ins.then_inc(st_ready, 1)

            def transpose_max(un, g):
                pe.wait_ge(sm_free, MX_BANKS + UJOBS * (un + 1))
                free_gen(g)
                nc.tensor.transpose(pg[0:HH * NT, 0:P], mx[:, :, :].rearrange("p h t -> p (h t)"), idf[:, :]
                                    ).then_inc(gen_ready, 1)

            def values(un, half, q):
                pe.wait_ge(st_free, ST_BANKS + UJOBS * un + 2 * JOBS * (q + 1))
                pe.wait_ge(pv_free, 2 * un + q + 1)
                for t in range(NT):
                    for r in range(4):
                        pr, a = divmod(r, 2)
                        j, at = [(j, c[3]) for j, job in enumerate(KEY_JOBS) for c in job if c[:2] == (a, t)][0]
                        ins = nc.tensor.matmul(po[VW * r:VW * (r + 1), t * P:N], vaug[:, half, t, 4 * q + r, :],
                                               probs[:, q, JOBS * pr + j, at:at + N - t * P],
                                               start=(t == 0), stop=(t == NT - 1), skip_group_check=True,
                                               tile_position=(0, VW * r))
                ins.then_inc(pv_ready, 1)

            for c in range(DC):
                transpose_x(0, 0, c)
            for half in range(2):
                for a in range(2):
                    project(0, half, a, 2 + 3 * half + a)
                project_v(half, 4 + 3 * half)
            pe.wait_ge(ks_rel, 16)
            pe.wait_ge(r_low, H)
            for part in range(2):
                pe.wait_ge(rows_in[0][part], 64)
            for n in range(UJOBS):
                query_scores(0, 0, n)
            transpose_max(0, PROLOGUE_GEN - 1)

            def step(b, half, more):
                un = 2 * b + half
                g = PROLOGUE_GEN + GEN * b + half * STEP_GEN[0]
                ahead = more or half == 0
                qk = g + (2 if half == 0 else 0)
                neg = qk + 2 if more else g
                pe.wait_ge(max_in, 16 * (un + 1))
                for n in range(UJOBS):
                    if more and half == 0 and n in X_AT:
                        transpose_x(b + 1, g, X_AT.index(n))
                    if more and n in QK_AT:
                        a = QK_AT.index(n)
                        project(b + 1, half, a, qk + a)
                    if n == PV_AT:
                        values(un, half, 0)
                    key_scores(un, half, n)
                    if ahead:
                        if n % (UJOBS // 2) == 0:
                            pe.wait_ge(rows_in[1 - half][2 * n // UJOBS], 64 * (b + 1 + half))
                        query_scores(un + 1, 1 - half, n)
                if ahead:
                    transpose_max(un + 1, neg)
                values(un, half, 1)
                if more:
                    project_v(half, neg + 1)

            with pe.Fori(0, B - 1) as b:
                for half in range(2):
                    step(b, half, True)
            for half in range(2):
                step(B - 1, half, False)


BIG = float(1 << 20)
PACK = 64
RANKS = E


class Sorting:

    STEPS = 22

    def __init__(self, nc, ctx, w):
        def sb(name, shape, dt=F32):
            return ctx.enter_context(nc.sbuf_tensor(name, shape, dt))

        self.nc, self.w = nc, w
        self.wo_s = sb("wo_s", [P, DC, D])
        self.bo_s = sb("bo_s", [P, D])
        self.wg_s = sb("wg_s", [P, DC, E])
        self.idf = sb("idf2", [P, P])
        self.below = sb("below", [P, P], BF16)
        self.ones = sb("ones", [P, P], BF16)
        self.zero = sb("zero", [P, D])
        self.empty = sb("empty", [P, 2, P, 2], I32)
        self.ov = sb("ov2", [P, 4, N])
        self.xt = sb("xt2", [P, NT, D])
        self.row0 = sb("row0", [P, P])
        self.before = sb("before", [P, NT + 1, E], BF16)
        self.cums = [sb(f"cum{i}", [P, NT, 2 * E]) for i in range(4)]
        self.ebase = sb("ebase", [P, NT, E])
        self.rank = sb("rank", [P, RANKS, E])
        self.tied = sb("tied", [1, 4])
        self.lim = sb("lim", [1, E, ET])
        self.tcum = [sb(f"tcum{i}", [1, 1, 2 * E]) for i in range(4)]
        self.tokf = sb("tokf", [P, NT, RANKS])
        self.w_in, self.o_in, self.x_in, self.c_done, self.spare_out, self.empty_out = (
            ctx.enter_context(nc.semaphore(name))
            for name in ("w_in2", "o_in", "x_in2", "c_done", "spare_out", "empty_out"))

    def load(self, sp, rows, acc, slots):
        w = self.w
        for dst, src in ((self.wo_s[:, :, :], w["wo"].rearrange("(k p) o -> p k o", p=P)),
                         (self.bo_s[:, :], w["bo"].partition_broadcast(P)),
                         (self.wg_s[:, :, :], w["wg"].rearrange("(k p) e -> p k e", p=P))):
            sp.dma_start(dst, src).then_inc(self.w_in, 16)
        sp.wait_ge(self.c_done, self.STEPS)
        for dst in (rows, acc):
            sp.dma_start(dst[T:T + SPARE, :], self.zero[:, :]).then_inc(self.spare_out, 16)
        sp.dma_start(slots.rearrange("(p s) c -> p (s c)", p=P),
                     self.empty[:, :, :, :].rearrange("p a s c -> p (a s c)")).then_inc(self.empty_out, 16)

    def load_heads(self, sp, scratch_o, b):
        sp.dma_start(self.ov[:, :, :], scratch_o[bass.ds(4 * b, 4), :, :].rearrange("q p n -> p q n")
                     ).then_inc(self.o_in, 16)

    def load_rows(self, sp, b):
        sp.dma_start(self.xt[:, :, :], self.w["x"][bass.ds(b, 1), :, :].rearrange("a (t p) d -> p (a t) d", p=P)
                     ).then_inc(self.x_in, 16)

    def prepare(self, pool):
        nc = self.nc
        nc.gpsimd.memset(self.idf[:, :], 0.0).then_inc(self.c_done, 1)
        nc.gpsimd.memset(self.below[:, :], 0.0).then_inc(self.c_done, 1)
        nc.gpsimd.memset(self.row0[:, :], 0.0).then_inc(self.c_done, 1)
        nc.gpsimd.memset(self.ones[:, :], 1.0).then_inc(self.c_done, 1)
        nc.gpsimd.memset(self.zero[:, :], 0.0).then_inc(self.c_done, 1)
        nc.gpsimd.memset(self.empty[:, :, :, :], 0).then_inc(self.c_done, 1)
        nc.gpsimd.memset(self.before[:, 0, :], 0.0).then_inc(self.c_done, 1)
        for start in self.cums[:3] + self.tcum[:3]:
            nc.gpsimd.memset(start[:, :, 0:E], 0.0).then_inc(self.c_done, 1)
        nc.gpsimd.memset(self.tied[:, :], 0.0).then_inc(self.c_done, 1)
        nc.gpsimd.iota(self.tokf[:, :, :], pattern=[[P, NT], [0, RANKS]], base=0, channel_multiplier=1,
                       allow_small_or_imprecise_dtypes=True).then_inc(self.c_done, 1)
        pool.wait_ge(self.c_done, 15)
        nc.gpsimd.memset(self.row0[0:1, :], 1.0).then_inc(self.c_done, 1)
        nc.gpsimd.affine_select(out=self.idf[:, :], in_=self.idf[:, :], compare_op=ALU.not_equal, fill=1.0, base=0,
                                pattern=[[-1, P]], channel_multiplier=1).then_inc(self.c_done, 1)
        nc.gpsimd.affine_select(out=self.below[:, :], in_=self.below[:, :], compare_op=ALU.is_ge, fill=1.0, base=0,
                                pattern=[[-1, P]], channel_multiplier=1).then_inc(self.c_done, 1)
        nc.gpsimd.iota(self.empty[:, :, :, 0], pattern=[[0, 2], [1, P]], base=T, channel_multiplier=0
                       ).then_inc(self.c_done, 1)
        nc.gpsimd.iota(self.ebase[:, :, :], pattern=[[0, NT], [T, E]], base=-int(BIG), channel_multiplier=0,
                       allow_small_or_imprecise_dtypes=True).then_inc(self.c_done, 1)
        nc.gpsimd.iota(self.rank[:, :, :], pattern=[[1, RANKS], [0, E]], base=1, channel_multiplier=0,
                       allow_small_or_imprecise_dtypes=True).then_inc(self.c_done, 1)
        nc.gpsimd.iota(self.lim[:, :, :], pattern=[[0, E], [MT, ET]], base=0, channel_multiplier=0,
                       allow_small_or_imprecise_dtypes=True).then_inc(self.c_done, 1)


def after_attention(nc, w, c, scratch_o, rows, acc, table, slots, w1_s, w2_s, experts_in):
    ctx = ExitStack()
    with ctx:
        def sb(name, shape, dt=F32):
            return ctx.enter_context(nc.sbuf_tensor(name, shape, dt))

        def pb(name, shape, dt=F32):
            return ctx.enter_context(nc.psum_tensor(name, shape, dt))

        def sem(name):
            return ctx.enter_context(nc.semaphore(name))

        rec = sb("rec", [P, NT, H])
        oh = sb("oh", [P, NT, D])
        oT = sb("oT", [P, NT, DC * P])
        res = sb("res", [P, NT, D])
        st6 = sb("st62", [P, NT, 6])
        mv = sb("mv2", [P, NT, 2])
        rs = sb("rs2", [P, NT])
        shift = sb("shift2", [P, NT])
        rt = sb("rt2", [P, 3, NT])
        x1 = sb("x1", [P, NT, D])
        x1T = sb("x1T", [P, NT, DC * P])
        gate = sb("gate", [P, NT, E])
        top = sb("top", [P, NT, E])
        masked_cum = sb("masked_cum", [P, NT, E])
        picked_b = sb("picked_b", [P, NT, E], BF16)
        expo = sb("expo", [P, NT, E])
        expm = sb("expm", [P, NT, E])
        tot = sb("tot", [P, NT])
        rtot = sb("rtot", [P, NT])
        wt = sb("wt", [P, NT, E])
        slot = sb("slot", [P, NT, E])
        pickm = sb("pickm", [P, NT, RANKS, E])
        tmp1 = sb("tmp1", [P, NT, RANKS, E])
        tmp2 = sb("tmp2", [P, NT, RANKS, E])
        idxf = sb("idxf", [P, NT, RANKS])
        weights = sb("weights", [P, NT, RANKS])
        idx = sb("idx", [P, NT, RANKS], I32)
        pay = sb("pay", [P, NT, RANKS, 2], I32)
        tied_i = sb("tied_i", [1, 2], I32)
        cnt = sb("cnt", [1, E])
        over = sb("over", [1, E, ET])
        tiles = sb("tiles", [1, E])
        earlier_tiles = sb("earlier_tiles", [1, E])

        wo_s, bo_s, wg_s, idf, below, ones, row0 = c.wo_s, c.bo_s, c.wg_s, c.idf, c.below, c.ones, c.row0
        ov, xt, before, cums, tcum, ebase, rank, lim, tied, tokf = (
            c.ov, c.xt, c.before, c.cums, c.tcum, c.ebase, c.rank, c.lim, c.tied, c.tokf)
        w_in, o_in, x_in, c_done = c.w_in, c.o_in, c.x_in, c.c_done

        pa = pb("pa", [P, NT, BANK])
        pt = pb("pt", [P, 2, BANK])
        pc = pb("pc", [P, 2, BANK])

        a_ready, oh_ready, b_ready, oT_ready = sem("a_ready"), sem("oh_ready"), sem("b_ready"), sem("oT_ready")
        c_ready, d = sem("c_ready"), sem("dve_step")
        x1_ready, d_ready, x1T_ready, g_ready = sem("x1_ready"), sem("d_ready"), sem("x1T_ready"), sem("g_ready")
        diff_ready, expo_ready, picked_ready = sem("diff_ready"), sem("expo_ready"), sem("picked_ready")
        shift_ready, x1_part, pool_step = sem("shift_ready2"), sem("x1_part"), sem("pool_step")
        pos_used, gate_ready, gate_used = sem("pos_used"), sem("gate_ready"), sem("gate_used")
        pos_ready, idx_ready, x1_out = sem("pos_ready"), sem("idx_ready"), sem("x1_out")
        scat, scat_ties = sem("scat"), sem("scat_ties")
        wait_apart = sem("wait_apart2")
        table_ready, picks_taken = sem("table_ready"), sem("picks_taken")
        block = ctx.enter_context(nc.Block())

        CONSTS = c.STEPS
        @block.sync
        def _(sp):
            sp.sem_inc(x1_out, 32)
            with sp.Fori(1, B) as b:
                sp.wait_ge(a_ready, b)
                c.load_heads(sp, scratch_o, b)
                sp.wait_ge(shift_ready, b)
                c.load_rows(sp, b)
            for e in range(2):
                load_weights(sp, w, e, w1_s[e], w2_s[e], experts_in[e])
            sp.wait_ge(x1_out, 32 + 32 * B)
            sp.wait_ge(c.spare_out, 32)

        @block.gpsimd
        def _(pool):
            pool.sem_inc(picks_taken, 1)
            pool.wait_ge(w_in, 48)
            pool.wait_ge(c.empty_out, 16)

            def scatter(t, r, done):
                nc.gpsimd.indirect_dma_start(out=slots, out_offset=bass.IndirectOffsetOnAxis(idx[:, t, r:r + 1], 0),
                                             in_=pay[:, t, r, :], in_offset=None, bounds_check=E * T - 1,
                                             oob_is_err=False).then_inc(done, 16)

            def lists(b):
                pool.wait_ge(idx_ready, b + 1).then_inc(wait_apart, 1)
                nc.gpsimd.tensor_copy(pay[:, :, :, 0], tokf[:, :, :]).then_inc(pool_step, 1)
                nc.gpsimd.tensor_tensor(tied[0:1, 2:3], tied[0:1, 2:3], tied[0:1, 1:2], ALU.add).then_inc(pool_step, 1)
                nc.gpsimd.tensor_copy(pay[:, :, :, 1].bitcast(F32), weights[:, :, :]).then_inc(pool_step, 1)
                nc.gpsimd.tensor_scalar(idx[:, :, :], idxf[:, :, :], BIG, None, ALU.add).then_inc(pool_step, 1)
                pool.wait_ge(pool_step, 7 * b + 4).then_inc(wait_apart, 1)
                nc.gpsimd.tensor_scalar(tied[0:1, 1:2], tied[0:1, 0:1], float(TOPK * N), None, ALU.is_gt
                                        ).then_inc(pool_step, 1)
                nc.gpsimd.tensor_scalar(tokf[:, :, :], tokf[:, :, :], float(N), None, ALU.add).then_inc(pool_step, 1)
                pool.wait_ge(pool_step, 7 * b + 6).then_inc(wait_apart, 1)
                nc.gpsimd.tensor_copy(tied_i[0:1, :], tied[0:1, 1:3]).then_inc(pool_step, 1)
                pool.wait_ge(pool_step, 7 * b + 7).then_inc(wait_apart, 1)
                pool.sem_inc(picks_taken, 1)
                for t in range(NT):
                    for r in range(TOPK):
                        scatter(t, r, scat)
                some = pool.value_load(tied_i[0:1, 0:1], min_val=0, max_val=1)
                earlier = pool.value_load(tied_i[0:1, 1:2], min_val=0, max_val=B)
                with pool.If(some > 0):
                    for t in range(NT):
                        for r in range(TOPK, RANKS):
                            scatter(t, r, scat_ties)
                    pool.wait_ge(scat_ties, (earlier + 1) * (16 * NT * (RANKS - TOPK))).then_inc(wait_apart, 1)
                pool.wait_ge(scat, (b + 1) * (16 * NT * TOPK)).then_inc(wait_apart, 1)

            with pool.Fori(0, B) as b:
                lists(b)

        @block.scalar
        def _(act):
            def heads_out(b):
                for k in range(2):
                    act.wait_ge(b_ready, 2 * b + k + 1)
                    nc.scalar.copy(oT[:, 2 * k:2 * k + 2, :].rearrange("p t n -> p (t n)"), pt[:, k, :]
                                   ).then_inc(oT_ready, 1)

            def exponentials(b):
                act.wait_ge(diff_ready, b + 1)
                nc.scalar.activation(expo[:, :, :], expo[:, :, :], ACT.Exp).then_inc(expo_ready, 1)

            def step(b, earlier, more):
                act.wait_ge(x1_out, 32 * (b + 1))
                if earlier:
                    act.wait_ge(d_ready, 2 * b)
                act.wait_ge(shift_ready, b + 1)
                for t in range(NT):
                    nc.scalar.activation(x1[:, t, :], res[:, t, :], ACT.Identity, bias=shift[:, t:t + 1],
                                         scale=rs[:, t:t + 1]).then_inc(x1_part if t < NT - 1 else x1_ready, 1)
                act.wait_ge(x1_part, (NT - 1) * (b + 1))
                act.wait_ge(x1_ready, b + 1)
                for dst in (rows, acc):
                    act.dma_start(dst[bass.ds(N * b, N), :].rearrange("(t p) d -> p t d", p=P), x1[:, :, :]
                                  ).then_inc(x1_out, 16)
                if earlier:
                    exponentials(b - 1)
                if more:
                    heads_out(b + 1)
                for k in range(2):
                    act.wait_ge(d_ready, 2 * b + k + 1)
                    nc.scalar.copy(x1T[:, 2 * k:2 * k + 2, :].rearrange("p t n -> p (t n)"), pt[:, k, :]
                                   ).then_inc(x1T_ready, 1)
                if earlier:
                    act.wait_ge(gate_used, b)
                act.wait_ge(g_ready, b + 1)
                nc.scalar.copy(gate[:, :, :], pa[:, 0, 0:NT * E].rearrange("p (t e) -> p t e", e=E)
                               ).then_inc(gate_ready, 1)

            heads_out(0)
            step(0, False, True)
            with act.Fori(1, B - 1) as b:
                step(b, True, True)
            step(B - 1, True, False)
            exponentials(B - 1)

        @block.tensor
        def _(pe):
            pe.wait_ge(c_done, CONSTS)
            pe.wait_ge(w_in, 48)
            def heads_to_rows(b):
                pe.wait_ge(o_in, 16 * (b + 1))
                for t in range(NT):
                    for q in range(4):
                        ins = nc.tensor.transpose(pa[:, t, q * P:(q + 1) * P], ov[:, q, t * P:(t + 1) * P], idf[:, :])
                ins.then_inc(a_ready, 1)

            def normal_heads(b):
                pe.wait_ge(oh_ready, b + 1)
                for t in range(NT):
                    for c in range(DC):
                        ins = nc.tensor.transpose(pt[:, t // 2, (t % 2 * DC + c) * P:(t % 2 * DC + c + 1) * P],
                                                  oh[:, t, c * P:(c + 1) * P], idf[:, :])
                    if t % 2:
                        ins.then_inc(b_ready, 1)

            def bias():
                for t in range(NT):
                    nc.tensor.matmul(pc[:, t // 2, t % 2 * D:(t % 2 + 1) * D], row0[:, :], bo_s[:, :],
                                     start=(t % 2 == 0), stop=False, skip_group_check=True)

            def project_out(b, k):
                pe.wait_ge(oT_ready, 2 * b + k + 1)
                for t in (2 * k, 2 * k + 1):
                    for c in range(DC):
                        ins = nc.tensor.matmul(pc[:, k, t % 2 * D:(t % 2 + 1) * D], oT[:, t, c * P:(c + 1) * P],
                                               wo_s[:, c, :], start=False, stop=(c == DC - 1),
                                               skip_group_check=True)
                ins.then_inc(c_ready, 1)

            def gates(b):
                pe.wait_ge(x1_ready, b + 1)
                for t in range(NT):
                    for c in range(DC):
                        ins = nc.tensor.transpose(pt[:, t // 2, (t % 2 * DC + c) * P:(t % 2 * DC + c + 1) * P],
                                                  x1[:, t, c * P:(c + 1) * P], idf[:, :])
                    if t % 2:
                        ins.then_inc(d_ready, 1)
                for t in range(NT):
                    if t % 2 == 0:
                        pe.wait_ge(x1T_ready, 2 * b + t // 2 + 1)
                    for c in range(DC):
                        ins = nc.tensor.matmul(pa[:, 0, t * E:(t + 1) * E], x1T[:, t, c * P:(c + 1) * P],
                                               wg_s[:, c, :], start=(t == 0 and c == 0), stop=(c == DC - 1),
                                               skip_group_check=True)
                ins.then_inc(g_ready, 1)

            def positions(b):
                pe.wait_ge(picked_ready, b + 1)
                nc.tensor.matmul(pa[:, 1, 0:NT * E], below[:, :], picked_b[:, :, :].rearrange("p t e -> p (t e)"),
                                 start=True, stop=False, skip_group_check=True)
                nc.tensor.matmul(pa[:, 1, 0:NT * E], ones[:, :], before[:, 0:NT, :].rearrange("p t e -> p (t e)"),
                                 start=False, stop=True, skip_group_check=True)
                nc.tensor.matmul(pa[:, 1, NT * E:2 * NT * E], ones[:, :],
                                 picked_b[:, :, :].rearrange("p t e -> p (t e)"),
                                 start=False, stop=True, skip_group_check=True).then_inc(pos_ready, 1)

            def step(b, earlier, more, two_more):
                if more:
                    pe.wait_ge(shift_ready, b + 1)
                    bias()
                    normal_heads(b + 1)
                    project_out(b + 1, 0)
                if earlier:
                    positions(b - 1)
                if more:
                    project_out(b + 1, 1)
                if earlier:
                    pe.wait_ge(gate_ready, b)
                gates(b)
                if two_more:
                    if earlier:
                        pe.wait_ge(pos_used, b)
                    pe.wait_ge(gate_ready, b + 1)
                    heads_to_rows(b + 2)

            heads_to_rows(0)
            bias()
            normal_heads(0)
            for k in range(2):
                project_out(0, k)
            heads_to_rows(1)
            step(0, False, True, True)
            with pe.Fori(1, B - 2) as b:
                step(b, True, True, True)
            step(B - 2, True, True, False)
            step(B - 1, True, False, False)
            positions(B - 1)
            pe.wait_ge(idx_ready, B)
            nc.tensor.matmul(pc[:, 0, 0:E], ones[:, :], before[:, 0, :], start=True, stop=True).then_inc(pos_ready, 1)

        @block.vector
        def _(dve):
            dve.wait_ge(c_done, CONSTS)
            at = [0]

            def wide(ap, shape):
                return ap.to_broadcast(shape)

            ROWS_STEPS, PICKS_STEPS = 22, 23
            STEPS = ROWS_STEPS + PICKS_STEPS + 1
            base = [0]

            def link(ins):
                ins.then_inc(d, 1)
                at[0] += 1
                dve.wait_ge(d, base[0] + at[0])

            def normalise_heads(b):
                dve.wait_ge(a_ready, b + 1)
                heads = pa[:, :, :].rearrange("p t (h e) -> p t h e", h=H)
                link(nc.vector.reciprocal(rec[:, :, :], heads[:, :, :, DH]))
                nc.vector.tensor_tensor(oh[:, :, :].rearrange("p t (h e) -> p t h e", h=H), heads[:, :, :, 0:DH],
                                        wide(rec[:, :, :].rearrange("p t (h a) -> p t h a", a=1), [P, NT, H, DH]),
                                        ALU.mult).then_inc(oh_ready, 1)

            def normalise_rows(b, earlier):
                dve.wait_ge(x_in, 16 * (b + 1))
                if earlier:
                    dve.wait_ge(x1_ready, b)
                for k in range(2):
                    dve.wait_ge(c_ready, 2 * b + k + 1)
                    link(nc.vector.tensor_tensor(res[:, 2 * k:2 * k + 2, :].rearrange("p t n -> p (t n)"), pc[:, k, :],
                                                 xt[:, 2 * k:2 * k + 2, :].rearrange("p t n -> p (t n)"), ALU.add))
                for t in range(NT):
                    ins = nc.vector.bn_stats(st6[:, t, :], res[:, t, :])
                    if t < NT - 1:
                        ins.then_inc(d, 1)
                        at[0] += 1
                ins.then_inc(d, 1)
                at[0] += 1
                dve.wait_ge(d, base[0] + at[0]).then_inc(wait_apart, 1)
                for t in range(NT):
                    ins = nc.vector.bn_aggr(mv[:, t, :], st6[:, t, :])
                    if t < NT - 1:
                        ins.then_inc(d, 1)
                        at[0] += 1
                link(ins)
                rsqrt(nc, dve, mv[:, :, 1], rs[:, :], [rt[:, k, :] for k in range(3)], d, base[0] + at[0])
                at[0] += RSQRT_STEPS
                dve.wait_ge(d, base[0] + at[0])
                nc.vector.scalar_tensor_tensor(shift[:, :], mv[:, :, 0], -1.0, rs[:, :], ALU.mult, ALU.mult
                                               ).then_inc(shift_ready, 1)

            def picks(b):
                dve.wait_ge(gate_ready, b + 1).then_inc(wait_apart, 1)
                for t in range(NT):
                    ins = nc.vector.max(top[:, t, :], gate[:, t, :])
                    if t < NT - 1:
                        ins.then_inc(d, 1)
                        at[0] += 1
                link(ins)
                full = [P, NT, E]
                nc.vector.tensor_tensor(expo[:, :, :], gate[:, :, :], wide(top[:, :, 0:1], full), ALU.subtract
                                        ).then_inc(diff_ready, 1)
                picked = cums[0][:, :, E:2 * E]
                link(nc.vector.tensor_tensor(picked, gate[:, :, :], wide(top[:, :, TOPK - 1:TOPK], full), ALU.is_ge))
                dve.sem_inc(gate_used, 1)
                link(nc.vector.tensor_copy(picked_b[:, :, :], picked))
                for t in range(NT):
                    ins = nc.vector.tensor_tensor(before[:, t + 1, :], before[:, t, :], picked_b[:, t, :], ALU.add)
                    if t < NT - 1:
                        link(ins)
                ins.then_inc(picked_ready, 1)
                for k in range(3):
                    s = 1 << k
                    link(nc.vector.tensor_tensor(cums[k + 1][:, :, E:2 * E], cums[k][:, :, E:2 * E],
                                                 cums[k][:, :, E - s:2 * E - s], ALU.add))
                dve.wait_ge(expo_ready, b + 1)
                link(nc.vector.tensor_tensor(expm[:, :, :], expo[:, :, :], picked, ALU.mult))
                link(nc.vector.tensor_reduce(tot[:, :], expm[:, :, :], AX.X, ALU.add))
                link(nc.vector.reciprocal(rtot[:, :], tot[:, :]))
                link(nc.vector.scalar_tensor_tensor(wt[:, :, :], expm[:, :, :], 1.0 / E,
                                                    wide(rtot[:, :].rearrange("p (t a) -> p t a", a=1), full),
                                                    ALU.mult, ALU.mult))
                four = [P, NT, RANKS, E]

                def over_ranks(ap):
                    return wide(ap.rearrange("p t (a e) -> p t a e", a=1), four)

                link(nc.vector.tensor_tensor(masked_cum[:, :, :], cums[3][:, :, E:2 * E], picked, ALU.mult))
                link(nc.vector.tensor_tensor(pickm[:, :, :, :], over_ranks(masked_cum[:, :, :]),
                                             wide(rank[:, :, :].rearrange("p (a r) e -> p a r e", a=1), four),
                                             ALU.is_equal))
                link(nc.vector.tensor_tensor(tmp2[:, :, :, :], pickm[:, :, :, :], over_ranks(wt[:, :, :]), ALU.mult))
                dve.wait_ge(picks_taken, b + 1)
                link(nc.vector.tensor_reduce(weights[:, :, :], tmp2[:, :, :, :], AX.X, ALU.add))
                dve.wait_ge(pos_ready, b + 1)
                link(nc.vector.tensor_tensor(slot[:, :, :], pa[:, 1, 0:NT * E].rearrange("p (t e) -> p t e", e=E),
                                             ebase[:, :, :], ALU.add))
                nc.vector.tensor_reduce(tied[0:1, 0:1], pa[0:1, 1, NT * E:2 * NT * E], AX.X, ALU.add).then_inc(pos_used, 1)
                link(nc.vector.tensor_copy(before[:, 0, :], before[:, NT, :]))
                link(nc.vector.tensor_tensor(tmp1[:, :, :, :], pickm[:, :, :, :], over_ranks(slot[:, :, :]), ALU.mult))
                nc.vector.tensor_reduce(idxf[:, :, :], tmp1[:, :, :, :], AX.X, ALU.add).then_inc(idx_ready, 1)

            def step(b, earlier, more, before_it):
                at[0] = 0
                base[0] = before_it
                normalise_rows(b, earlier)
                assert at[0] == ROWS_STEPS, at[0]
                if more:
                    normalise_heads(b + 1)
                if earlier:
                    picks(b - 1)
                    if more:
                        assert at[0] == STEPS, at[0]

            normalise_heads(0)
            step(0, False, True, 1)
            with dve.Fori(1, B - 1) as b:
                step(b, True, True, b * STEPS + (2 + ROWS_STEPS - STEPS))
            step(B - 1, True, False, (B - 1) * STEPS + 2 + ROWS_STEPS - STEPS)
            picks(B - 1)


            dve.wait_ge(pos_ready, B + 1)
            link(nc.vector.tensor_copy(cnt[:, :], pc[0:1, 0, 0:E]))
            link(nc.vector.tensor_tensor(over[:, :, :], wide(cnt[:, :].rearrange("p (e c) -> p e c", c=1), [1, E, ET]),
                                         lim[:, :, :], ALU.is_gt))
            link(nc.vector.tensor_reduce(tiles[:, :], over[:, :, :], AX.X, ALU.add))
            link(nc.vector.tensor_copy(tcum[0][:, 0, E:2 * E], tiles[:, :]))
            for k in range(3):
                s = 1 << k
                link(nc.vector.tensor_tensor(tcum[k + 1][:, :, E:2 * E], tcum[k][:, :, E:2 * E],
                                             tcum[k][:, :, E - s:2 * E - s], ALU.add))
            link(nc.vector.tensor_copy(table[:, E:E + 1], tcum[3][:, 0, 2 * E - 1:2 * E]))
            link(nc.vector.tensor_tensor(earlier_tiles[:, :], tcum[3][:, 0, E:2 * E], tiles[:, :], ALU.subtract))
            nc.vector.scalar_tensor_tensor(table[:, 0:E], earlier_tiles[:, :], float(PACK), tiles[:, :], ALU.mult, ALU.add
                                           ).then_inc(table_ready, 1)


def load_weights(sp, w, e, w1_s, w2_s, done):
    for dst, src in ((w1_s, w["w1"][bass.ds(e, 1), :, :].rearrange("a (k p) f -> p (a k) f", p=P)),
                     (w2_s, w["w2"][bass.ds(e, 1), :, :].rearrange("a (k p) d -> p (a k) d", p=P))):
        sp.dma_start(dst[:, :, :], src).then_inc(done, 16)


def experts(nc, w, rows, acc, slots, table, w1_s, w2_s, w_in):
    ctx = ExitStack()
    with ctx:
        def sb(name, shape, dt=F32):
            return ctx.enter_context(nc.sbuf_tensor(name, shape, dt))

        def pb(name, shape, dt=F32):
            return ctx.enter_context(nc.psum_tensor(name, shape, dt))

        def sem(name):
            return ctx.enter_context(nc.semaphore(name))

        def two(name):
            return [sem(f"{name}{i}") for i in range(2)]

        w1_hi = [sb(f"w1_hi{i}", [P, DC, FF], F32R) for i in range(2)]
        w1_lo = [sb(f"w1_lo{i}", [P, DC, FF], F32R) for i in range(2)]
        w2_hi = [sb(f"w2_hi{i}", [P, FC, D], F32R) for i in range(2)]
        w2_lo = [sb(f"w2_lo{i}", [P, FC, D], F32R) for i in range(2)]
        b1_s = [sb(f"b1_s{i}", [P, FC]) for i in range(2)]
        b2_s = [sb(f"b2_s{i}", [P, D]) for i in range(2)]
        lst = sb("lst", [P, 2, P, 2], I32)
        ids = sb("ids", [P, 2, P])
        tok_s = sb("tok_s", [P, 2 * P], I32)
        wts_s = sb("wts_s", [P, 2 * P])
        idf = sb("idf3", [P, P])
        spare = sb("spare", [P, MH], I32)
        idx = [sb(f"idx3{i}", [P, MH], I32) for i in range(3)]
        xg = sb("xg", [P, MH, D])
        xT_hi = sb("xT_hi", [P, DC, MT], F32R)
        xT_lo = sb("xT_lo", [P, DC, MT], F32R)
        hT = sb("hT", [P, FC, MT])
        hT_hi = sb("hT_hi", [P, FC, MT], F32R)
        hT_lo = sb("hT_lo", [P, FC, MT], F32R)
        yb = sb("yb", [P, MH, D])
        ys = sb("ys", [P, MH, D])

        px = pb("px", [P, DC, MT])
        ph = [pb(f"ph{i}", [P, 2, MT]) for i in range(FC // 2)]
        py = [pb(f"py{i}", [P, BANK]) for i in range(MH)]

        b_in = two("b_in")
        lst_in, ids_f, lists_t, lists_ready, c_done = (sem("lst_in"), sem("ids_f"), sem("lists_t"),
                                                       sem("lists_ready"), sem("c_done3"))
        pe_done, act_done, dve_done = sem("pe_done"), sem("act_done"), sem("dve_done")
        w_hi_ready, w1_ready, w2_ready = sem("w_hi_ready"), sem("w1_ready"), sem("w2_ready")
        idx_step, xg_in = sem("idx_step"), sem("xg_in")
        wait_apart = sem("wait_apart3")
        px_ready, xT_hi_ready, xT_ready = sem("px_ready"), sem("xT_hi_ready"), sem("xT_ready")
        ph_ready, h_ready, h_hi_ready, h_lo_ready = sem("ph_ready"), sem("h_ready"), sem("h_hi_ready"), sem("h_lo_ready")
        y_ready, y_free, yb_ready, ys_ready = sem("y_ready"), sem("y_free"), sem("yb_ready"), sem("ys_ready")
        ys_free, added = sem("ys_free"), sem("added")
        block = ctx.enter_context(nc.Block())

        GROUP = 4

        def walk(eng, body, start=None, end=None):
            with eng.Fori(0, E // 2) as pair:
                counts = [eng.value_load(table[0:1, bass.ds(2 * pair + q, 1)], min_val=0, max_val=PACK * (E * ET + 1) - 1)
                          for q in range(2)]
                for q in range(2):
                    e = 2 * pair + q
                    tiles, before = counts[q] % PACK, counts[q] // PACK
                    if start:
                        start(pair, e, q)
                    with eng.Fori(0, ET // GROUP) as group:
                        with eng.If(group * GROUP < tiles):
                            with eng.Fori(0, GROUP) as i:
                                with eng.If(group * GROUP + i < tiles):
                                    body(e, q, group * GROUP + i, before + group * GROUP + i)
                    if end:
                        end(pair, e, q)

        def ahead(eng, split, pair, e, q):
            eng.wait_ge(pe_done, e + 1).then_inc(wait_apart, 1)
            if q == 0:
                split(e + 1, 1, pair + 1)
            else:
                with eng.If(pair < E // 2 - 1):
                    split(e + 1, 0, pair + 2)

        @block.sync
        def _(sp):
            sp.dma_start(lst[:, :, :, :].rearrange("p a s c -> p a (s c)"),
                         slots.rearrange("(a p s) c -> p a (s c)", a=2, p=P)).then_inc(lst_in, 16)

            def load_biases(e, q):
                for dst, src in ((b1_s[q], w["b1"][bass.ds(e, 1), :, :].rearrange("a p c -> (a p) c")),
                                 (b2_s[q], w["b2"][bass.ds(e, 1), :].to_broadcast([P, D]))):
                    sp.dma_start(dst[:, :], src).then_inc(b_in[q], 16)

            for e in range(2):
                load_biases(e, e)
            with sp.Fori(0, E // 2 - 1) as pair:
                for q in range(2):
                    e = 2 * pair + q
                    sp.wait_ge(w2_ready, e + 1)
                    load_weights(sp, w, e + 2, w1_s[q], w2_s[q], w_in[q])
                    sp.wait_ge(act_done, e + 1)
                    sp.wait_ge(dve_done, e + 1)
                    load_biases(e + 2, q)

        @block.gpsimd
        def _(pool):
            nc.gpsimd.memset(idf[:, :], 0.0).then_inc(c_done, 1)
            nc.gpsimd.iota(spare[:, :], pattern=[[0, MH]], base=T, channel_multiplier=1).then_inc(c_done, 1)
            pool.wait_ge(c_done, 2)
            nc.gpsimd.affine_select(out=idf[:, :], in_=idf[:, :], compare_op=ALU.not_equal, fill=1.0, base=0,
                                    pattern=[[-1, P]], channel_multiplier=1).then_inc(c_done, 1)
            for i in range(2):
                nc.gpsimd.tensor_copy(idx[i][:, :], spare[:, :]).then_inc(idx_step, 1)
            pool.sem_inc(px_ready, 1)
            pool.wait_ge(lists_ready, 4)

            def shift(k, source):
                pool.wait_ge(idx_step, 3 * k + 2).then_inc(wait_apart, 1)
                nc.gpsimd.tensor_copy(idx[2][:, :], idx[1][:, :]).then_inc(idx_step, 1)
                pool.wait_ge(idx_step, 3 * k + 3).then_inc(wait_apart, 1)
                nc.gpsimd.tensor_copy(idx[1][:, :], idx[0][:, :]).then_inc(idx_step, 1)
                pool.wait_ge(idx_step, 3 * k + 4).then_inc(wait_apart, 1)
                nc.gpsimd.tensor_copy(idx[0][:, :], source).then_inc(idx_step, 1)
                pool.wait_ge(idx_step, 3 * k + 5).then_inc(wait_apart, 1)

            def gather():
                for h in range(MH):
                    nc.gpsimd.indirect_dma_start(out=xg[:, h, :], out_offset=None, in_=rows,
                                                 in_offset=bass.IndirectOffsetOnAxis(idx[0][:, h:h + 1], 0),
                                                 bounds_check=T + SPARE - 1, oob_is_err=True).then_inc(xg_in, 16)

            def add(k):
                pool.wait_ge(ys_ready, k + 1).then_inc(wait_apart, 1)
                for h in range(MH):
                    nc.gpsimd.indirect_dma_start(out=acc, out_offset=bass.IndirectOffsetOnAxis(idx[2][:, h:h + 1], 0),
                                                 in_=ys[:, h, :], in_offset=None, bounds_check=T + SPARE - 1,
                                                 oob_is_err=True, compute_op=ALU.add).then_inc(added, 16)
                    pool.wait_ge(added, k * (16 * MH) + 16 * (h + 1)).then_inc(wait_apart, 1)
                pool.sem_inc(ys_free, 1)

            def body(e, q, t, k):
                pool.wait_ge(px_ready, k + 1).then_inc(wait_apart, 1)
                shift(k, tok_s[:, bass.ds(e * (MH * ET) + t * MH, MH)])
                gather()
                add(k)

            walk(pool, body)
            last = pool.value_load(table[0:1, E:E + 1], min_val=0, max_val=E * ET)
            pool.wait_ge(px_ready, last + 1).then_inc(wait_apart, 1)
            shift(last, spare[:, :])
            gather()
            add(last)
            shift(last + 1, spare[:, :])
            add(last + 1)

        @block.tensor
        def _(pe):
            pe.sem_inc(pe_done, 1)
            pe.wait_ge(c_done, 3)
            for c in range(2):
                pe.wait_ge(ids_f, c + 1)
                nc.tensor.transpose(ph[c][:, 0, 0:P], ids[:, c, :], idf[:, :]).then_inc(lists_t, 1)
            for c in range(2):
                nc.tensor.transpose(ph[2 + c][:, 0, 0:P], lst[:, c, :, 1].bitcast(F32), idf[:, :]).then_inc(lists_t, 1)
            pe.wait_ge(lists_ready, 4)

            def transpose_rows(k):
                pe.wait_ge(xg_in, (k + 1) * (16 * MH))
                for h in range(MH):
                    for c in range(DC):
                        ins = nc.tensor.transpose(px[:, c, h * P:(h + 1) * P], xg[:, h, c * P:(c + 1) * P], idf[:, :])
                ins.then_inc(px_ready, 1)

            def start(pair, e, q):
                pe.wait_ge(w1_ready, e + 1).then_inc(wait_apart, 1)

            def body(e, q, t, k):
                pe.wait_ge(xT_ready, k + 1)
                for i in range(FC // 2):
                    for f in (2 * i, 2 * i + 1):
                        cols = slice(f * P, (f + 1) * P)
                        for c in range(DC):
                            for n, (lhs, rhs) in enumerate(((w1_hi, xT_hi), (w1_hi, xT_lo), (w1_lo, xT_hi))):
                                ins = nc.tensor.matmul(ph[i][:, f % 2, :], lhs[q][:, c, cols], rhs[:, c, :],
                                                       start=(f % 2 == 0 and c == 0 and n == 0),
                                                       stop=(c == DC - 1 and n == 2), skip_group_check=True)
                    ins.then_inc(ph_ready, 1)
                transpose_rows(k + 1)
                pe.wait_ge(w2_ready, e + 1)
                pe.wait_ge(y_free, k + 1)
                for i in range(FC // 2):
                    pe.wait_ge(h_lo_ready, FC // 2 * k + i + 1)
                    for f in (2 * i, 2 * i + 1):
                        for h in range(MH):
                            cols = slice(h * P, (h + 1) * P)
                            for n, (lhs, rhs) in enumerate(((hT_hi, w2_hi), (hT_hi, w2_lo), (hT_lo, w2_hi))):
                                ins = nc.tensor.matmul(py[h][:, 0:D], lhs[:, f, cols], rhs[q][:, f, :],
                                                       start=(f == 0 and n == 0), stop=(f == FC - 1 and n == 2))
                            if f == FC - 1:
                                ins.then_inc(y_ready, 1)

            def end(pair, e, q):
                pe.drain().then_inc(pe_done, 1)

            transpose_rows(0)
            walk(pe, body, start, end)

        @block.scalar
        def _(act):
            act.wait_ge(lists_ready, 4)

            def x_hi(k):
                act.wait_ge(px_ready, k + 2)
                nc.scalar.copy(xT_hi[:, :, :], px[:, :, :]).then_inc(xT_hi_ready, 1)

            def split_high(x, q, loads):
                act.wait_ge(w_in[q], 32 * loads).then_inc(wait_apart, 1)
                for c in range(DC):
                    nc.scalar.copy(w1_hi[q][:, c, :], w1_s[q][:, c, :]).then_inc(w_hi_ready, 1)
                for c in range(2):
                    half = slice(FC // 2 * c, FC // 2 * (c + 1))
                    nc.scalar.copy(w2_hi[q][:, half, :], w2_s[q][:, half, :]).then_inc(w_hi_ready, 1)

            def start(pair, e, q):
                act.wait_ge(b_in[q], 32 * (pair + 1)).then_inc(wait_apart, 1)
                ahead(act, split_high, pair, e, q)

            def body(e, q, t, k):
                def h_hi(i):
                    act.wait_ge(h_ready, FC * k + 2 * i + 2)
                    nc.scalar.copy(hT_hi[:, 2 * i:2 * i + 2, :], hT[:, 2 * i:2 * i + 2, :]).then_inc(h_hi_ready, 1)

                for i in range(FC // 2):
                    act.wait_ge(ph_ready, FC // 2 * k + i + 1)
                    for f in (2 * i, 2 * i + 1):
                        nc.scalar.activation(hT[:, f, :], ph[i][:, f % 2, :], ACT.Relu, bias=b1_s[q][:, f:f + 1],
                                             scale=1.0).then_inc(h_ready, 1)
                    if i:
                        h_hi(i - 1)
                h_hi(FC // 2 - 1)
                x_hi(k + 1)

            def end(pair, e, q):
                act.drain().then_inc(act_done, 1)

            split_high(0, 0, 1)
            x_hi(0)
            walk(act, body, start, end)

        @block.vector
        def _(dve):
            dve.sem_inc(y_free, 1)
            nc.vector.memset(ys[:, :, :], 0.0).then_inc(ys_ready, 2)
            dve.wait_ge(lst_in, 16)
            for c in range(2):
                nc.vector.tensor_copy(ids[:, c, :], lst[:, c, :, 0]).then_inc(ids_f, 1)
            dve.wait_ge(lists_t, 4)
            for c in range(2):
                nc.vector.tensor_copy(tok_s[:, c * P:(c + 1) * P], ph[c][:, 0, 0:P]).then_inc(lists_ready, 1)
                nc.vector.tensor_copy(wts_s[:, c * P:(c + 1) * P], ph[2 + c][:, 0, 0:P]).then_inc(lists_ready, 1)
            dve.wait_ge(lists_ready, 4)

            def x_lo(k):
                dve.wait_ge(xT_hi_ready, k + 1)
                nc.vector.tensor_tensor(xT_lo[:, :, :], px[:, :, :], xT_hi[:, :, :].bitcast(F32), ALU.subtract
                                        ).then_inc(xT_ready, 1)

            def split_low(x, q, loads):
                for c in range(DC):
                    dve.wait_ge(w_hi_ready, 4 * x + c + 1)
                    ins = nc.vector.tensor_tensor(w1_lo[q][:, c, :], w1_s[q][:, c, :],
                                                  w1_hi[q][:, c, :].bitcast(F32), ALU.subtract)
                ins.then_inc(w1_ready, 1)
                for c in range(2):
                    half = slice(FC // 2 * c, FC // 2 * (c + 1))
                    dve.wait_ge(w_hi_ready, 4 * x + c + 3)
                    ins = nc.vector.tensor_tensor(w2_lo[q][:, half, :], w2_s[q][:, half, :],
                                                  w2_hi[q][:, half, :].bitcast(F32), ALU.subtract)
                ins.then_inc(w2_ready, 1)

            def start(pair, e, q):
                dve.wait_ge(b_in[q], 32 * (pair + 1)).then_inc(wait_apart, 1)
                ahead(dve, split_low, pair, e, q)

            def body(e, q, t, k):
                for i in range(FC // 2):
                    dve.wait_ge(h_hi_ready, FC // 2 * k + i + 1)
                    pair_of = slice(2 * i, 2 * i + 2)
                    nc.vector.tensor_tensor(hT_lo[:, pair_of, :], hT[:, pair_of, :], hT_hi[:, pair_of, :].bitcast(F32),
                                            ALU.subtract).then_inc(h_lo_ready, 1)
                x_lo(k + 1)
                for h in range(MH):
                    dve.wait_ge(y_ready, MH * k + h + 1)
                    nc.vector.tensor_tensor(yb[:, h, :], py[h][:, 0:D], b2_s[q][:, :], ALU.add
                                            ).then_inc(y_free if h == MH - 1 else yb_ready, 1)
                dve.wait_ge(y_free, k + 2)
                dve.wait_ge(ys_free, k + 2)
                for h in range(MH):
                    ins = nc.vector.tensor_scalar(ys[:, h, :], yb[:, h, :],
                                                  wts_s[:, bass.ds(e * (MH * ET) + t * MH + h, 1)], None, ALU.mult)
                ins.then_inc(ys_ready, 1)

            def end(pair, e, q):
                dve.drain().then_inc(dve_done, 1)

            split_low(0, 0, 1)
            x_lo(0)
            walk(dve, body, start, end)


def last_layernorm(nc, acc, out):
    GB = 2
    GT = GB * NT
    GROUPS = B // GB
    ctx = ExitStack()
    with ctx:
        def sb(name, shape, dt=F32):
            return ctx.enter_context(nc.sbuf_tensor(name, shape, dt))

        def sem(name):
            return ctx.enter_context(nc.semaphore(name))

        a = [sb(f"a4{i}", [P, GT, D]) for i in range(GROUPS)]
        y = [sb(f"y4{i}", [P, GT, D]) for i in range(GROUPS)]
        st6 = sb("st64", [P, GT, 6])
        mv = [sb(f"mv4{i}", [P, GT, 2]) for i in range(GROUPS)]
        rs = [sb(f"rs4{i}", [P, GT]) for i in range(GROUPS)]
        shift = [sb(f"shift4{i}", [P, GT]) for i in range(GROUPS)]
        rt = [sb(f"rt4{i}", [P, 2, GT]) for i in range(GROUPS)]
        a_in = [sem(f"a_in{i}") for i in range(GROUPS)]
        rs_step = [sem(f"rs_step{i}") for i in range(GROUPS)]
        stats_step, shift_ready, y_ready, y_out = sem("stats_step"), sem("shift_ready4"), sem("y_ready4"), sem("y_out")
        block = ctx.enter_context(nc.Block())

        @block.sync
        def _(sp):
            for g in range(GROUPS):
                sp.dma_start(a[g][:, :, :], acc[g * GB * N:(g + 1) * GB * N, :].rearrange("(t p) d -> p t d", p=P)
                             ).then_inc(a_in[g], 16)

        @block.scalar
        def _(act):
            for g in range(GROUPS):
                act.wait_ge(shift_ready, g + 1)
                for t in range(GT):
                    nc.scalar.activation(y[g][:, t, :], a[g][:, t, :], ACT.Identity, bias=shift[g][:, t:t + 1],
                                         scale=rs[g][:, t:t + 1]).then_inc(y_ready, 1)
                act.wait_ge(y_ready, GT * (g + 1))
                act.dma_start(out[GB * g:GB * (g + 1), :, :].rearrange("a (t p) d -> p (a t) d", p=P), y[g][:, :, :]
                              ).then_inc(y_out, 16)
            act.wait_ge(y_out, 16 * GROUPS)

        @block.vector
        def _(dve):
            for g in range(GROUPS):
                dve.wait_ge(a_in[g], 16)
                for t in range(GT):
                    nc.vector.bn_stats(st6[:, t, :], a[g][:, t, :]).then_inc(stats_step, 1)
                dve.wait_ge(stats_step, GT * (2 * g + 1))
                for t in range(GT):
                    nc.vector.bn_aggr(mv[g][:, t, :], st6[:, t, :]).then_inc(stats_step, 1)
                dve.wait_ge(stats_step, GT * (2 * g + 2))
                guess(nc, dve, mv[g][:, :, 1], rs[g][:, :], [rt[g][:, k, :] for k in range(2)], rs_step[g], 0)

        @block.gpsimd
        def _(pool):
            for g in range(GROUPS):
                done, scale, var, t1 = rs_step[g], rs[g][:, :], rt[g][:, 0, :], rt[g][:, 1, :]
                for k in range(NEWTON):
                    pool.wait_ge(done, 3 + 4 * k)
                    nc.gpsimd.tensor_tensor(t1, scale, scale, ALU.mult).then_inc(done, 1)
                    pool.wait_ge(done, 4 + 4 * k)
                    nc.gpsimd.tensor_tensor(t1, t1, var, ALU.mult).then_inc(done, 1)
                    pool.wait_ge(done, 5 + 4 * k)
                    nc.gpsimd.tensor_scalar(t1, t1, -0.5, 1.5, ALU.mult, ALU.add).then_inc(done, 1)
                    pool.wait_ge(done, 6 + 4 * k)
                    nc.gpsimd.tensor_tensor(scale, scale, t1, ALU.mult).then_inc(done, 1)
                pool.wait_ge(done, 3 + 4 * NEWTON)
                nc.gpsimd.tensor_tensor(t1, mv[g][:, :, 0], scale, ALU.mult).then_inc(done, 1)
                pool.wait_ge(done, 4 + 4 * NEWTON)
                nc.gpsimd.tensor_scalar(shift[g][:, :], t1, -1.0, None, ALU.mult).then_inc(shift_ready, 1)


def build(nc, w, out):
    scratch_qk = nc.dram_tensor("scratch_qk", (2, 2, 2, P, N), F32).ap()
    scratch_o = nc.dram_tensor("scratch_o", (4 * B, P, N), F32).ap()
    rows = nc.dram_tensor("rows", (T + SPARE, D), F32).ap()
    acc = nc.dram_tensor("acc", (T + SPARE, D), F32).ap()
    slots = nc.dram_tensor("slots", (E * T, 2), I32).ap()
    ctx = ExitStack()
    with ctx:
        sorting = Sorting(nc, ctx, w)
        attention(nc, w["x"], w["mt"], w, w["rel"], scratch_qk, scratch_o, sorting, rows, acc, slots)
        table = ctx.enter_context(nc.sbuf_tensor("table", [1, E + 1], I32))
        w1_s = [ctx.enter_context(nc.sbuf_tensor(f"w1_s{i}", [P, DC, FF], F32)) for i in range(2)]
        w2_s = [ctx.enter_context(nc.sbuf_tensor(f"w2_s{i}", [P, FC, D], F32)) for i in range(2)]
        experts_in = [ctx.enter_context(nc.semaphore(f"experts_in{i}")) for i in range(2)]
        after_attention(nc, w, sorting, scratch_o, rows, acc, table, slots, w1_s, w2_s, experts_in)
        experts(nc, w, rows, acc, slots, table, w1_s, w2_s, experts_in)
        last_layernorm(nc, acc, out)


def interpolation():
    import numpy as np
    at = np.arange(N) * (S - 1)
    low, part = at // (N - 1), at % (N - 1)
    m = np.zeros((N, S), np.float32)
    np.add.at(m, (np.arange(N), low), N - 1 - part)
    np.add.at(m, (np.arange(N), np.minimum(low + 1, S - 1)), part)
    m[-1] = 0
    return np.ascontiguousarray(m.T)


def kernel(**inputs):
    import numpy as np
    import concourse.bacc as bacc
    from concourse.bass_utils import run_bass_kernel_spmd

    a = {k: np.asarray(v) for k, v in inputs.items()}

    def by_lane(wt):
        return wt.reshape(2, HH, DH, D).transpose(3, 0, 2, 1).reshape(D, D)

    arrays = {
        "x": a["L0_attn_x"], "mt": interpolation(), "rel": a["L0_attn_rel_bias"],
        "wq": by_lane(a["L0_attn_Wq"]), "wk": by_lane(a["L0_attn_Wk"]),
        "wv": a["L0_attn_Wv"].T, "wo": a["L0_attn_Wo"].T,
        "bq": a["L0_attn_bq"].reshape(2, HH, DH).transpose(2, 1, 0).reshape(P, 2),
        "bk": a["L0_attn_bk"].reshape(2, HH, DH).transpose(2, 1, 0).reshape(P, 2),
        "bv": a["L0_attn_bv"], "bo": a["L0_attn_bo"],
        "gamma": a["L0_attn_gamma"].reshape(DC, P).T, "beta": a["L0_attn_beta"].reshape(DC, P).T,
        "wg": a["L0_ffn_W_gate"], "w1": a["L0_ffn_W1"],
        "b1": a["L0_ffn_b1"].reshape(E, FC, P).transpose(0, 2, 1),
        "w2": a["L0_ffn_W2"], "b2": a["L0_ffn_b2"],
    }
    arrays = {k: np.ascontiguousarray(v) for k, v in arrays.items()}
    nc = bacc.Bacc("TRN2", target_bir_lowering=False, num_devices=1)
    w = {k: nc.dram_tensor("in_" + k, v.shape, mybir.dt.from_np(v.dtype), kind="ExternalInput").ap()
         for k, v in arrays.items()}
    out = nc.dram_tensor("out", (B, N, D), F32, kind="ExternalOutput").ap()
    build(nc, w, out)
    r = run_bass_kernel_spmd(nc, [{"in_" + k: v for k, v in arrays.items()}], core_ids=[0])
    return r.results[0]["out"]
```
